# Optimizing a Trainium2 kernel written in Bass

```python
import numpy as np
import jax
import jax.numpy as jnp

def _softmax(x, axis=-1):
    return jax.nn.softmax(x, axis=axis)

def _gelu(x):
    return jax.nn.gelu(x, approximate=True)

def _silu(x):
    return jax.nn.silu(x)

def _sigmoid(x):
    return jax.nn.sigmoid(x)

def _layernorm(x, axis=-1, eps=1e-05):
    m = jnp.mean(x, axis=axis, keepdims=True)
    v = jnp.var(x, axis=axis, keepdims=True)
    return (x - m) / jnp.sqrt(v + eps)

def _scatter_add(tgt, idx, src, axis=0):
    return tgt.at[idx].add(src)

def _segment_sum(src, seg, n):
    return jax.ops.segment_sum(src, seg, n)
kernel_name = 'mk_hybrid_d2_jaxref_r4_5d9b63'

def setup_inputs(seed: int=0):
    np.random.seed(seed)
    _w = jnp.asarray

    def _L0_attn_a_setup():
        import jax, jax.numpy as jnp
        import numpy as np
        import math
        B, S, D = (4, 512, 256)
        H = 16
        HD = D // H
        DL = 64
        LAMBDA_DECAY = 0.01
        key = jax.random.key(seed)
        ks = jax.random.split(key, 8)
        sc = lambda fan_in: 1.0 / math.sqrt(fan_in)
        return {'x': jax.random.normal(ks[0], (B, S, D), dtype=jnp.float32), 'W_q': jax.random.normal(ks[1], (D, D), dtype=jnp.float32) * sc(D), 'W_k': jax.random.normal(ks[2], (D, D), dtype=jnp.float32) * sc(D), 'W_v': jax.random.normal(ks[3], (D, D), dtype=jnp.float32) * sc(D), 'W_o': jax.random.normal(ks[4], (D, D), dtype=jnp.float32) * sc(D), 'W_down_kv': jax.random.normal(ks[5], (D, DL), dtype=jnp.float32) * sc(D), 'W_up_k': jax.random.normal(ks[6], (DL, D), dtype=jnp.float32) * sc(DL), 'W_up_v': jax.random.normal(ks[7], (DL, D), dtype=jnp.float32) * sc(DL)}
    _L0_attn_a_in = _L0_attn_a_setup()

    def _L0_attn_b_setup():
        import jax, jax.numpy as jnp
        import numpy as np
        B, L, D = (2, 512, 256)
        H = 16
        DH = D // H

        def rope_tables(seq_len, dim):
            inv_freq = 1.0 / 10000.0 ** (jnp.arange(0, dim, 2, dtype=jnp.float32) / dim)
            t = jnp.arange(seq_len, dtype=jnp.float32)
            freqs = jnp.outer(t, inv_freq)
            emb = jnp.concatenate([freqs, freqs], -1)
            return (jnp.cos(emb), jnp.sin(emb))

        def rotate_half(x):
            x1, x2 = (x[..., :x.shape[-1] // 2], x[..., x.shape[-1] // 2:])
            return jnp.concatenate([-x2, x1], axis=-1)
        key = jax.random.key(seed)
        k1, k2, k3 = jax.random.split(key, 3)
        x = jax.random.normal(k1, (B, L, D), dtype=jnp.float32)
        Wqkv = jax.random.normal(k2, (D, 3 * D), dtype=jnp.float32) / np.sqrt(D)
        Wo = jax.random.normal(k3, (D, D), dtype=jnp.float32) / np.sqrt(D)
        return {'x': x, 'Wqkv': Wqkv, 'Wo': Wo}
    _L0_attn_b_in = _L0_attn_b_setup()

    def _L0_ffn_setup():
        import jax, jax.numpy as jnp
        import numpy as np
        B, S, D, E = (4, 1024, 256, 8)
        key = jax.random.key(seed)
        k1, k2, k3, k4, k5 = jax.random.split(key, 5)
        scale = 1.0 / np.sqrt(D)
        return {'x': jax.random.normal(k1, (B, S, D), dtype=jnp.float32), 'Wg': jax.random.normal(k2, (D, D), dtype=jnp.float32) * scale, 'bg': jnp.zeros((D,), dtype=jnp.float32), 'We': jax.random.normal(k3, (E, D, D), dtype=jnp.float32) * scale, 'be': jnp.zeros((E, D), dtype=jnp.float32)}
    _L0_ffn_in = _L0_ffn_setup()

    def _L1_attn_a_setup():
        import jax, jax.numpy as jnp
        import numpy as np
        B, T, C = (4, 512, 256)
        key = jax.random.key(seed)
        k1, k2, k3 = jax.random.split(key, 3)
        x = jax.random.normal(k1, (B, T, C), dtype=jnp.float32)
        qkv_w = jax.random.normal(k2, (3 * C, C), dtype=jnp.float32) * (1.0 / np.sqrt(C))
        out_w = jax.random.normal(k3, (C, C), dtype=jnp.float32) * (1.0 / np.sqrt(C))
        out_b = jnp.zeros((C,), dtype=jnp.float32)
        return {'x': x, 'qkv_w': qkv_w, 'out_w': out_w, 'out_b': out_b}
    _L1_attn_a_in = _L1_attn_a_setup()

    def _L1_attn_b_setup():
        import jax, jax.numpy as jnp
        import numpy as np
        B, T, D = (2, 512, 256)
        H = 16
        DH = D // H
        C = 128
        ROPE_BASE = 10000.0

        def _rope_cos_sin(t_len, d_head, dtype):
            inv_freq = 1.0 / ROPE_BASE ** (jnp.arange(0, d_head, 2, dtype=jnp.float32) / d_head)
            freqs = jnp.arange(t_len, dtype=jnp.float32)[:, None] * inv_freq[None, :]
            emb = jnp.concatenate([freqs, freqs], axis=-1)
            return (jnp.cos(emb).astype(dtype), jnp.sin(emb).astype(dtype))

        def _rotate_half(x):
            x1, x2 = jnp.split(x, 2, axis=-1)
            return jnp.concatenate([-x2, x1], axis=-1)

        def _apply_rope(x, cos, sin):
            return x * cos[None, None] + _rotate_half(x) * sin[None, None]
        key = jax.random.key(seed)
        ks = jax.random.split(key, 12)
        s = 0.02
        return {'x': jax.random.normal(ks[0], (B, T, D), dtype=jnp.float32), 'w_dk': jax.random.normal(ks[1], (D, C), dtype=jnp.float32) * s, 'b_dk': jnp.zeros((C,), dtype=jnp.float32), 'w_dv': jax.random.normal(ks[2], (D, C), dtype=jnp.float32) * s, 'b_dv': jnp.zeros((C,), dtype=jnp.float32), 'w_uk': jax.random.normal(ks[3], (C, D), dtype=jnp.float32) * s, 'b_uk': jnp.zeros((D,), dtype=jnp.float32), 'w_uv': jax.random.normal(ks[4], (C, D), dtype=jnp.float32) * s, 'b_uv': jnp.zeros((D,), dtype=jnp.float32), 'w_o': jax.random.normal(ks[5], (D, D), dtype=jnp.float32) * s, 'b_o': jnp.zeros((D,), dtype=jnp.float32)}
    _L1_attn_b_in = _L1_attn_b_setup()

    def _L1_ffn_setup():
        import math
        import jax, jax.numpy as jnp
        import numpy as np
        B, S, D, F, E = (8, 512, 256, 1024, 8)
        CAPACITY_FACTOR = 1.0
        key = jax.random.key(seed)
        k1, k2, k3, k4 = jax.random.split(key, 4)
        x = jax.random.normal(k1, (B, S, D), dtype=jnp.float32)
        Wr = jax.random.normal(k2, (D, E), dtype=jnp.float32) * (1.0 / math.sqrt(D))
        W1 = jax.random.normal(k3, (E, D, F), dtype=jnp.float32) * (1.0 / math.sqrt(D))
        W2 = jax.random.normal(k4, (E, F, D), dtype=jnp.float32) * (1.0 / math.sqrt(F))
        return {'x': x, 'Wr': Wr, 'W1': W1, 'W2': W2}
    _L1_ffn_in = _L1_ffn_setup()
    _d = {'L0_attn_a_x': _L0_attn_a_in['x'], 'L0_attn_a_W_q': _L0_attn_a_in['W_q'], 'L0_attn_a_W_k': _L0_attn_a_in['W_k'], 'L0_attn_a_W_v': _L0_attn_a_in['W_v'], 'L0_attn_a_W_o': _L0_attn_a_in['W_o'], 'L0_attn_a_W_down_kv': _L0_attn_a_in['W_down_kv'], 'L0_attn_a_W_up_k': _L0_attn_a_in['W_up_k'], 'L0_attn_a_W_up_v': _L0_attn_a_in['W_up_v'], 'L0_attn_b_Wqkv': _L0_attn_b_in['Wqkv'], 'L0_attn_b_Wo': _L0_attn_b_in['Wo'], 'L0_ffn_Wg': _L0_ffn_in['Wg'], 'L0_ffn_bg': _L0_ffn_in['bg'], 'L0_ffn_We': _L0_ffn_in['We'], 'L0_ffn_be': _L0_ffn_in['be'], 'L1_attn_a_qkv_w': _L1_attn_a_in['qkv_w'], 'L1_attn_a_out_w': _L1_attn_a_in['out_w'], 'L1_attn_a_out_b': _L1_attn_a_in['out_b'], 'L1_attn_b_w_dk': _L1_attn_b_in['w_dk'], 'L1_attn_b_b_dk': _L1_attn_b_in['b_dk'], 'L1_attn_b_w_dv': _L1_attn_b_in['w_dv'], 'L1_attn_b_b_dv': _L1_attn_b_in['b_dv'], 'L1_attn_b_w_uk': _L1_attn_b_in['w_uk'], 'L1_attn_b_b_uk': _L1_attn_b_in['b_uk'], 'L1_attn_b_w_uv': _L1_attn_b_in['w_uv'], 'L1_attn_b_b_uv': _L1_attn_b_in['b_uv'], 'L1_attn_b_w_o': _L1_attn_b_in['w_o'], 'L1_attn_b_b_o': _L1_attn_b_in['b_o'], 'L1_ffn_Wr': _L1_ffn_in['Wr'], 'L1_ffn_W1': _L1_ffn_in['W1'], 'L1_ffn_W2': _L1_ffn_in['W2']}
    _x0 = _d['L0_attn_a_x']
    _d['L0_attn_a_x'] = jax.random.normal(jax.random.fold_in(jax.random.key(seed), 1), (8, 512, 256), dtype=_x0.dtype)
    del _x0
    return _d

def reference(L0_attn_a_x, L0_attn_a_W_q, L0_attn_a_W_k, L0_attn_a_W_v, L0_attn_a_W_o, L0_attn_a_W_down_kv, L0_attn_a_W_up_k, L0_attn_a_W_up_v, L0_attn_b_Wqkv, L0_attn_b_Wo, L0_ffn_Wg, L0_ffn_bg, L0_ffn_We, L0_ffn_be, L1_attn_a_qkv_w, L1_attn_a_out_w, L1_attn_a_out_b, L1_attn_b_w_dk, L1_attn_b_b_dk, L1_attn_b_w_dv, L1_attn_b_b_dv, L1_attn_b_w_uk, L1_attn_b_b_uk, L1_attn_b_w_uv, L1_attn_b_b_uv, L1_attn_b_w_o, L1_attn_b_b_o, L1_ffn_Wr, L1_ffn_W1, L1_ffn_W2):

    def _L0_attn_a_ref(x, W_q, W_k, W_v, W_o, W_down_kv, W_up_k, W_up_v):
        import jax, jax.numpy as jnp
        import numpy as np
        import math
        B, S, D = (4, 512, 256)
        H = 16
        HD = D // H
        DL = 64
        LAMBDA_DECAY = 0.01
        b, s, d = x.shape
        q = x @ W_q
        k = x @ W_k
        v = x @ W_v
        latent_kv = (k + v) @ W_down_kv
        k_rec = (latent_kv @ W_up_k).reshape(b, s, H, HD).transpose(0, 2, 1, 3)
        v_rec = (latent_kv @ W_up_v).reshape(b, s, H, HD).transpose(0, 2, 1, 3)
        qh = q.reshape(b, s, H, HD).transpose(0, 2, 1, 3)
        scores = jnp.einsum('bhqd,bhkd->bhqk', qh, k_rec) / math.sqrt(d)
        t = jnp.arange(s, dtype=jnp.float32)
        decay = jnp.exp(-LAMBDA_DECAY * jnp.abs(t[:, None] - t[None, :]))
        scores = scores * decay[None, None, :, :]
        attn = jax.nn.softmax(scores, axis=-1)
        out = jnp.einsum('bhqk,bhkd->bhqd', attn, v_rec)
        out = out.transpose(0, 2, 1, 3).reshape(b, s, d)
        return out @ W_o

    def _L0_attn_b_ref(x, Wqkv, Wo):
        import jax, jax.numpy as jnp
        import numpy as np
        B, L, D = (2, 512, 256)
        H = 16
        DH = D // H

        def rope_tables(seq_len, dim):
            inv_freq = 1.0 / 10000.0 ** (jnp.arange(0, dim, 2, dtype=jnp.float32) / dim)
            t = jnp.arange(seq_len, dtype=jnp.float32)
            freqs = jnp.outer(t, inv_freq)
            emb = jnp.concatenate([freqs, freqs], -1)
            return (jnp.cos(emb), jnp.sin(emb))

        def rotate_half(x):
            x1, x2 = (x[..., :x.shape[-1] // 2], x[..., x.shape[-1] // 2:])
            return jnp.concatenate([-x2, x1], axis=-1)
        b, l, d = x.shape
        qkv = (x @ Wqkv).reshape(b, l, 3, H, DH)
        q, k, v = (qkv[:, :, 0], qkv[:, :, 1], qkv[:, :, 2])
        cos, sin = rope_tables(l, DH)
        cos = cos[:, None, :]
        sin = sin[:, None, :]
        q = q * cos + rotate_half(q) * sin
        k = k * cos + rotate_half(k) * sin
        scale = DH ** (-0.5)
        scores = jnp.einsum('bqhd,bkhd->bhqk', q, k) * scale
        attn = jax.nn.softmax(scores, axis=-1)
        out = jnp.einsum('bhqk,bkhd->bqhd', attn, v)
        out = out.reshape(b, l, d)
        return out @ Wo

    def _L0_ffn_ref(x, Wg, bg, We, be):
        import jax, jax.numpy as jnp
        import numpy as np
        B, S, D, E = (4, 1024, 256, 8)
        probs = jax.nn.softmax(x @ Wg + bg, axis=-1)
        idx = jnp.argmax(probs, axis=-1)
        p = jnp.take_along_axis(probs, idx[..., None], axis=-1)[..., 0]
        e_idx = idx % We.shape[0]
        h = jax.nn.relu(jnp.einsum('bsd,edf->besf', x, We) + be[None, :, None, :])
        onehot = jax.nn.one_hot(e_idx, We.shape[0], dtype=x.dtype)
        out = jnp.einsum('besf,bse->bsf', h, onehot) * p[..., None]
        return out

    def _L1_attn_a_ref(x, qkv_w, out_w, out_b):
        import jax, jax.numpy as jnp
        import numpy as np
        B, T, C = (4, 512, 256)
        scale = 1.0 / jnp.sqrt(jnp.asarray(x.shape[-1], x.dtype))
        qkv = jnp.einsum('btc,dc->btd', x, qkv_w)
        q, k, v = jnp.split(qkv, 3, axis=-1)
        att = jnp.einsum('btc,bsc->bts', q, k) * scale
        causal = jnp.triu(jnp.ones((x.shape[1], x.shape[1]), dtype=bool), k=1)
        att = jnp.where(causal[None, :, :], jnp.asarray(-jnp.inf, att.dtype), att)
        att = jax.nn.softmax(att, axis=-1)
        out = jnp.einsum('bts,bsc->btc', att, v)
        return jnp.einsum('btc,dc->btd', out, out_w) + out_b

    def _L1_attn_b_ref(x, w_dk, b_dk, w_dv, b_dv, w_uk, b_uk, w_uv, b_uv, w_o, b_o):
        import jax, jax.numpy as jnp
        import numpy as np
        B, T, D = (2, 512, 256)
        H = 16
        DH = D // H
        C = 128
        ROPE_BASE = 10000.0

        def _rope_cos_sin(t_len, d_head, dtype):
            inv_freq = 1.0 / ROPE_BASE ** (jnp.arange(0, d_head, 2, dtype=jnp.float32) / d_head)
            freqs = jnp.arange(t_len, dtype=jnp.float32)[:, None] * inv_freq[None, :]
            emb = jnp.concatenate([freqs, freqs], axis=-1)
            return (jnp.cos(emb).astype(dtype), jnp.sin(emb).astype(dtype))

        def _rotate_half(x):
            x1, x2 = jnp.split(x, 2, axis=-1)
            return jnp.concatenate([-x2, x1], axis=-1)

        def _apply_rope(x, cos, sin):
            return x * cos[None, None] + _rotate_half(x) * sin[None, None]
        Bx, Tx, Dx = x.shape
        c_k = x @ w_dk + b_dk
        c_v = x @ w_dv + b_dv
        k = c_k @ w_uk + b_uk
        v = c_v @ w_uv + b_uv

        def split_heads(t):
            return t.reshape(Bx, Tx, H, DH).transpose(0, 2, 1, 3)
        q = split_heads(x)
        k = split_heads(k)
        v = split_heads(v)
        cos, sin = _rope_cos_sin(Tx, DH, x.dtype)
        q = _apply_rope(q, cos, sin)
        k = _apply_rope(k, cos, sin)
        scale = 1.0 / np.sqrt(DH)
        attn = jnp.einsum('bhid,bhjd->bhij', q, k) * scale
        attn = jax.nn.softmax(attn, axis=-1)
        out = jnp.einsum('bhij,bhjd->bhid', attn, v)
        out = out.transpose(0, 2, 1, 3).reshape(Bx, Tx, Dx)
        return out @ w_o + b_o

    def _L1_ffn_ref(x, Wr, W1, W2):
        import math
        import jax, jax.numpy as jnp
        import numpy as np
        B, S, D, F, E = (8, 512, 256, 1024, 8)
        CAPACITY_FACTOR = 1.0
        b, s, d = x.shape
        t = b * s
        cap = max(math.ceil(t * CAPACITY_FACTOR / E), 1)
        xf = x.reshape(t, d)
        probs = jax.nn.softmax(xf.astype(jnp.float32) @ Wr, axis=-1)
        eidx = jnp.argmax(probs, axis=-1)
        p_tok = jnp.take_along_axis(probs, eidx[:, None], axis=1)[:, 0]
        onehot = jax.nn.one_hot(eidx, E, dtype=jnp.int32)
        rank_all = jnp.cumsum(onehot, axis=0) - onehot
        rank = jnp.take_along_axis(rank_all, eidx[:, None], axis=1)[:, 0]
        keep = rank < cap
        slot = jnp.where(keep, rank, cap)
        dispatch = jnp.zeros((E, cap + 1), dtype=jnp.int32).at[eidx, slot].set(jnp.arange(t, dtype=jnp.int32))
        valid = jnp.zeros((E, cap + 1), dtype=bool).at[eidx, slot].set(keep)
        dispatch = dispatch[:, :cap]
        valid = valid[:, :cap]
        xe = xf[dispatch]
        h = jnp.maximum(jnp.einsum('ecd,edf->ecf', xe, W1), 0.0)
        ye = jnp.einsum('ecf,efd->ecd', h, W2)
        pe = p_tok[dispatch]
        ye = ye * (pe * valid.astype(ye.dtype))[:, :, None]
        y = jnp.zeros((t, d), dtype=x.dtype).at[dispatch.reshape(-1)].add(ye.reshape(E * cap, d).astype(x.dtype))
        return y.reshape(b, s, d)
    x = L0_attn_a_x
    x = x + _L0_attn_a_ref(_layernorm(x, axis=-1), L0_attn_a_W_q, L0_attn_a_W_k, L0_attn_a_W_v, L0_attn_a_W_o, L0_attn_a_W_down_kv, L0_attn_a_W_up_k, L0_attn_a_W_up_v)
    x = x + _L0_ffn_ref(_layernorm(x, axis=-1), L0_ffn_Wg, L0_ffn_bg, L0_ffn_We, L0_ffn_be)
    x = x + _L0_attn_b_ref(_layernorm(x, axis=-1), L0_attn_b_Wqkv, L0_attn_b_Wo)
    x = x + _L0_ffn_ref(_layernorm(x, axis=-1), L0_ffn_Wg, L0_ffn_bg, L0_ffn_We, L0_ffn_be)
    x = x + _L1_attn_a_ref(_layernorm(x, axis=-1), L1_attn_a_qkv_w, L1_attn_a_out_w, L1_attn_a_out_b)
    x = x + _L1_ffn_ref(_layernorm(x, axis=-1), L1_ffn_Wr, L1_ffn_W1, L1_ffn_W2)
    x = x + _L1_attn_b_ref(_layernorm(x, axis=-1), L1_attn_b_w_dk, L1_attn_b_b_dk, L1_attn_b_w_dv, L1_attn_b_b_dv, L1_attn_b_w_uk, L1_attn_b_b_uk, L1_attn_b_w_uv, L1_attn_b_b_uv, L1_attn_b_w_o, L1_attn_b_b_o)
    x = x + _L1_ffn_ref(_layernorm(x, axis=-1), L1_ffn_Wr, L1_ffn_W1, L1_ffn_W2)
    return x

_drawn_inputs = setup_inputs


def setup_inputs(seed=0):
    import zlib

    import numpy as np

    out = dict(_drawn_inputs(seed))
    spreads = {'L0_ffn_bg': (0.0, 0.1),
     'L0_ffn_be': (0.0, 0.31),
     'L1_attn_a_out_b': (0.0, 0.1),
     'L1_attn_b_b_dk': (0.0, 0.8),
     'L1_attn_b_b_dv': (0.0, 0.279),
     'L1_attn_b_b_uk': (0.0, 0.8),
     'L1_attn_b_b_uv': (0.0, 0.1),
     'L1_attn_b_b_o': (0.0, 0.1)}
    factors = {'L1_attn_b_w_dk': 8.0,
     'L1_attn_b_w_dv': 3.334,
     'L1_attn_b_w_uk': 8.0,
     'L1_attn_b_w_uv': 3.049}
    for name, (base, spread) in spreads.items():
        noise = np.random.default_rng([zlib.crc32(name.encode()), seed]).standard_normal(out[name].shape)
        drawn = base * np.exp(spread * noise) if base else spread * noise
        out[name] = jnp.asarray(drawn.astype(out[name].dtype))
    for name, factor in factors.items():
        out[name] = (out[name] * factor).astype(out[name].dtype)
    return out
```

```python
from contextlib import ExitStack

import numpy as np

import concourse.bass as bass
from concourse import mybir

F32, BF16 = mybir.dt.float32, mybir.dt.bfloat16
I32, U32 = mybir.dt.int32, mybir.dt.uint32
ALU, ACT, AX = mybir.AluOpType, mybir.ActivationFunctionType, mybir.AxisListType

P = 128
NB, S, D = 8, 512, 256
H, HD = 16, 16
E = 8
F = 1024
T = NB * S
NT = T // P
EPS = 1e-5


def apart(eng, value, held):
    if isinstance(value, int):
        return value
    value = eng.to_reg(value)
    eng.wait_ge(held, 16)
    return value


SLOTS = T + E * P
ZERO_ROW = SLOTS
CAP = T // E
BIG = 65536.0
EXPERT_TILES = SLOTS // P


def routing(nc, g, ins, capacity):
    X, MV, RSTD, XN = g["X"], g["MV"], g["RSTD"], g["XN"]
    ident, con = g["ident"], g["con"]
    slot, back, weight, te = g["slot"], g["back"], g["weight"], g["te"]
    G = E if capacity else D
    NQ = NT // 4

    with ExitStack() as ctx:
        def sb(name, shape, dt):
            return ctx.enter_context(nc.sbuf_tensor(f"{g['layer']}r_{name}", shape, dt))

        def sem(name):
            return nc.alloc_semaphore(f"{g['layer']}r_{name}")

        psT = ctx.enter_context(nc.psum_tensor(f"{g['layer']}r_turned", [P, 2, S], F32))
        psL = ctx.enter_context(nc.psum_tensor(f"{g['layer']}r_logits", [P, 2, 2, D], F32))
        psR = ctx.enter_context(nc.psum_tensor(f"{g['layer']}r_ranks", [P, NT, E], F32))
        psC = ctx.enter_context(nc.psum_tensor(f"{g['layer']}r_totals", [P, NT, E], F32))
        wg = sb("wg", [P, 2, G], F32)
        xnT = sb("xnT", [P, 2, 2, S], F32)
        lg = sb("lg", [P, NT, E] if capacity else [P, 2, 2, D], F32)
        if not capacity:
            bg = sb("bg", [P, D], F32)
            top = sb("top", [P, 4, 8], F32)
            ntop = sb("ntop", [P, NT], F32)
            idx = sb("idx", [P, 4, 8], U32)
            first = sb("first", [P, NT], U32)
            low3 = sb("low3", [P, NT], U32)
            ex = sb("ex", [P, 2, D], F32)
            cnt_i = sb("cnt_i", [P, E], I32)
            blk, blk_inc = sb("blk", [P, E], F32), sb("blk_inc", [P, E], F32)
            past = sb("past", [P, EXPERT_TILES, E], F32)
            tef = sb("tef", [P, EXPERT_TILES], F32)
        sums = sb("sums", [P, NT], F32)
        best = sb("best", [P, NT], F32)
        oh, ohb = sb("oh", [P, NT, E], F32), sb("ohb", [P, NT, E], BF16)
        tot, inc = sb("tot", [P, E, NT], F32), sb("inc", [P, E, NT], F32)
        rk = sb("rk", [P, NT, E], F32)
        rank, keep = sb("rank", [P, NT], F32), sb("keep", [P, NT], F32)

        loaded = sem("loaded")
        root, rstd_done = sem("root"), sem("rstd_done")
        xn_ready = sem("xn_ready")
        t_ready, t_taken = sem("turned_ready"), sem("turned_taken")
        l_ready, l_taken = sem("logits_ready"), sem("logits_taken")
        top_done, first_done, exp_done = sem("top_done"), sem("first_done"), sem("exp_done")
        steps = sem("steps")
        oh_ready, counted = sem("oh_ready"), sem("counted")
        LP = 1 if capacity else 2

        block = ctx.enter_context(nc.Block())

        @block.sync
        def _(sp):
            sp.dma_start(wg[:, :, :], ins["wg"]).then_inc(loaded, 16)
            if not capacity:
                sp.dma_start(bg[:, :], ins["bg"]).then_inc(loaded, 16)

        @block.tensor
        def _(pe):
            pe.wait_ge(loaded, 16 if capacity else 32)

            def turn(q, par):
                pe.wait_ge(xn_ready, q * 4 + 4)
                for c in range(2):
                    if not (isinstance(q, int) and q == 0):
                        pe.wait_ge(t_taken, q * 2 + (c - 1))
                    for t in range(4):
                        last = pe.transpose(psT[:, c, t * P:(t + 1) * P], XN[:, q * 4 + t, c * P:(c + 1) * P], ident[:, :])
                    last.then_inc(t_ready, 1)

            def score(q, par):
                pe.wait_ge(t_taken, q * 2 + 2)
                for pair in range(2):
                    n = q * 2 + pair
                    if not capacity:
                        if not (isinstance(n, int) and n < 2):
                            pe.wait_ge(l_taken, n - 1)
                    elif pair == 0 and not (isinstance(q, int) and q < 2):
                        pe.wait_ge(l_taken, q - 1)
                    for t in range(2):
                        tok = (2 * pair + t) * P
                        if capacity:
                            out = psL[:, par, 0, (2 * pair + t) * E:(2 * pair + t + 1) * E]
                        else:
                            out = psL[:, pair, t, :]
                        for c in range(2):
                            last = pe.matmul(out, xnT[:, par, c, tok:tok + P], wg[:, c, :], start=(c == 0), stop=(c == 1))
                    if not capacity or pair == 1:
                        last.then_inc(l_ready, 1)

            turn(0, 0)
            for q in range(1, NQ):
                turn(q, q % 2)
                score(q - 1, (q - 1) % 2)
            score(NQ - 1, (NQ - 1) % 2)
            pe.wait_ge(oh_ready, 1)
            flat = ohb[:, :, :].rearrange("p t e -> p (t e)")
            pe.matmul(psR[:, :, :].rearrange("p t e -> p (t e)"), g["before"][:, :], flat, start=True, stop=True).then_inc(
                counted, 1)
            pe.matmul(psC[:, :, :].rearrange("p t e -> p (t e)"), g["ones"][:, :], flat, start=True, stop=True).then_inc(
                counted, 1)

        @block.scalar
        def _(act):
            act.activation(RSTD[:, 1, :], MV[:, :, 1], ACT.Sqrt, bias=g["eps"][:, :]).then_inc(root, 1)

            def take(q, par):
                for c in range(2):
                    act.wait_ge(t_ready, q * 2 + (c + 1))
                    if c == 0 and not (isinstance(q, int) and q < 2):
                        act.wait_ge(l_ready, q * LP - LP)
                    act.copy(xnT[:, par, c, :], psT[:, c, :]).then_inc(t_taken, 1)

            def exps(q):
                if capacity:
                    return
                for t in range(4):
                    i = q * 4 + t
                    act.wait_ge(top_done, i * 3 + 4 - t % 2)
                    if not (isinstance(i, int) and i < 2):
                        act.wait_ge(exp_done, i - 1)
                    act.activation(ex[:, t % 2, :], lg[:, t // 2, t % 2, :], ACT.Exp, bias=ntop[:, bass.ds(i, 1)],
                                   accum_out=sums[:, bass.ds(i, 1)]).then_inc(exp_done, 1)

            def pair(j):
                take(j * 2 + 1, 1)
                exps(j * 2)
                take(j * 2 + 2, 0)
                exps(j * 2 + 1)

            take(0, 0)
            pair(0)
            with act.Fori(1, NQ // 2 - 1) as j:
                pair(j)
            take(NQ - 1, 1)
            exps(NQ - 2)
            exps(NQ - 1)
            if capacity:
                act.wait_ge(steps, 2)
                flat = lg[:, :, :].rearrange("p t e -> p (t e)")
                act.activation(flat, flat, ACT.Exp).then_inc(exp_done, 1)

        @block.vector
        def _(dve):
            dve.wait_ge(root, 1)
            dve.reciprocal(RSTD[:, 0, :], RSTD[:, 1, :]).then_inc(rstd_done, 1)
            dve.wait_ge(rstd_done, 1)
            dve.wait_ge(loaded, 16 if capacity else 32)

            def normalise(q):
                for t in range(4):
                    i = q * 4 + t
                    dve.tensor_scalar(XN[:, i, :], X[:, i, :], MV[:, i, 0:1], RSTD[:, 0, bass.ds(i, 1)],
                                      ALU.subtract, ALU.mult).then_inc(xn_ready, 1)

            def top_logits(q, par):
                if capacity:
                    dve.wait_ge(l_ready, q + 1)
                    dve.tensor_copy(lg[:, bass.ds(q * 4, 4), :], psL[:, par, 0, 0:4 * E].rearrange(
                        "p (t e) -> p t e", t=4)).then_inc(l_taken, 1)
                    return
                for pair in range(2):
                    n = q * 2 + pair
                    dve.wait_ge(l_ready, n + 1)
                    if not (isinstance(n, int) and n < 2):
                        dve.wait_ge(exp_done, n * 2 - 2)
                    dve.tensor_tensor(lg[:, pair, :, :], psL[:, pair, :, :],
                                      bg[:, :].unsqueeze(1).to_broadcast([P, 2, D]), ALU.add).then_inc(l_taken, 1)
                    dve.wait_ge(l_taken, apart(dve, n + 1, loaded))
                    for t in range(2):
                        dve.max(top[:, 2 * pair + t, :], lg[:, pair, t, :]).then_inc(top_done, 1)
                    dve.wait_ge(top_done, apart(dve, (q * 4 + 2 * pair) * 3 + 2, loaded))
                    for t in range(2):
                        i = q * 4 + (2 * pair + t)
                        k = 2 * pair + t
                        dve.max_index(idx[:, k, :], top[:, k, :], lg[:, pair, t, :]).then_inc(top_done, 1)
                        dve.tensor_scalar(ntop[:, bass.ds(i, 1)], top[:, k, 0:1], -1.0, None, ALU.mult).then_inc(top_done, 1)
                dve.wait_ge(top_done, q * 12 + 12)
                dve.tensor_copy(first[:, bass.ds(q * 4, 4)], idx[:, :, 0]).then_inc(first_done, 1)

            def pair(j):
                normalise(j * 2 + 1)
                top_logits(j * 2, 0)
                normalise(j * 2 + 2)
                top_logits(j * 2 + 1, 1)

            normalise(0)
            pair(0)
            with dve.Fori(1, NQ // 2 - 1) as j:
                pair(j)
            normalise(NQ - 1)
            top_logits(NQ - 2, 0)
            top_logits(NQ - 1, 1)

            done = [0]

            def link(ins_):
                done[0] += 1
                ins_.then_inc(steps, 1)
                dve.wait_ge(steps, done[0])

            def over_experts(ap):
                return ap.unsqueeze(2).to_broadcast([P, NT, E])

            def over_tiles(ap):
                return ap.unsqueeze(1).to_broadcast([P, NT, E])

            if capacity:
                dve.wait_ge(l_taken, NQ)
                link(dve.tensor_reduce(best[:, :], lg[:, :, :], AX.X, ALU.max))
                link(dve.tensor_tensor(lg[:, :, :], lg[:, :, :], over_experts(best[:, :]), ALU.subtract))
                dve.wait_ge(exp_done, 1)
                link(dve.tensor_reduce(sums[:, :], lg[:, :, :], AX.X, ALU.add))
                link(dve.tensor_scalar(rk[:, :, :], lg[:, :, :], 1.0, None, ALU.is_ge))
                link(dve.tensor_tensor(rk[:, :, :], rk[:, :, :], over_tiles(con["down8"]), ALU.mult))
                link(dve.tensor_reduce(best[:, :], rk[:, :, :], AX.X, ALU.max))
                link(dve.tensor_tensor(oh[:, :, :], over_tiles(con["down8"]), over_experts(best[:, :]), ALU.is_equal))
            else:
                dve.wait_ge(exp_done, NT)
                dve.wait_ge(first_done, NQ)
                link(dve.tensor_scalar(low3[:, :], first[:, :], E - 1, None, ALU.bitwise_and))
                link(dve.tensor_copy(best[:, :], low3[:, :]))
                link(dve.tensor_tensor(oh[:, :, :], over_tiles(con["up8"]), over_experts(best[:, :]), ALU.is_equal))
            dve.tensor_copy(ohb[:, :, :], oh[:, :, :]).then_inc(oh_ready, 1)
            link(dve.reciprocal(weight[:, :], sums[:, :]))
            dve.wait_ge(counted, 2)
            link(dve.tensor_copy(tot[:, :, :], psC[:, :, :].rearrange("p t e -> p e t")))
            link(dve.tensor_tensor_scan(inc[:, :, :].rearrange("p e t -> p (e t)"), con["resets"],
                                        tot[:, :, :].rearrange("p e t -> p (e t)"), 0.0, ALU.mult, ALU.add))
            link(dve.tensor_tensor(tot[:, :, :], inc[:, :, :], tot[:, :, :], ALU.subtract))
            link(dve.tensor_tensor(rk[:, :, :], psR[:, :, :], tot[:, :, :].rearrange("p e t -> p t e"), ALU.add))
            if not capacity:
                link(dve.tensor_scalar(cnt_i[:, :], inc[:, :, NT - 1], float(P - 1), None, ALU.add))
                link(dve.tensor_scalar(cnt_i[:, :], cnt_i[:, :], P.bit_length() - 1, None, ALU.arith_shift_right))
                link(dve.tensor_copy(blk[:, :], cnt_i[:, :]))
                link(dve.tensor_tensor_scan(blk_inc[:, :], con["ones8"], blk[:, :], 0.0, ALU.mult, ALU.add))
                link(dve.tensor_tensor(blk[:, :], blk_inc[:, :], blk[:, :], ALU.subtract))
                link(dve.tensor_scalar(blk[:, :], blk[:, :], float(P), None, ALU.mult))
                link(dve.tensor_tensor(rk[:, :, :], rk[:, :, :], over_tiles(blk[:, :]), ALU.add))
                link(dve.tensor_tensor(past[:, :, :], con["tiles"].unsqueeze(2).to_broadcast([P, EXPERT_TILES, E]),
                                       blk_inc[:, :].unsqueeze(1).to_broadcast([P, EXPERT_TILES, E]), ALU.is_ge))
                link(dve.tensor_reduce(tef[:, :], past[:, :, :], AX.X, ALU.add))
                link(dve.tensor_scalar(tef[:, :], tef[:, :], float(E - 1), float(D), ALU.min, ALU.mult))
                link(dve.tensor_copy(te[:, :], tef[:, :]))
            link(dve.tensor_tensor(rk[:, :, :], rk[:, :, :], oh[:, :, :], ALU.mult))
            link(dve.tensor_reduce(rank[:, :], rk[:, :, :], AX.X, ALU.add))
            if capacity:
                link(dve.tensor_scalar(keep[:, :], rank[:, :], float(CAP), BIG, ALU.is_ge, ALU.mult))
                link(dve.tensor_tensor(rank[:, :], rank[:, :], keep[:, :], ALU.add))
                link(dve.tensor_scalar(best[:, :], best[:, :], -float(CAP), float(CAP * E), ALU.mult, ALU.add))
                link(dve.tensor_tensor(rank[:, :], rank[:, :], best[:, :], ALU.add))
            link(dve.tensor_copy(slot[:, :], rank[:, :]))
            link(dve.tensor_scalar(keep[:, :], rank[:, :], float(ZERO_ROW), None, ALU.min))
            link(dve.tensor_copy(back[:, :], keep[:, :]))


def dispatch(pool, g, scattered):
    for i in range(NT):
        pool.indirect_dma_start(out=g["xe"][0:SLOTS, :], out_offset=bass.IndirectOffsetOnAxis(ap=g["slot"][:, i:i + 1], axis=0),
                                in_=g["XN"][:, i, :], in_offset=None, bounds_check=SLOTS - 1,
                                oob_is_err=False).then_inc(scattered, 16)


def collect(pool, g, gathered, added):
    NG = len(gathered)
    for i in range(NT):
        if i >= NG:
            pool.wait_ge(added, i - NG + 1)
        pool.indirect_dma_start(out=g["XN"][:, i, :], out_offset=None, in_=g["ye"][0:SLOTS + 1, :],
                                in_offset=bass.IndirectOffsetOnAxis(ap=g["back"][:, i:i + 1], axis=0)).then_inc(
            gathered[i % NG], 16)


def statistics(dve, g, st, bns_done, i):
    dve.bn_stats(st[:, i % 4, :], g["X"][:, i, :]).then_inc(bns_done, 1)
    dve.wait_ge(bns_done, i + 1)
    dve.bn_aggr(g["MV"][:, i, :], st[:, i % 4, :])


def experts_small(nc, g, ins):
    X, XN, te, weight = g["X"], g["XN"], g["te"], g["weight"]
    RING = 4
    with ExitStack() as ctx:
        def sb(name, shape, dt):
            return ctx.enter_context(nc.sbuf_tensor(f"{g['layer']}x_{name}", shape, dt))

        def sem(name):
            return nc.alloc_semaphore(f"{g['layer']}x_{name}")

        psT = ctx.enter_context(nc.psum_tensor(f"{g['layer']}x_turned", [P, 2, S], F32))
        psY = ctx.enter_context(nc.psum_tensor(f"{g['layer']}x_results", [P, 2, S], F32))
        we, be = sb("we", [P, 2, E * D], F32), sb("be", [P, E * D], F32)
        xin, xT = sb("xin", [P, RING, D], F32), sb("xT", [P, 2, 2, P], F32)
        y, st = sb("y", [P, RING, D], F32), sb("st", [P, 4, 6], F32)
        loaded, scattered = sem("loaded"), sem("scattered")
        x_loaded = [sem(f"x_loaded{i}") for i in range(RING)]
        y_stored = [sem(f"y_stored{i}") for i in range(RING)]
        t_ready, t_taken, y_ready, y_taken = sem("t_ready"), sem("t_taken"), sem("y_ready"), sem("y_taken")
        gathered = [sem(f"gathered{i}") for i in range(8)]
        relu_done, added, bns_done = sem("relu_done"), sem("added"), sem("bns_done")
        block = ctx.enter_context(nc.Block())
        NB4 = EXPERT_TILES // RING

        @block.gpsimd
        def _(pool):
            dispatch(pool, g, scattered)
            for r in range(RING):
                pool.wait_ge(y_stored[r], 16 * NB4)
            collect(pool, g, gathered, added)

        @block.sync
        def _(sp):
            sp.dma_start(we[:, :, :], ins["we"]).then_inc(loaded, 16)
            sp.dma_start(be[:, :], ins["be"]).then_inc(loaded, 16)
            sp.wait_ge(scattered, 16 * NT)

            def load(b, r):
                if not (isinstance(b, int) and b == 0):
                    sp.wait_ge(t_ready, b * RING + (r - RING + 1))
                sp.dma_start(xin[:, r, :], g["xe"][bass.ds((b * RING + r) * P, P), :]).then_inc(x_loaded[r], 16)

            def store(b, r):
                sp.wait_ge(y_taken, b * RING + (r + 1))
                sp.dma_start(g["ye"][bass.ds((b * RING + r) * P, P), :], y[:, r, :]).then_inc(y_stored[r], 16)

            for r in range(RING):
                load(0, r)
            with sp.Fori(0, NB4 - 1) as b:
                for r in range(RING):
                    store(b, r)
                    load(b + 1, r)
            for r in range(RING):
                store(NB4 - 1, r)
            for r in range(RING):
                sp.wait_ge(y_stored[r], 16 * NB4)

        @block.tensor
        def _(pe):
            pe.wait_ge(loaded, 32)

            def turn(b, r):
                pe.wait_ge(x_loaded[r], b * 16 + 16)
                n = b * RING + r
                if not (isinstance(n, int) and n < 2):
                    pe.wait_ge(t_taken, n - 1)
                for c in range(2):
                    last = pe.transpose(psT[:, r % 2, c * P:(c + 1) * P], xin[:, r, c * P:(c + 1) * P], g["ident"][:, :])
                last.then_inc(t_ready, 1)

            def expert(b, r):
                n = b * RING + r
                at = pe.value_load(te[0:1, bass.ds(n, 1)], min_val=0, max_val=(E - 1) * D)
                pe.wait_ge(t_taken, n + 1)
                if not (isinstance(n, int) and n < 2):
                    pe.wait_ge(y_taken, n - 1)
                for c in range(2):
                    last = pe.matmul(psY[:, r % 2, 0:D], xT[:, r % 2, c, :], we[:, c, bass.ds(at, D)], start=(c == 0), stop=(c == 1))
                last.then_inc(y_ready, 1)

            def ring(b, more):
                for r in range(RING):
                    if r < RING - 1:
                        turn(b, r + 1)
                    elif more:
                        turn(b + 1, 0)
                    expert(b, r)

            turn(0, 0)
            ring(0, True)
            with pe.Fori(1, NB4 - 1) as b:
                ring(b, True)
            ring(NB4 - 1, False)

        @block.scalar
        def _(act):
            def take(b, r):
                n = b * RING + r
                act.wait_ge(t_ready, n + 1)
                if not (isinstance(n, int) and n < 2):
                    act.wait_ge(y_ready, n - 1)
                act.copy(xT[:, r % 2, :, :].rearrange("p c t -> p (c t)"), psT[:, r % 2, 0:D]).then_inc(t_taken, 1)

            for r in range(RING):
                take(0, r)
            with act.Fori(1, NB4) as b:
                for r in range(RING):
                    take(b, r)
            for i in range(NT):
                act.wait_ge(gathered[i % 8], 16 * (i // 8 + 1))
                act.activation(XN[:, i, :], XN[:, i, :], ACT.Relu, scale=weight[:, i:i + 1]).then_inc(relu_done, 1)

        @block.vector
        def _(dve):
            dve.wait_ge(loaded, 32)

            def result(b, r):
                n = b * RING + r
                at = dve.value_load(te[0:1, bass.ds(n, 1)], min_val=0, max_val=(E - 1) * D)
                dve.wait_ge(y_ready, n + 1)
                if not (isinstance(b, int) and b == 0):
                    dve.wait_ge(y_stored[r], b * 16)
                dve.tensor_tensor(y[:, r, :], psY[:, r % 2, 0:D], be[:, bass.ds(at, D)], ALU.add).then_inc(y_taken, 1)

            for r in range(RING):
                result(0, r)
            with dve.Fori(1, NB4) as b:
                for r in range(RING):
                    result(b, r)
            for i in range(NT):
                dve.wait_ge(relu_done, i + 1)
                dve.tensor_tensor(X[:, i, :], X[:, i, :], XN[:, i, :], ALU.add).then_inc(added, 1)
                dve.wait_ge(added, i + 1)
                statistics(dve, g, st, bns_done, i)


def experts_large(nc, g, ins, last_layer):
    X, XN, weight = g["X"], g["XN"], g["weight"]
    FC = F // P
    QT = CAP // P
    with ExitStack() as ctx:
        def sb(name, shape, dt):
            return ctx.enter_context(nc.sbuf_tensor(f"{g['layer']}x_{name}", shape, dt))

        def sem(name):
            return nc.alloc_semaphore(f"{g['layer']}x_{name}")

        psT = ctx.enter_context(nc.psum_tensor(f"{g['layer']}x_turned", [P, 2, S], F32))
        psH = ctx.enter_context(nc.psum_tensor(f"{g['layer']}x_inner", [P, 3, S], F32))
        psY = ctx.enter_context(nc.psum_tensor(f"{g['layer']}x_results", [P, 2, S], F32))
        w1, w2 = sb("w1", [P, 2, 2, F], F32), sb("w2", [P, 2, FC, D], F32)
        xin, xT = sb("xin", [P, 2, QT, D], F32), sb("xT", [P, 2, 2, S], F32)
        hT = sb("hT", [P, FC, S], F32)
        y, st = sb("y", [P, 2, QT, D], F32), sb("st", [P, 4, 6], F32)
        scattered = sem("scattered")
        w_loaded = [sem(f"w_loaded{i}") for i in range(2)]
        x_loaded = [sem(f"x_loaded{i}") for i in range(2)]
        y_stored = [sem(f"y_stored{i}") for i in range(2)]
        t_ready, t_taken = sem("t_ready"), sem("t_taken")
        h_ready, y_ready = sem("h_ready"), sem("y_ready")
        h_even, h_odd = sem("h_even_taken"), sem("h_odd_taken")
        y_taken = sem("y_taken")
        gathered = [sem(f"gathered{i}") for i in range(8)]
        added, bns_done, out_stored = sem("added"), sem("bns_done"), sem("out_stored")
        block = ctx.enter_context(nc.Block())

        @block.gpsimd
        def _(pool):
            dispatch(pool, g, scattered)
            for p in range(2):
                pool.wait_ge(y_stored[p], 16 * (E // 2))
            collect(pool, g, gathered, added)

        @block.sync
        def _(sp):
            def weights(e, p):
                sp.dma_start(w1[:, p, :, :], ins["w1"][e]).then_inc(w_loaded[p], 16)
                sp.dma_start(w2[:, p, :, :], ins["w2"][e]).then_inc(w_loaded[p], 16)

            def tokens(e, p):
                sp.dma_start(xin[:, p, :, :], g["xe"][bass.ds(e * CAP, CAP), :].rearrange("(q p) d -> p q d", p=P)).then_inc(
                    x_loaded[p], 16)

            def store(e, p):
                sp.wait_ge(y_taken, e * QT + QT)
                sp.dma_start(g["ye"][bass.ds(e * CAP, CAP), :].rearrange("(q p) d -> p q d", p=P), y[:, p, :, :]).then_inc(
                    y_stored[p], 16)

            for p in range(2):
                weights(p, p)
            sp.wait_ge(scattered, 16 * NT)
            for p in range(2):
                tokens(p, p)
            with sp.Fori(0, E // 2 - 1) as j:
                for p in range(2):
                    e = j * 2 + p
                    store(e, p)
                    weights(e + 2, p)
                    tokens(e + 2, p)
            for p in range(2):
                store(E - 2 + p, p)
            for p in range(2):
                sp.wait_ge(y_stored[p], 16 * (E // 2))
            if last_layer:
                for q in range(NB):
                    sp.wait_ge(added, 4 * q + 4)
                    sp.dma_start(ins["out"][q], X[:, 4 * q:4 * q + 4, :]).then_inc(out_stored, 16)
                sp.wait_ge(out_stored, 16 * NB)

        @block.tensor
        def _(pe):
            def turn(j, p):
                pe.wait_ge(x_loaded[p], j * 16 + 16)
                n = j * 2 + p
                for c in range(2):
                    if not (isinstance(n, int) and n == 0):
                        pe.wait_ge(t_taken, n * 2 + (c - 1))
                    for t in range(QT):
                        last = pe.transpose(psT[:, c, t * P:(t + 1) * P], xin[:, p, t, c * P:(c + 1) * P], g["ident"][:, :])
                    last.then_inc(t_ready, 1)

            def inner(j, p):
                n = j * 2 + p
                pe.wait_ge(w_loaded[p], j * 32 + 32)
                pe.wait_ge(t_taken, n * 2 + 2)
                for f in range(FC):
                    if not (isinstance(n, int) and n == 0 and f < 2):
                        pe.wait_ge(h_even if f % 2 == 0 else h_odd, n * (FC // 2) + f // 2)
                    for c in range(2):
                        last = pe.matmul(psH[:, f % 2, :], w1[:, p, c, f * P:(f + 1) * P], xT[:, p, c, :],
                                         start=(c == 0), stop=(c == 1))
                    last.then_inc(h_ready, 1)

            def outer(j, p):
                n = j * 2 + p
                pe.wait_ge(h_even, n * (FC // 2) + FC // 2)
                pe.wait_ge(h_odd, n * (FC // 2) + FC // 2)
                for t in range(QT):
                    if not (isinstance(n, int) and n == 0 and t < 2):
                        pe.wait_ge(y_taken, n * QT + (t - 1))
                    for f in range(FC):
                        last = pe.matmul(psY[:, t % 2, 0:D], hT[:, f, t * P:(t + 1) * P], w2[:, p, f, :],
                                         start=(f == 0), stop=(f == FC - 1))
                    last.then_inc(y_ready, 1)

            turn(0, 0)

            def pair(j, more):
                inner(j, 0)
                turn(j, 1)
                outer(j, 0)
                inner(j, 1)
                if more:
                    turn(j + 1, 0)
                outer(j, 1)

            pair(0, True)
            with pe.Fori(1, E // 2 - 1) as j:
                pair(j, True)
            pair(E // 2 - 1, False)

        @block.scalar
        def _(act):
            def take(j, p):
                n = j * 2 + p
                for c in range(2):
                    act.wait_ge(t_ready, n * 2 + (c + 1))
                    act.copy(xT[:, p, c, :], psT[:, c, :]).then_inc(t_taken, 1)

            def relus(j, p):
                n = j * 2 + p
                for f in range(0, FC, 2):
                    act.wait_ge(h_ready, n * FC + (f + 1))
                    if not (isinstance(n, int) and n == 0):
                        act.wait_ge(y_ready, n * QT)
                    act.activation(hT[:, f, :], psH[:, f % 2, :], ACT.Relu).then_inc(h_even, 1)

            take(0, 0)

            def pair(j, more):
                relus(j, 0)
                take(j, 1)
                relus(j, 1)
                if more:
                    take(j + 1, 0)

            pair(0, True)
            with act.Fori(1, E // 2 - 1) as j:
                pair(j, True)
            pair(E // 2 - 1, False)

        @block.vector
        def _(dve):
            def relus(j, p):
                n = j * 2 + p
                for f in range(1, FC, 2):
                    dve.wait_ge(h_ready, n * FC + (f + 1))
                    if not (isinstance(n, int) and n == 0):
                        dve.wait_ge(y_ready, n * QT)
                    dve.tensor_scalar(hT[:, f, :], psH[:, f % 2, :], 0.0, None, ALU.max).then_inc(h_odd, 1)

            def results(j, p):
                n = j * 2 + p
                for t in range(QT):
                    dve.wait_ge(y_ready, n * QT + (t + 1))
                    if t == 0 and not (isinstance(j, int) and j == 0):
                        dve.wait_ge(y_stored[p], j * 16)
                    dve.tensor_copy(y[:, p, t, :], psY[:, t % 2, 0:D]).then_inc(y_taken, 1)

            def pair(j):
                for p in range(2):
                    relus(j, p)
                    results(j, p)

            pair(0)
            with dve.Fori(1, E // 2) as j:
                pair(j)
            for i in range(NT):
                dve.wait_ge(gathered[i % 8], 16 * (i // 8 + 1))
                dve.scalar_tensor_tensor(X[:, i, :], XN[:, i, :], weight[:, i:i + 1], X[:, i, :], ALU.mult,
                                         ALU.add).then_inc(added, 1)
                if not last_layer:
                    dve.wait_ge(added, i + 1)
                    statistics(dve, g, st, bns_done, i)
CON = [("up8", E), ("down8", E), ("ones8", E), ("resets", E * NT), ("tiles", EXPERT_TILES)]
CON_WIDTH = sum(n for _, n in CON)


def global_tensors(nc, ctx):
    def sb(name, shape, dt):
        return ctx.enter_context(nc.sbuf_tensor(name, shape, dt))

    g = {"X": sb("X", [P, NT, D], F32), "MV": sb("MV", [P, NT, 2], F32), "RSTD": sb("RSTD", [P, 2, NT], F32),
         "ident": sb("ident_sb", [P, P], F32), "identb": sb("identb", [P, P], BF16), "eps": sb("eps", [P, 1], F32),
         "before": sb("before", [P, P], BF16), "ones": sb("ones", [P, P], BF16),
         "con_sb": sb("con_sb", [P, CON_WIDTH], F32),
         "xe": nc.dram_tensor("dispatched", [SLOTS, D], F32, kind="Internal").ap(),
         "ye": nc.dram_tensor("expert_results", [SLOTS + 1, D], F32, kind="Internal").ap()}
    at, g["con"] = 0, {}
    for name, n in CON:
        g["con"][name] = g["con_sb"][:, at:at + n]
        at += n
    return g


def load_tokens(nc, g, ins):
    with ExitStack() as ctx:
        fl = ctx.enter_context(nc.sbuf_tensor("before_f", [P, P], F32))
        zero = ctx.enter_context(nc.sbuf_tensor("zero", [P, D], F32))
        st = ctx.enter_context(nc.sbuf_tensor("st", [P, NT, 6], F32))
        x_loaded = [nc.alloc_semaphore(f"x_loaded{q}") for q in range(NB)]
        con_loaded = nc.alloc_semaphore("con_loaded")
        zeroed = nc.alloc_semaphore("zeroed")
        cleared = nc.alloc_semaphore("cleared")
        bns_done = nc.alloc_semaphore("bns_done")
        block = ctx.enter_context(nc.Block())

        @block.sync
        def _(sp):
            for q in range(NB):
                sp.dma_start(g["X"][:, 4 * q:4 * q + 4, :], ins["x"][q]).then_inc(x_loaded[q], 16)
            sp.dma_start(g["ident"][:, :], ins["ident"]).then_inc(con_loaded, 16)
            sp.dma_start(fl[:, :], ins["before"]).then_inc(con_loaded, 16)
            sp.dma_start(g["con_sb"][:, :], ins["con"]).then_inc(con_loaded, 16)
            sp.wait_ge(zeroed, 1)
            sp.dma_start(g["xe"].rearrange("(a p) d -> p a d", p=P),
                         zero[:, :].unsqueeze(1).to_broadcast([P, EXPERT_TILES, D])).then_inc(cleared, 16)
            sp.dma_start(g["ye"][ZERO_ROW:ZERO_ROW + 1, :], zero[0:1, :]).then_inc(cleared, 16)
            sp.wait_ge(cleared, 32)

        @block.gpsimd
        def _(pool):
            pool.memset(zero[:, :], 0.0).then_inc(zeroed, 1)
            pool.memset(g["eps"][:, :], EPS)
            pool.memset(g["ones"][:, :], 1.0)

        @block.vector
        def _(dve):
            for q in range(NB):
                dve.wait_ge(x_loaded[q], 16)
                for i in range(4 * q, 4 * q + 4):
                    dve.bn_stats(st[:, i, :], g["X"][:, i, :]).then_inc(bns_done, 1)
            dve.wait_ge(bns_done, NT)
            for i in range(NT):
                dve.bn_aggr(g["MV"][:, i, :], st[:, i, :])
            dve.wait_ge(con_loaded, 48)
            dve.tensor_copy(g["identb"][:, :], g["ident"][:, :])
            dve.tensor_copy(g["before"][:, :], fl[:, :])


def routed_layer(nc, g, ins, capacity, last_layer=False):
    with ExitStack() as ctx:
        def sb(name, shape, dt):
            return ctx.enter_context(nc.sbuf_tensor(f"{g['layer']}_{name}", shape, dt))

        g = dict(g, XN=sb("XN", [P, NT, D], F32), slot=sb("slot", [P, NT], I32), back=sb("back", [P, NT], I32),
                 weight=sb("weight", [P, NT], F32), te=None if capacity else sb("te", [P, EXPERT_TILES], I32))
        routing(nc, g, ins, capacity)
        if capacity:
            experts_large(nc, g, ins, last_layer)
        else:
            experts_small(nc, g, ins)


def shape_constants():
    rows = {"up8": np.arange(E), "down8": E - np.arange(E), "ones8": np.ones(E),
            "resets": (np.arange(E * NT) % NT != 0), "tiles": np.arange(EXPERT_TILES)}
    row = np.concatenate([rows[n] for n, _ in CON]).astype(np.float32)
    return np.ascontiguousarray(np.broadcast_to(row, (P, CON_WIDTH)))
DL = 64
FOLDED = {"a_wk": [P, 2, D], "a_wv": [P, 2, D], "c_wg": [P, 2, D], "c_wv": [P, 2, D], "d_wk": [P, 2, D],
          "d_wv": [P, 2, D], "d_kb": [P, 2], "d_xb": [P, D]}


def fold_weights(nc, w, folded):
    SHAPES = {"wkT": [P, 2, D], "wvT": [P, 2, D], "wdown": [P, 2, DL], "upk": [DL, D], "upv": [DL, D],
              "cq": [P, 2, D], "ck": [P, 2, D], "cv": [P, 2, D], "coT": [P, 2, D],
              "dkT": [P, D], "dvT": [P, D], "uk": [P, D], "uv": [P, D], 
              "bdk": [P, 1], "bdv": [P, 1], "buk": [P, 2], "buv": [P, 2], "dwo": [P, 2, D], "bo": [P, D]}
    BANKS = ["a_wk", "a_wv", "c_wg", "c_wv", "d_wk", "d_wv"]
    with ExitStack() as ctx:
        t = {n: ctx.enter_context(nc.sbuf_tensor(f"fold_{n}", s, F32)) for n, s in SHAPES.items() if n in w}
        lat = ctx.enter_context(nc.sbuf_tensor("fold_lat", [DL, D], F32))
        res = ctx.enter_context(nc.sbuf_tensor("fold_res", [P, len(BANKS), 2 * D], F32))
        kb = ctx.enter_context(nc.sbuf_tensor("fold_kb", [P, 2], F32))
        vb = ctx.enter_context(nc.sbuf_tensor("fold_vb", [P, 2], F32))
        vbw = ctx.enter_context(nc.sbuf_tensor("fold_vbw", [P, 2, P], F32))
        xb = ctx.enter_context(nc.sbuf_tensor("fold_xb", [P, D], F32))
        psF = ctx.enter_context(nc.psum_tensor("fold_products", [P, 8, S], F32))

        def sem(name):
            return nc.alloc_semaphore(f"fold_{name}")

        loaded = {n: sem(f"{n}_loaded") for n in ("a", "c", "d")}
        lat_ready, lat_taken = sem("lat_ready"), sem("lat_taken")
        bias_ready, bias_done, xb_ready = sem("bias_ready"), sem("bias_done"), sem("xb_ready")
        ready, taken, stored = sem("ready"), sem("taken"), sem("stored")
        groups = {"a": ["wkT", "wvT", "wdown", "upk", "upv"], "c": ["cq", "ck", "cv", "coT"],
                  "d": ["dkT", "dvT", "uk", "uv", "bdk", "bdv", "buk", "buv", "dwo", "bo"]}
        block = ctx.enter_context(nc.Block())

        @block.sync
        def _(sp):
            for grp, names in groups.items():
                for n in names:
                    sp.dma_start(t[n][tuple(slice(None) for _ in SHAPES[n])], w[n]).then_inc(loaded[grp], 16)
            for i, n in enumerate(BANKS):
                sp.wait_ge(taken, i + 1)
                sp.dma_start(folded[n].rearrange("p c d -> p (c d)"), res[:, i, :]).then_inc(stored, 16)
            sp.wait_ge(bias_done, 2)
            sp.dma_start(folded["d_kb"], kb[:, :]).then_inc(stored, 16)
            sp.wait_ge(bias_done, 4)
            sp.dma_start(folded["d_xb"], xb[:, :]).then_inc(stored, 16)
            sp.wait_ge(stored, 16 * (len(BANKS) + 2))

        @block.tensor
        def _(pe):
            pe.wait_ge(loaded["a"], 16 * len(groups["a"]))
            for i, n in enumerate(("wkT", "wvT")):
                for c in range(2):
                    last = pe.matmul(psF[0:DL, 0, 0:D], t["wdown"][:, c, :], t[n][:, c, :], start=(i + c == 0),
                                     stop=(i + c == 2))
            last.then_inc(lat_ready, 1)
            pe.wait_ge(lat_taken, 1)
            for bank, n in ((1, "upk"), (2, "upv")):
                for m in range(2):
                    last = pe.matmul(psF[:, bank, m * D:(m + 1) * D], lat[:, m * P:(m + 1) * P], t[n][:, :],
                                     start=True, stop=True)
                last.then_inc(ready, 1)
            pe.wait_ge(loaded["c"], 16 * len(groups["c"]))
            for bank, a, b in ((3, "cq", "ck"), (4, "cv", "coT")):
                for m in range(2):
                    for c in range(2):
                        last = pe.matmul(psF[:, bank, m * D:(m + 1) * D], t[a][:, c, m * P:(m + 1) * P], t[b][:, c, :],
                                         start=(c == 0), stop=(c == 1))
                last.then_inc(ready, 1)
            pe.wait_ge(loaded["d"], 16 * len(groups["d"]))
            for bank, a, b in ((5, "dkT", "uk"), (6, "dvT", "uv")):
                for m in range(2):
                    last = pe.matmul(psF[:, bank, m * D:(m + 1) * D], t[a][:, m * P:(m + 1) * P], t[b][:, :],
                                     start=True, stop=True)
                last.then_inc(ready, 1)
            for i, (up, b) in enumerate((("uk", "bdk"), ("uv", "bdv"))):
                for m in range(2):
                    last = pe.matmul(psF[:, 0, 2 * i + m:2 * i + m + 1], t[up][:, m * P:(m + 1) * P], t[b][:, :],
                                     start=True, stop=True)
            last.then_inc(bias_ready, 1)
            pe.wait_ge(bias_done, 3)
            for m in range(2):
                last = pe.matmul(psF[:, 7, 0:D], vbw[:, m, :], t["dwo"][:, m, :], start=(m == 0), stop=(m == 1))
            last.then_inc(xb_ready, 1)

        @block.scalar
        def _(act):
            act.wait_ge(lat_ready, 1)
            act.copy(lat[:, :], psF[0:DL, 0, 0:D]).then_inc(lat_taken, 1)
            for i in range(len(BANKS)):
                act.wait_ge(ready, i + 1)
                act.copy(res[:, i, :], psF[:, i + 1, :]).then_inc(taken, 1)

        @block.vector
        def _(dve):
            dve.wait_ge(bias_ready, 1)
            dve.tensor_tensor(vb[:, :], psF[:, 0, 2:4], t["buv"][:, :], ALU.add).then_inc(bias_done, 1)
            dve.tensor_tensor(kb[:, :], psF[:, 0, 0:2], t["buk"][:, :], ALU.add).then_inc(bias_done, 1)
            dve.wait_ge(bias_done, 2)
            dve.tensor_copy(vbw[:, :, :], vb[:, :].unsqueeze(2).to_broadcast([P, 2, P])).then_inc(bias_done, 1)
            dve.wait_ge(xb_ready, 1)
            dve.tensor_tensor(xb[:, :], psF[:, 7, 0:D], t["bo"][:, :], ALU.add).then_inc(bias_done, 1)


def mha_layer(nc, g, ins, decay, scale, project_q, biased):
    X, MV, RSTD = g["X"], g["MV"], g["RSTD"]
    ident, identb = g["ident"], g["identb"]
    NV = 2 if decay else 1
    NCH = 4 * NV
    NA = 64 if decay else 32
    NAG = NA // 4
    A_AT = [0, 1, 2, 3, 4, 5, 6, 7, 8, 8, 9, 9, 10, 10, 11, 11] if decay else [0, 2, 3, 5, 6, 8, 9, 11]
    ROW_DMAS = 3 * NV
    PSLOTS = 4 if decay else 2
    XN = 4 if project_q else 8
    PV_AT = 3 if decay else 1
    KQ = ["k0", "k1"] + (["q0", "q1"] if project_q else [])
    PRO = ["xT0", "xT1"] + KQ + ["v0", "v1"]
    PREV = ["OT3", "aT0", "aT1", "Wo0", "Wo1"]
    USES = [(4 + 2 * decay, "OT3"), (7, "xT0"), (8, "xT1"), (10, "k0"), (12, "aT0"), (13, "mT1"), (15, "k1"),
            (17, "aT1"), (19, "q0"), (20 + 2 * decay, "OT0"), (23, "q1"), (24, "Wo0"), (26, "Wo1"), (28, "v0"),
            (29, "mT2"), (31, "v1"), (37 + 2 * decay, "OT1"), (45, "mT3"), (53 + 2 * decay, "OT2"), (61, "mT0")]
    USES = [u for u in USES if u[1] in PRO + PREV + ["OT0", "OT1", "OT2", "mT0", "mT1", "mT2", "mT3"]]
    MID = [n for _, n in USES]
    ORDER = {"pre": PRO + ["mT0"], "first": [n for n in MID if n not in PREV], "mid": MID,
             "last": [n for n in MID if n not in PRO + ["mT0"]], "post": PREV}
    BY_ACT = PRO + ["mT0", "mT1", "mT2", "mT3", "aT0", "aT1"]
    CHAINS = [(o, c, v) for o in "kq" for c in range(2) for v in range(NV)]
    USE_STEP = {n: s for s, n in USES}
    START = []
    for o, c, v in CHAINS:
        at = USE_STEP.get(f"{o}{c}", USE_STEP["k1"] + 4 + 3 * c) + 2 + 2 * v
        START.append(max(at, START[-1] + 2) if START else at)

    def base(tag, b):
        if tag == "pre":
            return 0
        if tag == "first":
            return len(ORDER["pre"])
        if tag == "post":
            return base("last", NB - 1) + len(ORDER["last"])
        return (b - 1) * len(MID) + (len(ORDER["pre"]) + len(ORDER["first"]))

    def use(tag, b, name):
        return base(tag, b) + ORDER[tag].index(name)

    with ExitStack() as ctx:
        def sb(name, shape, dt):
            return ctx.enter_context(nc.sbuf_tensor(f"{g['layer']}_{name}", shape, dt))

        def sem(name):
            return nc.alloc_semaphore(f"{g['layer']}_{name}")

        psA = ctx.enter_context(nc.psum_tensor(f"{g['layer']}_scores_q", [P, 4, S], F32))
        psB = ctx.enter_context(nc.psum_tensor(f"{g['layer']}_scores_k", [P, 2, S], F32))
        psO = ctx.enter_context(nc.psum_tensor(f"{g['layer']}_out_heads", [P, S], F32))
        psM = ctx.enter_context(nc.psum_tensor(f"{g['layer']}_work", [P, S], F32))
        psMb = psM[:, :].bitcast(BF16)

        wk, wv, wo = (sb(n, [P, 2, D], F32) for n in ("wk", "wv", "wo"))
        wq = sb("wq", [P, 2, D], F32) if project_q else None
        xn, xnT = sb("xn", [P, 4, D], F32), sb("xnT", [P, 2, S], F32)
        f, fc = sb("f", [P, 2, S], F32), sb("fc", [P, 2, S], F32)
        rr = sb("rr", [P, 2, S], F32)
        parts = sb("parts", [P, 2, 3, S], BF16)
        QS = sb("QS", [99, NV, 2, 8, S], BF16)
        KS = sb("KS", [99, NV, 2, 8, S], BF16)
        probs = sb("probs", [P, PSLOTS, 4, S], F32)
        Vraw, Vaug = sb("Vraw", [P, 4, D], F32), sb("Vaug", [P, 4, H, 32], F32)
        mx, mr = sb("mx", [P, 4, 4], F32), sb("mr", [P, 4, 4], F32)
        mp, mT = sb("mp", [P, 4, 3, 4], BF16), sb("mT", [12, S], BF16)
        Osb = sb("Osb", [P, S], F32)
        rec = sb("rec", [P, 4, 4], F32)
        attn, attnT = sb("attn", [P, 4, D], F32), sb("attnT", [P, 2, S], F32)
        st, mv = sb("st", [P, 2, 6], F32), sb("mv", [P, 2, 2], F32)
        if decay:
            tab = sb("tab", [P, 2, S], F32)
            corr = sb("corr", [P, 4, S], F32)
            low = sb("low", [P, 2, 4, P], F32)
            junk = sb("junk", [P, 2, S], BF16)
        else:
            tab = sb("tab", [P, 2, S], F32)
            sh = sb("sh", [P, 2, S], F32)
        if biased:
            kb = sb("kb", [P, 2], F32)
            xb = sb("xb", [P, D], F32)
        scr = nc.dram_tensor(f"{g['layer']}_parts_dram", [2, NV, 2, 3, P, S], BF16, kind="Internal").ap()

        loaded = sem("loaded")
        folded = sem("folded")
        ones_set = sem("ones_set")
        root, rstd_done = sem("root"), sem("rstd_done")
        xn_ready = sem("xn_ready")
        xbias_done = sem("xbias_done")
        m_ready = sem("work_ready")
        m_taken = sem("work_taken")
        rot_done, sin_done, sum_done = sem("rot_done"), sem("sin_done"), sem("sum_done")
        p0_done, r1_done, p1_done, p2_done = (sem(n) for n in ("p0_done", "r1_done", "p1_done", "p2_done"))
        scr_written = [sem(f"scr_written{i}") for i in range(2)]
        half_loaded = [sem(f"half_loaded{i}") for i in range(2)]
        a_ready, a_done = sem("a_ready"), sem("a_done")
        ms_done = sem("max_split")
        rows_loaded = sem("rows_loaded")
        b_ready, exp_done = sem("b_ready"), sem("exp_done")
        e_ready, e_exp, sel_done = sem("e_ready"), sem("e_exp"), sem("sel_done")
        vaug_done, pv_done, o_taken = sem("vaug_done"), sem("pv_done"), sem("o_taken")
        rec_done = sem("rec_done")
        bns_done, agg_done = sem("bns_done"), sem("agg_done")
        NLOAD = len(ins["load"])

        tiles = {"wq": wq, "wk": wk, "wv": wv, "wo": wo, "tab": tab}
        if decay:
            tiles["corr"] = corr
        if biased:
            tiles["kb"], tiles["xb"] = kb, xb

        def wait_parts(eng, nb, j):
            cnt = nb * (16 * NCH // 2) + 16 * (j // 2)
            if not (isinstance(cnt, int) and cnt == 0):
                eng.wait_ge(scr_written[j % 2], cnt)

        block = ctx.enter_context(nc.Block())

        @block.sync
        def _(sp):
            for name, src in ins["load"]:
                sp.dma_start(tiles[name][:], src).then_inc(loaded, 16)

            def write_parts(nb, j):
                o, c, v = CHAINS[j]
                sp.wait_ge(p2_done, nb * NCH + (j + 1))
                sp.dma_start(scr["kq".index(o), v, c].rearrange("s p t -> p s t"), parts[:, j % 2, :, :]).then_inc(
                    scr_written[j % 2], 16)

            def load_half(nb, c):
                for n in range(2):
                    sp.wait_ge(scr_written[n], (nb + 1) * (16 * NCH // 2))
                for v in range(NV):
                    k3, q3 = scr[0, v, c], scr[1, v, c]
                    for at, n in ((0, 3), (48, 2), (80, 1)):
                        dst = KS[at:at + 16 * n, v, c, :, :].rearrange("p h t -> p (h t)")
                        src = k3[0:n].rearrange("s (d h) t -> (s d) (h t)", d=16)
                        sp.dma_start(dst, src).then_inc(half_loaded[c], 16)
                    for part, (at, n) in enumerate(((0, 3), (48, 2), (80, 1))):
                        dst = QS[at:at + 16 * n, v, c, :, :].rearrange("p h t -> p (h t)")
                        one = q3[part].rearrange("(d h) t -> d (h t)", d=16)
                        src = bass.AP(one.tensor, one.offset, [[0, n]] + [list(x) for x in one.ap])
                        sp.dma_start(dst, src if n > 1 else one).then_inc(half_loaded[c], 16)

            def max_rows(tag, b, nb, grp):
                sp.wait_ge(m_taken, use(tag, b, f"mT{grp}") + 1)
                c, h0 = grp // 2, 4 * (grp % 2)
                for v in range(NV):
                    for s in range(3):
                        sp.dma_start(QS[96 + s:97 + s, v, c, h0:h0 + 4, :], mT[4 * s:4 * s + 4, :]).then_inc(
                            rows_loaded, 16)

            for j in range(NCH):
                write_parts(0, j)
            load_half(0, 0)
            max_rows("pre", 0, 0, 0)

            def body(tag, b):
                if tag != "first":
                    sp.wait_ge(b_ready, apart(sp, b * 64, loaded))
                    if decay:
                        sp.wait_ge(e_ready, b * 16)
                load_half(b, 1)
                if tag == "last":
                    for grp in (1, 2, 3):
                        max_rows(tag, b, b, grp)
                    return
                max_rows(tag, b, b, 1)
                for c in range(2):
                    sp.wait_ge(half_loaded[c], (b + 1) * (16 * 6 * NV))
                cut = NCH // 2 + 1
                for j in range(cut):
                    write_parts(b + 1, j)
                max_rows(tag, b, b, 2)
                for j in range(cut, NCH):
                    write_parts(b + 1, j)
                sp.wait_ge(b_ready, apart(sp, b * 64 + 32, loaded))
                if decay:
                    sp.wait_ge(e_ready, b * 16 + 8)
                load_half(b + 1, 0)
                max_rows(tag, b, b, 3)
                max_rows(tag, b, b + 1, 0)

            body("first", 0)
            with sp.Fori(1, NB - 1) as b:
                body("mid", b)
            body("last", NB - 1)

        @block.tensor
        def _(pe):
            pe.wait_ge(loaded, 16 * NLOAD)

            def open_work(tag, b, name):
                n = use(tag, b, name)
                if not (isinstance(n, int) and n == 0):
                    pe.wait_ge(m_taken, n)

            def work(tag, b, nb, name):
                open_work(tag, b, name)
                kind, n = name[:-1], int(name[-1])
                if kind == "xT":
                    pe.wait_ge(xn_ready, (nb + 1) * XN)
                    for t in range(4):
                        src = xn[:, t, n * P:(n + 1) * P]
                        last = pe.transpose(psM[:, t * P:(t + 1) * P], src, ident[:, :])
                elif kind in "kq":
                    w = wk if kind == "k" else wq
                    for c in range(2):
                        last = pe.matmul(psM[:, :], w[:, c, n * P:(n + 1) * P], xnT[:, c, :], start=(c == 0), stop=(c == 1))
                elif kind == "v":
                    for t in range(2):
                        for c in range(2):
                            tok = (2 * n + t) * P
                            last = pe.matmul(psM[:, t * D:(t + 1) * D], xnT[:, c, tok:tok + P], wv[:, c, :],
                                             start=(c == 0), stop=(c == 1))
                elif kind == "mT":
                    grp = nb * 4 + n
                    pe.wait_ge(ms_done, grp * 4 + 4)
                    for t in range(4):
                        last = pe.transpose(psMb[0:12, t * P:(t + 1) * P],
                                            mp[:, t, :, :].rearrange("p s h -> p (s h)"), identb[:, :])
                elif kind == "OT":
                    pe.wait_ge(o_taken, nb * 4 + (n + 1))
                    for t in range(4):
                        last = pe.transpose(psM[:, t * P:(t + 1) * P], Osb[:, t * P:(t + 1) * P], ident[:, :])
                elif kind == "aT":
                    for t in range(4):
                        last = pe.transpose(psM[:, t * P:(t + 1) * P], attn[:, t, n * P:(n + 1) * P], ident[:, :])
                elif kind == "Wo":
                    for t in range(2):
                        for c in range(2):
                            tok = (2 * n + t) * P
                            last = pe.matmul(psM[:, t * D:(t + 1) * D], attnT[:, c, tok:tok + P], wo[:, c, :],
                                             start=(c == 0), stop=(c == 1))
                last.then_inc(m_ready, 1)

            def max_scores(nb, grp, a):
                n = nb * NA + (grp * NAG + a)
                if a == 0:
                    pe.wait_ge(half_loaded[grp // 2], (nb + 1) * (16 * 6 * NV))
                c, h0 = grp // 2, 4 * (grp % 2)
                if decay:
                    qt, h = divmod(a, 4)
                    if not (isinstance(n, int) and n < 2):
                        pe.wait_ge(a_done, n - 1)
                    pe.matmul(psA[:, a % 2, :], QS[0:96, 0, c, h0 + h, qt * P:(qt + 1) * P],
                              KS[0:96, 1, c, h0 + h, :], start=True, stop=True).then_inc(a_ready, 1)
                else:
                    qt, pair = divmod(a, 2)
                    if not (isinstance(n, int) and n < 2):
                        pe.wait_ge(a_done, n - 1)
                    for i in range(2):
                        hh = h0 + 2 * pair + i
                        last = pe.matmul(psA[:, 2 * (a % 2) + i, :], QS[0:96, 0, c, hh, qt * P:(qt + 1) * P],
                                         KS[0:96, 0, c, hh, :], start=True, stop=True)
                    last.then_inc(a_ready, 1)

            def exp_scores(b, s):
                grp, kt, h = s // 16, s // 4 % 4, s % 4
                c, hh = grp // 2, 4 * (grp % 2) + h
                if s % 16 == 0:
                    pe.wait_ge(rows_loaded, (b * 4 + (grp + 1)) * (16 * ROW_DMAS))
                if not (isinstance(b, int) and b * 64 + s < 2):
                    pe.wait_ge(exp_done, b * 64 + (s - 1))
                keys = slice(kt * P, (kt + 1) * P)
                if not decay:
                    last = pe.matmul(psB[:, s % 2, :], KS[:, 0, c, hh, keys], QS[:, 0, c, hh, :], start=True, stop=True)
                else:
                    end = (kt + 1) * P
                    last = pe.matmul(psB[:, s % 2, 0:end], KS[:, 1, c, hh, keys], QS[:, 0, c, hh, 0:end],
                                     start=True, stop=True)
                    if end < S:
                        last = pe.matmul(psB[:, s % 2, end:S], KS[:, 0, c, hh, keys], QS[:, 1, c, hh, end:S],
                                         start=True, stop=True)
                last.then_inc(b_ready, 1)
                if decay and h == 3:
                    kk = s // 4
                    if not (isinstance(b, int) and b * 16 + kk < 1):
                        pe.wait_ge(e_exp, b * 16 + kk)
                    for i in range(4):
                        hh = 4 * (grp % 2) + i
                        last = pe.matmul(psA[:, 3, i * P:(i + 1) * P], KS[:, 0, c, hh, keys], QS[:, 1, c, hh, keys],
                                         start=True, stop=True)
                    last.then_inc(e_ready, 1)

            def value_sums(b, kk):
                grp, kt = kk // 4, kk % 4
                if kk == 0:
                    pe.wait_ge(vaug_done, b + 1)
                if kt == 0 and not (isinstance(b, int) and b * 4 + grp < 1):
                    pe.wait_ge(o_taken, b * 4 + grp)
                pe.wait_ge(sel_done if decay else exp_done, (b * 16 + (kk + 1)) * (2 if decay else 4))
                if decay and kt:
                    for h in range(4):
                        pe.matmul(psO[32 * h:32 * h + 32, kt * P:(kt + 1) * P], Vaug[:, kt, 4 * grp + h, :],
                                  low[:, kk % 2, h, :], start=False, stop=False)
                for h in range(4):
                    last = pe.matmul(psO[32 * h:32 * h + 32, :], Vaug[:, kt, 4 * grp + h, :],
                                     probs[:, kk % PSLOTS, h, :], start=(kt == 0), stop=(kt == 3))
                if decay and not kt:
                    for h in range(4):
                        last = pe.matmul(psO[32 * h:32 * h + 32, 0:P], Vaug[:, kt, 4 * grp + h, :],
                                         low[:, kk % 2, h, :], start=False, stop=False)
                last.then_inc(pv_done, 1)

            for name in ORDER["pre"][:-1]:
                work("pre", 0, 0, name)
            for a in range(NAG):
                max_scores(0, 0, a)
            work("pre", 0, 0, "mT0")

            def body(tag, b):
                for s in range(64):
                    grp, o = divmod(s, 16)
                    exp_scores(b, s)
                    if o % 4 == PV_AT:
                        if s > PV_AT:
                            value_sums(b, s // 4 - 1)
                        elif tag != "first":
                            value_sums(b - 1, 15)
                    if not (tag == "last" and grp == 3):
                        for a in range(NAG):
                            if A_AT[a] == o:
                                max_scores(b + 1 if grp == 3 else b, (grp + 1) % 4, a)
                    for at, name in USES:
                        if at == s and name in ORDER[tag]:
                            nb = b - 1 if name in PREV else b + 1 if name in PRO + ["mT0"] else b
                            work(tag, b, nb, name)

            body("first", 0)
            with pe.Fori(1, NB - 1) as b:
                body("mid", b)
            body("last", NB - 1)
            value_sums(NB - 1, 15)
            for name in ORDER["post"]:
                work("post", NB, NB - 1, name)

        @block.scalar
        def _(act):
            act.activation(RSTD[:, 1, :], MV[:, :, 1], ACT.Sqrt, bias=g["eps"][:, :]).then_inc(root, 1)
            act.wait_ge(loaded, 16 * NLOAD)

            def take(tag, b, nb, name):
                act.wait_ge(m_ready, use(tag, b, name) + 1)
                kind, n = name[:-1], int(name[-1])
                if kind == "xT":
                    if not project_q and not (isinstance(nb, int) and nb == 0):
                        act.wait_ge(rot_done, nb * 8)
                    ins_ = act.copy(xnT[:, n, :], psM[:, :])
                elif kind in "kq":
                    u = 2 * (kind == "q") + n
                    cnt = nb * 8 + (2 * u - 2)
                    if not (isinstance(cnt, int) and cnt <= 0):
                        act.wait_ge(rot_done, cnt)
                    if biased:
                        ins_ = act.activation(f[:, n, :], psM[:, :], ACT.Identity, bias=kb[:, n:n + 1])
                    else:
                        ins_ = act.copy(f[:, n, :], psM[:, :])
                elif kind == "v":
                    if not (isinstance(nb, int) and nb == 0):
                        act.wait_ge(vaug_done, nb)
                    ins_ = act.copy(Vraw[:, 2 * n:2 * n + 2, :].rearrange("p t d -> p (t d)"), psM[:, :])
                elif kind == "mT":
                    grp = nb * 4 + n
                    if not (isinstance(grp, int) and grp == 0):
                        act.wait_ge(rows_loaded, grp * (16 * ROW_DMAS))
                    ins_ = act.copy(mT[:, :], psMb[0:12, 0:S])
                else:
                    ins_ = act.copy(attnT[:, n, :], psM[:, :])
                ins_.then_inc(m_taken, 1)

            def middle_part(nb, j):
                act.wait_ge(r1_done, nb * NCH + (j + 1))
                wait_parts(act, nb, j)
                act.copy(parts[:, j % 2, 1, :], rr[:, j % 2, :]).then_inc(p1_done, 1)

            for name in ORDER["pre"][:2]:
                take("pre", 0, 0, name)
            for i, (o, c, v) in enumerate(CHAINS):
                if v == 0 and f"{o}{c}" in PRO:
                    take("pre", 0, 0, f"{o}{c}")
                if i:
                    middle_part(0, i - 1)
            middle_part(0, NCH - 1)
            for name in ("v0", "v1", "mT0"):
                take("pre", 0, 0, name)

            def take_heads(b, grp):
                act.wait_ge(pv_done, b * 16 + (4 * grp + 4))
                n = b * 4 + grp
                act.copy(Osb[:, :], psO[:, :]).then_inc(o_taken, 1)

            def body(tag, b):
                for s in range(64):
                    grp, o = divmod(s, 16)
                    kk, h = s // 4, s % 4
                    if h == 0 and not (isinstance(b, int) and b * 16 + kk < PSLOTS):
                        act.wait_ge(pv_done, b * 16 + (kk - PSLOTS + 1))
                    act.wait_ge(b_ready, b * 64 + (s + 1))
                    act.activation(probs[:, kk % PSLOTS, h, :], psB[:, s % 2, :], ACT.Exp, scale=scale).then_inc(
                        exp_done, 1)
                    if decay and h == 3:
                        act.wait_ge(e_ready, b * 16 + (kk + 1))
                        if not (isinstance(b, int) and b * 16 + kk < 2):
                            act.wait_ge(pv_done, b * 16 + (kk - 1))
                        act.activation(low[:, kk % 2, :, :].rearrange("p h q -> p (h q)"), psA[:, 3, :], ACT.Exp,
                                       scale=scale).then_inc(e_exp, 1)
                    if o == PV_AT + 1:
                        if grp:
                            take_heads(b, grp - 1)
                        elif tag != "first":
                            take_heads(b - 1, 3)
                    for at, name in USES:
                        if at + 1 == s and name in ORDER[tag] and name in BY_ACT:
                            nb = b - 1 if name in PREV else b + 1 if name in PRO + ["mT0"] else b
                            take(tag, b, nb, name)
                    if tag != "last":
                        for j in range(NCH):
                            if START[j] + 6 == s:
                                middle_part(b + 1, j)

            body("first", 0)
            with act.Fori(1, NB - 1) as b:
                body("mid", b)
            body("last", NB - 1)
            take_heads(NB - 1, 3)
            for name in ("aT0", "aT1"):
                take("post", NB, NB - 1, name)

        @block.vector
        def _(dve):
            dve.memset(Vaug[:, :, :, 16:32], 1.0).then_inc(ones_set, 1)
            for v in range(NV):
                dve.memset(KS[96:99, v, :, :, :], 1.0).then_inc(ones_set, 1)
            dve.wait_ge(root, 1)
            dve.reciprocal(RSTD[:, 0, :], RSTD[:, 1, :]).then_inc(rstd_done, 1)
            dve.wait_ge(rstd_done, 1)
            dve.wait_ge(ones_set, 1 + NV)
            dve.wait_ge(loaded, 16 * NLOAD)

            def normalise(nb, t):
                i = nb * 4 + t
                if project_q:
                    dve.tensor_scalar(xn[:, t, :], X[:, i, :], MV[:, i, 0:1], RSTD[:, 0, bass.ds(i, 1)],
                                      ALU.subtract, ALU.mult).then_inc(xn_ready, 1)
                    return
                for c in range(2):
                    half = slice(c * P, (c + 1) * P)
                    dve.tensor_scalar(xn[:, t, half].rearrange("p (a y h) -> p h y a", a=8, y=2),
                                      X[:, i, half].rearrange("p (h y a) -> p h y a", y=2, a=8), MV[:, i, 0:1],
                                      RSTD[:, 0, bass.ds(i, 1)], ALU.subtract, ALU.mult).then_inc(xn_ready, 1)

            def rotate(tag, b, nb, j):
                o, c, v = CHAINS[j]
                if project_q or o == "k":
                    dve.wait_ge(m_taken, apart(dve, use(tag, b, f"{o}{c}") + 1, loaded))
                    src = f[:, c, :]
                else:
                    dve.wait_ge(m_taken, apart(dve, use(tag, b, "xT1") + 1, loaded))
                    src = xnT[:, c, :]
                cnt = nb * NCH + (j - 1)
                if not (isinstance(cnt, int) and cnt <= 0):
                    dve.wait_ge(r1_done, apart(dve, cnt, loaded))
                if decay:
                    dve.tensor_tensor(fc[:, j % 2, :], src, tab[:, v, :], ALU.mult).then_inc(rot_done, 1)
                else:
                    dve.stream_shuffle(sh[:, j % 2, :], src, [i ^ 8 for i in range(32)]).then_inc(rot_done, 1)
                    dve.tensor_tensor(fc[:, j % 2, :], src, tab[:, 0, :], ALU.mult).then_inc(rot_done, 1)

            def first_part(nb, j):
                if decay:
                    dve.wait_ge(rot_done, nb * 8 + (j + 1))
                else:
                    dve.wait_ge(sum_done, nb * NCH + (j + 1))
                wait_parts(dve, nb, j)
                dve.tensor_copy(parts[:, j % 2, 0, :], fc[:, j % 2, :]).then_inc(p0_done, 1)

            def maxima(nb, grp, a):
                n = nb * NA + (grp * NAG + a)
                dve.wait_ge(a_ready, apart(dve, n + 1, loaded))
                if a == 0 and not (isinstance(nb, int) and nb * 4 + grp == 0):
                    dve.wait_ge(ms_done, apart(dve, (nb * 4 + grp) * 4, loaded))
                if decay:
                    qt, h = divmod(a, 4)
                    if not (isinstance(n, int) and n < 2):
                        dve.wait_ge(a_done, apart(dve, n - 1, loaded))
                    dve.tensor_tensor_reduce(junk[:, a % 2, :], psA[:, a % 2, :], corr[:, qt, :], 1.0, -3.0e38, ALU.mult,
                                             ALU.max, mx[:, qt, h:h + 1]).then_inc(a_done, 1)
                else:
                    qt, pair = divmod(a, 2)
                    i = 2 * (a % 2)
                    dve.tensor_reduce(mx[:, qt, 2 * pair:2 * pair + 2], psA[:, i:i + 2, :], AX.X,
                                      ALU.max).then_inc(a_done, 1)

            def split_maxima(tag, b, nb, grp):
                n = nb * 4 + grp
                dve.wait_ge(a_done, (n + 1) * NAG)
                dve.wait_ge(m_ready, use(tag, b, f"mT{grp}"))
                flat = mx[:, :, :]
                dve.tensor_scalar(mp[:, :, 0, :], flat, -1.0, None, ALU.mult).then_inc(ms_done, 1)
                dve.wait_ge(ms_done, n * 4 + 1)
                dve.scalar_tensor_tensor(mr[:, :, :], flat, -1.0, mp[:, :, 0, :], ALU.mult, ALU.subtract).then_inc(
                    ms_done, 1)
                dve.wait_ge(ms_done, n * 4 + 2)
                dve.tensor_copy(mp[:, :, 1, :], mr[:, :, :]).then_inc(ms_done, 1)
                dve.wait_ge(ms_done, n * 4 + 3)
                dve.tensor_tensor(mp[:, :, 2, :], mr[:, :, :], mp[:, :, 1, :], ALU.subtract).then_inc(ms_done, 1)

            def lay_values(tag, b):
                if tag == "first":
                    dve.wait_ge(m_taken, use("pre", 0, "v1") + 1)
                else:
                    dve.wait_ge(m_taken, base(tag, b))
                    dve.wait_ge(pv_done, b * 16)
                dve.tensor_copy(Vaug[:, :, :, 0:16], Vraw[:, :, :].rearrange("p t (h d) -> p t h d", d=16)).then_inc(
                    vaug_done, 1)

            def normalise_heads(tag, b, nb, name):
                n = use(tag, b, name)
                grp = int(name[-1])
                dve.wait_ge(m_ready, n + 1)
                ov = psM[:, :].rearrange("p (t h e) -> p t h e", t=4, h=4)
                dve.reciprocal(rec[:, :, :], ov[:, :, :, 16]).then_inc(rec_done, 1)
                dve.wait_ge(rec_done, nb * 4 + (grp + 1))
                dve.tensor_tensor(attn[:, :, 64 * grp:64 * grp + 64].rearrange("p t (h d) -> p t h d", d=16),
                                  ov[:, :, :, 0:16], rec[:, :, :].unsqueeze(3).to_broadcast([P, 4, 4, 16]),
                                  ALU.mult).then_inc(m_taken, 1)

            def add_out(tag, b, nb, name):
                j = int(name[-1])
                n = use(tag, b, name)
                dve.wait_ge(m_ready, n + 1)
                if biased:
                    dve.wait_ge(xbias_done, nb + 1)
                i = nb * 4 + 2 * j
                xs = X[:, bass.ds(i, 2), :]
                dve.tensor_tensor(xs, xs, psM[:, :].rearrange("p (t d) -> p t d", t=2), ALU.add).then_inc(m_taken, 1)
                dve.wait_ge(m_taken, apart(dve, n + 1, loaded))
                for t in range(2):
                    dve.bn_stats(st[:, t, :], X[:, i + t, :]).then_inc(bns_done, 1)
                dve.wait_ge(bns_done, apart(dve, nb * 4 + (2 * j + 2), loaded))
                for t in range(2):
                    dve.bn_aggr(mv[:, t, :], st[:, t, :]).then_inc(agg_done, 1)
                dve.wait_ge(agg_done, nb * 4 + (2 * j + 2))
                dve.tensor_copy(MV[:, bass.ds(i, 2), :], mv[:, :, :])

            for t in range(4):
                normalise(0, t)
            for j in range(NCH):
                rotate("pre", 0, 0, j)
                if j:
                    first_part(0, j - 1)
            first_part(0, NCH - 1)
            for a in range(NAG):
                maxima(0, 0, a)
            split_maxima("pre", 0, 0, 0)

            def body(tag, b):
                for s in range(64):
                    grp, o = divmod(s, 16)
                    if s == 0 and tag != "last":
                        dve.wait_ge(m_ready, base(tag, b))
                    if s < 4 and tag != "last":
                        normalise(b + 1, s)
                    if s == 2:
                        lay_values(tag, b)
                    if not (tag == "last" and grp == 3):
                        nb, ng = (b + 1 if grp == 3 else b), (grp + 1) % 4
                        for a in range(NAG):
                            if A_AT[a] == o:
                                maxima(nb, ng, a)
                        if o == 12:
                            split_maxima(tag, b, nb, ng)
                    for at, name in USES:
                        if at + 1 == s and name in ORDER[tag] and name not in BY_ACT:
                            nb = b - 1 if name in PREV else b
                            (normalise_heads if name[:2] == "OT" else add_out)(tag, b, nb, name)
                    if tag != "last":
                        for j in range(NCH):
                            if START[j] == s:
                                rotate(tag, b, b + 1, j)
                            if START[j] + (1 if decay else 4) == s:
                                first_part(b + 1, j)

            body("first", 0)
            with dve.Fori(1, NB - 1) as b:
                body("mid", b)
            body("last", NB - 1)
            for name in ("OT3", "Wo0", "Wo1"):
                (normalise_heads if name[:2] == "OT" else add_out)("post", NB, NB - 1, name)

        @block.gpsimd
        def _(pool):
            pool.wait_ge(loaded, 16 * NLOAD)

            def chain(nb, j):
                n = nb * NCH + j
                if not decay:
                    pool.wait_ge(rot_done, nb * 8 + (2 * j + 2))
                    nc.gpsimd.tensor_tensor(sh[:, j % 2, :], sh[:, j % 2, :], tab[:, 1, :], ALU.mult).then_inc(
                        sin_done, 1)
                    pool.wait_ge(sin_done, n + 1)
                    nc.gpsimd.tensor_tensor(fc[:, j % 2, :], fc[:, j % 2, :], sh[:, j % 2, :], ALU.add).then_inc(
                        sum_done, 1)
                pool.wait_ge(p0_done, n + 1)
                nc.gpsimd.tensor_tensor(rr[:, j % 2, :], fc[:, j % 2, :], parts[:, j % 2, 0, :],
                                        ALU.subtract).then_inc(r1_done, 1)
                pool.wait_ge(p1_done, n + 1)
                nc.gpsimd.tensor_tensor(parts[:, j % 2, 2, :], rr[:, j % 2, :], parts[:, j % 2, 1, :],
                                        ALU.subtract).then_inc(p2_done, 1)

            def add_bias(nb):
                pool.wait_ge(xn_ready, (nb + 1) * XN)
                xs = X[:, bass.ds(nb * 4, 4), :]
                nc.gpsimd.tensor_tensor(xs, xs, xb[:, :].unsqueeze(1).to_broadcast([P, 4, D]), ALU.add).then_inc(
                    xbias_done, 1)

            def select(b, kk):
                kt = kk % 4
                pool.wait_ge(exp_done, apart(pool, b * 64 + (4 * kk + 4), loaded))
                diag = probs[:, kk % PSLOTS, :, kt * P:(kt + 1) * P]
                nc.gpsimd.affine_select(out=diag, in_=diag, compare_op=ALU.is_ge, fill=0.0, base=0,
                                        pattern=[[0, 4], [-1, P]], channel_multiplier=1).then_inc(sel_done, 1)
                pool.wait_ge(e_exp, apart(pool, b * 16 + (kk + 1), loaded))
                lo = low[:, kk % 2, :, :]
                nc.gpsimd.affine_select(out=lo, in_=lo, compare_op=ALU.is_ge, fill=0.0, base=-1,
                                        pattern=[[0, 4], [1, P]], channel_multiplier=-1).then_inc(sel_done, 1)

            if biased:
                add_bias(0)
            for j in range(NCH):
                chain(0, j)

            def body(tag, b):
                for s in range(64):
                    if decay and s % 4 == 3:
                        select(b, s // 4)
                    if tag != "last":
                        if biased and s == 4:
                            add_bias(b + 1)
                        for j in range(NCH):
                            if START[j] + 1 == s:
                                chain(b + 1, j)

            body("first", 0)
            with pool.Fori(1, NB - 1) as b:
                body("mid", b)
            body("last", NB - 1)
def single_head_layer(nc, g, ins):
    X, MV, RSTD, ident = g["X"], g["MV"], g["RSTD"], g["ident"]
    scale = 1.0 / D ** 0.5
    WI = 6
    with ExitStack() as ctx:
        def sb(name, shape):
            return ctx.enter_context(nc.sbuf_tensor(f"{g['layer']}_{name}", shape, F32))

        def ps(name, shape):
            return ctx.enter_context(nc.psum_tensor(f"{g['layer']}_{name}", shape, F32))

        def sem(name):
            return nc.alloc_semaphore(f"{g['layer']}_{name}")

        psW, psS = ps("work", [P, 2, S]), ps("scores", [P, 2, S])
        psP, psO = ps("probs_turned", [P, 2, S]), ps("out", [P, 2, S])
        wg, wv, xb, mask = sb("wg", [P, 2, D]), sb("wv", [P, 2, D]), sb("xb", [P, D]), sb("mask", [P, S])
        xn, xnT = sb("xn", [P, 2, 4, D]), sb("xnT", [P, 2, 2, S])
        tT, v = sb("tT", [P, 2, 2, S]), sb("v", [P, 2, 4, D])
        sc, pr, pT = sb("masked", [P, 2, S]), sb("probs", [P, 2, S]), sb("probsT", [P, 2, S])
        mx, nm = sb("mx", [P, 4]), sb("nm", [P, 4])
        total, rec = sb("total", [P, 4]), sb("rec", [P, 4])
        st, mv = sb("st", [P, 4, 6]), sb("mv", [P, 4, 2])

        loaded, root, rstd_done = sem("loaded"), sem("root"), sem("rstd_done")
        xn_ready, xbias_done = sem("xn_ready"), sem("xbias_done")
        w_ready, w_taken = sem("work_ready"), sem("work_taken")
        s_ready, max_done, nm_done, exp_done = sem("scores_ready"), sem("max_done"), sem("nm_done"), sem("exp_done")
        p_ready, pT_taken = sem("probs_turned"), sem("probsT_taken")
        o_ready, rec_done, added = sem("out_ready"), sem("rec_done"), sem("added")
        bns_done, agg_done = sem("bns_done"), sem("agg_done")
        block = ctx.enter_context(nc.Block())
        LOADS = [(wg, ins["wg"]), (wv, ins["wv"]), (xb, ins["xb"]), (mask, ins["mask"])]

        @block.sync
        def _(sp):
            for to, src in LOADS:
                sp.dma_start(to[tuple(slice(None) for _ in src.shape)], src).then_inc(loaded, 16)

        @block.tensor
        def _(pe):
            pe.wait_ge(loaded, 16 * len(LOADS))

            def work(b, p, i):
                n = b * WI + i
                if not (isinstance(n, int) and n < 2):
                    pe.wait_ge(w_taken, n - 1)
                if i < 2:
                    pe.wait_ge(xn_ready, b * 4 + 4)
                    for t in range(4):
                        last = pe.transpose(psW[:, i, t * P:(t + 1) * P], xn[:, p, t, i * P:(i + 1) * P], ident[:, :])
                elif i < 4:
                    pe.wait_ge(w_taken, b * WI + 2)
                    for c in range(2):
                        last = pe.matmul(psW[:, i % 2, :], wg[:, c, (i - 2) * P:(i - 1) * P], xnT[:, p, c, :],
                                         start=(c == 0), stop=(c == 1))
                else:
                    for t in range(2):
                        k = 2 * (i - 4) + t
                        for c in range(2):
                            last = pe.matmul(psW[:, i % 2, t * D:(t + 1) * D], xnT[:, p, c, k * P:(k + 1) * P],
                                             wv[:, c, :], start=(c == 0), stop=(c == 1))
                last.then_inc(w_ready, 1)

            def scores(b, p, qt):
                n = b * 4 + qt
                if not (isinstance(n, int) and n < 2):
                    pe.wait_ge(max_done, n - 1)
                pe.wait_ge(w_taken, b * WI + 4)
                W = (qt + 1) * P
                for c in range(2):
                    last = pe.matmul(psS[:, qt % 2, 0:W], tT[:, p, c, qt * P:W], xnT[:, p, c, 0:W], start=(c == 0), stop=(c == 1))
                last.then_inc(s_ready, 1)

            def turn(b, qt):
                n = b * 4 + qt
                pe.wait_ge(exp_done, n + 1)
                if not (isinstance(n, int) and n < 2):
                    pe.wait_ge(pT_taken, n - 1)
                for k in range(qt + 1):
                    last = pe.transpose(psP[:, qt % 2, k * P:(k + 1) * P], pr[:, qt % 2, k * P:(k + 1) * P], ident[:, :])
                last.then_inc(p_ready, 1)

            def values(b, p, qt):
                n = b * 4 + qt
                pe.wait_ge(pT_taken, n + 1)
                pe.wait_ge(w_taken, b * WI + 6)
                if not (isinstance(n, int) and n < 2):
                    pe.wait_ge(added, n - 1)
                for k in range(qt + 1):
                    last = pe.matmul(psO[:, qt % 2, 0:D], pT[:, qt % 2, k * P:(k + 1) * P], v[:, p, k, :],
                                     start=(k == 0), stop=(k == qt))
                last.then_inc(o_ready, 1)

            for i in range(WI):
                work(0, 0, i)
            scores(0, 0, 0)
            scores(0, 0, 1)

            def body(b, p, last=False):
                def ahead(i):
                    if not last:
                        work(b + 1, 1 - p, i)
                ahead(0)
                turn(b, 0)
                ahead(1)
                values(b, p, 0)
                scores(b, p, 2)
                turn(b, 1)
                ahead(2)
                values(b, p, 1)
                scores(b, p, 3)
                turn(b, 2)
                ahead(3)
                values(b, p, 2)
                ahead(4)
                turn(b, 3)
                ahead(5)
                if not last:
                    scores(b + 1, 1 - p, 0)
                values(b, p, 3)
                if not last:
                    scores(b + 1, 1 - p, 1)

            body(0, 0)
            body(1, 1)
            with pe.Fori(1, NB // 2 - 1) as j:
                body(j * 2, 0)
                body(j * 2 + 1, 1)
            body(NB - 2, 0)
            body(NB - 1, 1, True)

        @block.scalar
        def _(act):
            act.activation(RSTD[:, 1, :], MV[:, :, 1], ACT.Sqrt, bias=g["eps"][:, :]).then_inc(root, 1)

            def take(b, p, i):
                act.wait_ge(w_ready, b * WI + (i + 1))
                src = psW[:, i % 2, :]
                if i < 2:
                    if not (isinstance(b, int) and b < 2) and i == 0:
                        act.wait_ge(s_ready, b * 4 - 4)
                    act.copy(xnT[:, p, i, :], src).then_inc(w_taken, 1)
                elif i < 4:
                    act.copy(tT[:, p, i - 2, :], src).then_inc(w_taken, 1)
                else:
                    if not (isinstance(b, int) and b < 2) and i == 4:
                        act.wait_ge(o_ready, b * 4 - 4)
                    k = 2 * (i - 4)
                    act.copy(v[:, p, k:k + 2, :].rearrange("p t d -> p (t d)"), src).then_inc(w_taken, 1)

            def exps(b, qt):
                n = b * 4 + qt
                W = (qt + 1) * P
                act.wait_ge(nm_done, n + 1)
                if not (isinstance(n, int) and n < 2):
                    act.wait_ge(p_ready, n - 1)
                if not (isinstance(n, int) and n < 4):
                    act.wait_ge(rec_done, n - 3)
                act.activation(pr[:, qt % 2, 0:W], sc[:, qt % 2, 0:W], ACT.Exp, bias=nm[:, qt:qt + 1], scale=scale,
                               accum_out=total[:, qt:qt + 1]).then_inc(exp_done, 1)

            def take_probs(b, qt):
                n = b * 4 + qt
                W = (qt + 1) * P
                act.wait_ge(p_ready, n + 1)
                if not (isinstance(n, int) and n < 2):
                    act.wait_ge(o_ready, n - 1)
                act.copy(pT[:, qt % 2, 0:W], psP[:, qt % 2, 0:W]).then_inc(pT_taken, 1)

            for i in range(WI):
                take(0, 0, i)
            exps(0, 0)
            exps(0, 1)

            def body(b, p, last=False):
                def ahead(i):
                    if not last:
                        take(b + 1, 1 - p, i)
                ahead(0)
                take_probs(b, 0)
                ahead(1)
                exps(b, 2)
                take_probs(b, 1)
                ahead(2)
                exps(b, 3)
                take_probs(b, 2)
                ahead(3)
                ahead(4)
                take_probs(b, 3)
                ahead(5)
                if not last:
                    exps(b + 1, 0)
                    exps(b + 1, 1)

            body(0, 0)
            body(1, 1)
            with act.Fori(1, NB // 2 - 1) as j:
                body(j * 2, 0)
                body(j * 2 + 1, 1)
            body(NB - 2, 0)
            body(NB - 1, 1, True)

        @block.vector
        def _(dve):
            dve.wait_ge(root, 1)
            dve.reciprocal(RSTD[:, 0, :], RSTD[:, 1, :]).then_inc(rstd_done, 1)
            dve.wait_ge(rstd_done, 1)
            dve.wait_ge(loaded, 16 * len(LOADS))

            def normalise(b, p):
                if not (isinstance(b, int) and b < 2):
                    dve.wait_ge(w_ready, b * WI - 10)
                for t in range(4):
                    i = b * 4 + t
                    dve.tensor_scalar(xn[:, p, t, :], X[:, i, :], MV[:, i, 0:1], RSTD[:, 0, bass.ds(i, 1)],
                                      ALU.subtract, ALU.mult).then_inc(xn_ready, 1)

            def maximum(b, qt):
                n = b * 4 + qt
                W = (qt + 1) * P
                dve.wait_ge(s_ready, apart(dve, n + 1, loaded))
                if not (isinstance(n, int) and n < 2):
                    dve.wait_ge(exp_done, apart(dve, n - 1, loaded))
                dve.tensor_tensor_reduce(sc[:, qt % 2, 0:W], psS[:, qt % 2, 0:W], mask[:, S - W:S], 1.0, -3.0e38, ALU.add,
                                         ALU.max, mx[:, qt:qt + 1]).then_inc(max_done, 1)
                dve.wait_ge(max_done, n + 1)
                dve.tensor_scalar(nm[:, qt:qt + 1], mx[:, qt:qt + 1], -scale, None, ALU.mult).then_inc(nm_done, 1)

            def add_out(b, qt):
                n = b * 4 + qt
                dve.wait_ge(exp_done, n + 1)
                dve.reciprocal(rec[:, qt:qt + 1], total[:, qt:qt + 1]).then_inc(rec_done, 1)
                dve.wait_ge(rec_done, n + 1)
                dve.wait_ge(o_ready, n + 1)
                if qt == 0:
                    dve.wait_ge(xbias_done, b + 1)
                dve.scalar_tensor_tensor(X[:, n, :], psO[:, qt % 2, 0:D], rec[:, qt:qt + 1], X[:, n, :], ALU.mult,
                                         ALU.add).then_inc(added, 1)
                dve.wait_ge(added, apart(dve, n + 1, loaded))
                dve.bn_stats(st[:, qt, :], X[:, n, :]).then_inc(bns_done, 1)
                dve.wait_ge(bns_done, apart(dve, n + 1, loaded))
                dve.bn_aggr(mv[:, qt, :], st[:, qt, :]).then_inc(agg_done, 1)
                if qt == 3:
                    dve.wait_ge(agg_done, n + 1)
                    dve.tensor_copy(MV[:, bass.ds(b * 4, 4), :], mv[:, :, :])

            normalise(0, 0)
            normalise(1, 1)
            maximum(0, 0)
            maximum(0, 1)

            def body(b, p, more=True, last=False):
                maximum(b, 2)
                add_out(b, 0)
                maximum(b, 3)
                if more:
                    normalise(b + 2, p)
                add_out(b, 1)
                add_out(b, 2)
                if not last:
                    maximum(b + 1, 0)
                    maximum(b + 1, 1)
                add_out(b, 3)

            body(0, 0)
            body(1, 1)
            with dve.Fori(1, NB // 2 - 1) as j:
                body(j * 2, 0)
                body(j * 2 + 1, 1)
            body(NB - 2, 0, False)
            body(NB - 1, 1, False, True)

        @block.gpsimd
        def _(pool):
            pool.wait_ge(loaded, 16 * len(LOADS))
            with pool.Fori(0, NB) as b:
                pool.wait_ge(xn_ready, b * 4 + 4)
                xs = X[:, bass.ds(b * 4, 4), :]
                nc.gpsimd.tensor_tensor(xs, xs, xb[:, :].unsqueeze(1).to_broadcast([P, 4, D]), ALU.add).then_inc(
                    xbias_done, 1)




HEAD_DIMS = [a + HD // 2 * y for a in range(HD // 2) for y in range(2)]
COLS = [(8 * c + h) * HD + d for c in range(2) for d in HEAD_DIMS for h in range(8)]


def hybrid_stack(nc, w, out):
    with ExitStack() as ctx:
        g = global_tensors(nc, ctx)
        folded = {n: nc.dram_tensor(f"folded_{n}", s, F32, kind="Internal").ap() for n, s in FOLDED.items()}
        experts_a = {"wg": w["gate_a"], "bg": w["gate_bias"], "we": w["we"], "be": w["be"]}
        experts_b = {"wg": w["gate_b"], "w1": w["w1"], "w2": w["w2"], "out": out}
        decay = {"load": [("wk", folded["a_wk"]), ("tab", w["decay_tab"]), ("wq", w["a_wq"]), ("wv", folded["a_wv"]),
                          ("wo", w["a_wo"]), ("corr", w["corr"])]}
        rope = {"load": [("wk", w["b_wk"]), ("tab", w["rope_tab"]), ("wq", w["b_wq"]), ("wv", w["b_wv"]), ("wo", w["b_wo"])]}
        causal = {"wg": folded["c_wg"], "wv": folded["c_wv"], "xb": w["c_bias"], "mask": w["mask"]}
        latent = {"load": [("wk", folded["d_wk"]), ("tab", w["rope_tab"]), ("wv", folded["d_wv"]), ("wo", w["dwo"]),
                           ("kb", folded["d_kb"]), ("xb", folded["d_xb"])]}

        def layer(name):
            g["layer"] = name
            return nc.cleanup_on_exit()

        with layer("tokens"):
            load_tokens(nc, g, w)
        with layer("fold"):
            fold_weights(nc, w, folded)
        with layer("decay"):
            mha_layer(nc, g, decay, True, 1.0 / D ** 0.5, True, False)
        with layer("experts1"):
            routed_layer(nc, g, experts_a, False)
        with layer("rope"):
            mha_layer(nc, g, rope, False, HD ** -0.5, True, False)
        with layer("experts2"):
            routed_layer(nc, g, experts_a, False)
        with layer("causal"):
            single_head_layer(nc, g, causal)
        with layer("experts3"):
            routed_layer(nc, g, experts_b, True)
        with layer("latent"):
            mha_layer(nc, g, latent, False, HD ** -0.5, False, True)
        with layer("experts4"):
            routed_layer(nc, g, experts_b, True, last_layer=True)


def chunked(a):
    return np.ascontiguousarray(a.reshape(-1, P, a.shape[-1]).transpose(1, 0, 2))


def every_partition(a):
    return np.ascontiguousarray(np.broadcast_to(a.reshape(-1), (P, a.size)))


def tables():
    i = np.arange(S)
    angles = np.outer(i, 1.0 / 10000.0 ** (np.arange(0, HD, 2) / HD))
    angles = np.concatenate([angles, angles], -1).T
    sign = np.where(np.arange(HD) < HD // 2, -1.0, 1.0)[:, None]
    dims = [d for d in HEAD_DIMS for _ in range(8)]
    rope = np.stack([np.cos(angles)[dims], (np.sin(angles) * sign)[dims]], 1)
    decay = np.broadcast_to(np.stack([np.exp(.01 * (i - S / 2)), np.exp(-.01 * (i - S / 2))]), (P, 2, S))
    q, k = i[:, None], i[None]
    corr = np.where(k >= q, 1.0, np.exp(-.02 * (q - k))).reshape(4, P, S).transpose(1, 0, 2)
    mask = np.where(k[:, :] - (S - P) > np.arange(P)[:, None], -1e30, 0.0)
    t = {"rope_tab": rope, "decay_tab": decay, "corr": corr, "mask": mask, "ident": np.eye(P),
         "before": np.triu(np.ones((P, P)), 1), "con": shape_constants()}
    return {n: np.ascontiguousarray(a, dtype=np.float32) for n, a in t.items()}


def layouts(L0_attn_a_x, L0_attn_a_W_q, L0_attn_a_W_k, L0_attn_a_W_v, L0_attn_a_W_o, L0_attn_a_W_down_kv,
            L0_attn_a_W_up_k, L0_attn_a_W_up_v, L0_attn_b_Wqkv, L0_attn_b_Wo, L0_ffn_Wg, L0_ffn_bg, L0_ffn_We, L0_ffn_be,
            L1_attn_a_qkv_w, L1_attn_a_out_w, L1_attn_a_out_b, L1_attn_b_w_dk, L1_attn_b_b_dk, L1_attn_b_w_dv,
            L1_attn_b_b_dv, L1_attn_b_w_uk, L1_attn_b_b_uk, L1_attn_b_w_uv, L1_attn_b_b_uv, L1_attn_b_w_o,
            L1_attn_b_b_o, L1_ffn_Wr, L1_ffn_W1, L1_ffn_W2):
    tiles = L0_attn_a_x.reshape(NB, 4, P, D).transpose(0, 2, 1, 3)
    q, k, v = (L0_attn_b_Wqkv[:, i * D:(i + 1) * D] for i in range(3))
    cq, ck, cv = (L1_attn_a_qkv_w[i * D:(i + 1) * D] for i in range(3))
    return {
        "x": tiles,
        "a_wq": chunked(L0_attn_a_W_q[:, COLS]), "a_wo": chunked(L0_attn_a_W_o),
        "wkT": chunked(L0_attn_a_W_k.T), "wvT": chunked(L0_attn_a_W_v.T), "wdown": chunked(L0_attn_a_W_down_kv),
        "upk": L0_attn_a_W_up_k[:, COLS], "upv": L0_attn_a_W_up_v,
        "b_wq": chunked(q[:, COLS]), "b_wk": chunked(k[:, COLS]), "b_wv": chunked(v), "b_wo": chunked(L0_attn_b_Wo),
        "gate_a": chunked(L0_ffn_Wg), "gate_bias": every_partition(L0_ffn_bg),
        "we": L0_ffn_We.reshape(E, 2, P, D).transpose(2, 1, 0, 3).reshape(P, 2, E * D), "be": every_partition(L0_ffn_be),
        "cq": chunked(cq), "ck": chunked(ck), "cv": chunked(cv), "coT": chunked(L1_attn_a_out_w.T),
        "c_bias": every_partition(L1_attn_a_out_b),
        "dkT": L1_attn_b_w_dk[COLS].T, "dvT": L1_attn_b_w_dv[COLS].T, "uk": L1_attn_b_w_uk[:, COLS], "uv": L1_attn_b_w_uv,
        "bdk": L1_attn_b_b_dk.reshape(P, 1), "bdv": L1_attn_b_b_dv.reshape(P, 1),
        "buk": L1_attn_b_b_uk[COLS].reshape(2, P).T, "buv": L1_attn_b_b_uv.reshape(2, P).T,
        "dwo": chunked(L1_attn_b_w_o), "bo": every_partition(L1_attn_b_b_o),
        "gate_b": chunked(L1_ffn_Wr),
        "w1": L1_ffn_W1.reshape(E, 2, P, F).transpose(0, 2, 1, 3),
        "w2": L1_ffn_W2.reshape(E, F // P, P, D).transpose(0, 2, 1, 3),
    }


def kernel(**inputs):
    import concourse.bacc as _bacc
    from concourse.bass_utils import run_bass_kernel_spmd as _run

    nc = _bacc.Bacc("TRN2", target_bir_lowering=False, num_devices=1)
    data = layouts(**{n: np.asarray(a) for n, a in inputs.items()})
    data.update(tables())
    arrays, w = {}, {}
    for name, a in data.items():
        a = np.ascontiguousarray(a)
        arrays[f"in_{name}_dram"] = a
        w[name] = nc.dram_tensor(f"in_{name}_dram", a.shape, mybir.dt.from_np(a.dtype), kind="ExternalInput").ap()
    out = nc.dram_tensor("out_0_dram", (NB, S, D), F32, kind="ExternalOutput").ap()
    hybrid_stack(nc, w, [out[q].rearrange("(t p) d -> p t d", p=P) for q in range(NB)])
    return _run(nc, [arrays], core_ids=[0]).results[0]["out_0_dram"]
```

```python
from contextlib import ExitStack

import numpy as np

import concourse.bass as bass
from concourse import mybir

F32, BF16 = mybir.dt.float32, mybir.dt.bfloat16
I32, U32 = mybir.dt.int32, mybir.dt.uint32
ALU, ACT, AX = mybir.AluOpType, mybir.ActivationFunctionType, mybir.AxisListType

P = 128
NB, S, D = 8, 512, 256
H, HD = 16, 16
E = 8
F = 1024
T = NB * S
NT = T // P
EPS = 1e-5


def apart(eng, value, held):
    if isinstance(value, int):
        return value
    value = eng.to_reg(value)
    eng.wait_ge(held, 16)
    return value


SLOTS = T + E * P
ZERO_ROW = SLOTS
CAP = T // E
BIG = 65536.0
EXPERT_TILES = SLOTS // P


def routing(nc, g, ins, capacity):
    X, MV, RSTD, XN = g["X"], g["MV"], g["RSTD"], g["XN"]
    ident, con = g["ident"], g["con"]
    slot, back, weight, te = g["slot"], g["back"], g["weight"], g["te"]
    G = E if capacity else D
    LP = 1 if capacity else 2
    NQ = NT // 4

    with ExitStack() as ctx:
        def sb(name, shape, dt):
            return ctx.enter_context(nc.sbuf_tensor(f"{g['layer']}r_{name}", shape, dt))

        def sem(name):
            return nc.alloc_semaphore(f"{g['layer']}r_{name}")

        psT = ctx.enter_context(nc.psum_tensor(f"{g['layer']}r_turned", [P, 2, S], F32))
        psL = ctx.enter_context(nc.psum_tensor(f"{g['layer']}r_logits", [P, 2, LP, 2, D], F32))
        psR = ctx.enter_context(nc.psum_tensor(f"{g['layer']}r_ranks", [P, NT, E], F32))
        psC = ctx.enter_context(nc.psum_tensor(f"{g['layer']}r_totals", [P, NT, E], F32))
        wg = sb("wg", [P, 2, G], F32)
        xnT = sb("xnT", [P, 2, 2, S], F32)
        lg = sb("lg", [P, NT, E] if capacity else [P, 2, 2, 2, D], F32)
        if not capacity:
            bg = sb("bg", [P, D], F32)
            top = sb("top", [P, 4, 8], F32)
            ntop = sb("ntop", [P, NT], F32)
            nmr = sb("nmr", [P, NT], F32)
            idx = sb("idx", [P, 4, 8], U32)
            first = sb("first", [P, NT], U32)
            low3 = sb("low3", [P, NT], U32)
            ex = sb("ex", [P, 2, D], F32)
            cnt_i = sb("cnt_i", [P, E], I32)
            blk, blk_inc = sb("blk", [P, E], F32), sb("blk_inc", [P, E], F32)
            past = sb("past", [P, EXPERT_TILES, E], F32)
            tef = sb("tef", [P, EXPERT_TILES], F32)
        sums = sb("sums", [P, NT], F32)
        best = sb("best", [P, NT], F32)
        oh, ohb = sb("oh", [P, NT, E], F32), sb("ohb", [P, NT, E], BF16)
        tot, inc = sb("tot", [P, E, NT], F32), sb("inc", [P, E, NT], F32)
        rk = sb("rk", [P, NT, E], F32)
        rank, keep = sb("rank", [P, NT], F32), sb("keep", [P, NT], F32)

        loaded = sem("loaded")
        root, rstd_done = sem("root"), sem("rstd_done")
        xn_ready = sem("xn_ready")
        t_ready, t_taken = sem("turned_ready"), sem("turned_taken")
        l_ready, l_taken = sem("logits_ready"), sem("logits_taken")
        top_done, first_done, exp_done = sem("top_done"), sem("first_done"), sem("exp_done")
        steps = sem("steps")
        oh_ready, counted = sem("oh_ready"), sem("counted")

        block = ctx.enter_context(nc.Block())

        @block.sync
        def _(sp):
            sp.dma_start(wg[:, :, :], ins["wg"]).then_inc(loaded, 16)
            if not capacity:
                sp.dma_start(bg[:, :], ins["bg"]).then_inc(loaded, 16)

        @block.tensor
        def _(pe):
            pe.wait_ge(loaded, 16 if capacity else 32)

            def turn(q, par):
                pe.wait_ge(xn_ready, q * 4 + 4)
                for c in range(2):
                    if q:
                        pe.wait_ge(t_taken, q * 2 + (c - 1))
                    for t in range(4):
                        last = pe.transpose(psT[:, c, t * P:(t + 1) * P], XN[:, q * 4 + t, c * P:(c + 1) * P], ident[:, :])
                    last.then_inc(t_ready, 1)

            def score(q, par):
                pe.wait_ge(t_taken, q * 2 + 2)
                for pair in range(2):
                    n = q * 2 + pair
                    if not capacity:
                        if n >= 4:
                            pe.wait_ge(l_taken, n - 3)
                    elif pair == 0 and q >= 2:
                        pe.wait_ge(l_taken, q - 1)
                    for t in range(2):
                        tok = (2 * pair + t) * P
                        if capacity:
                            out = psL[:, par, 0, 0, (2 * pair + t) * E:(2 * pair + t + 1) * E]
                        else:
                            out = psL[:, par, pair, t, :]
                        for c in range(2):
                            last = pe.matmul(out, xnT[:, par, c, tok:tok + P], wg[:, c, :], start=(c == 0), stop=(c == 1))
                    if not capacity or pair == 1:
                        last.then_inc(l_ready, 1)

            turn(0, 0)
            for q in range(1, NQ):
                turn(q, q % 2)
                score(q - 1, (q - 1) % 2)
            score(NQ - 1, (NQ - 1) % 2)
            pe.wait_ge(oh_ready, 1)
            flat = ohb[:, :, :].rearrange("p t e -> p (t e)")
            pe.matmul(psR[:, :, :].rearrange("p t e -> p (t e)"), g["before"][:, :], flat, start=True, stop=True).then_inc(
                counted, 1)
            pe.matmul(psC[:, :, :].rearrange("p t e -> p (t e)"), g["ones"][:, :], flat, start=True, stop=True).then_inc(
                counted, 1)

        @block.scalar
        def _(act):
            act.activation(RSTD[:, 1, :], MV[:, :, 1], ACT.Sqrt, bias=g["eps"][:, :]).then_inc(root, 1)

            def take(q, par):
                for c in range(2):
                    act.wait_ge(t_ready, q * 2 + (c + 1))
                    if c == 0 and not (isinstance(q, int) and q < 2):
                        act.wait_ge(l_ready, q * LP - LP)
                    act.copy(xnT[:, par, c, :], psT[:, c, :]).then_inc(t_taken, 1)

            def normalise(q):
                if capacity:
                    return
                for t in range(4):
                    i = q * 4 + t
                    act.activation(XN[:, i, :], X[:, i, :], ACT.Identity, bias=nmr[:, bass.ds(i, 1)],
                                   scale=RSTD[:, 0, bass.ds(i, 1)]).then_inc(xn_ready, 1)

            def exps(q, par):
                if capacity:
                    return
                for t in range(4):
                    i = q * 4 + t
                    act.wait_ge(top_done, i * 3 + 4 - t % 2)
                    if not (isinstance(i, int) and i < 2):
                        act.wait_ge(exp_done, i - 1)
                    act.activation(ex[:, t % 2, :], lg[:, par, t // 2, t % 2, :], ACT.Exp, bias=ntop[:, bass.ds(i, 1)],
                                   accum_out=sums[:, bass.ds(i, 1)]).then_inc(exp_done, 1)

            def pair(j):
                normalise(j * 2 + 2)
                take(j * 2 + 1, 1)
                exps(j * 2, 0)
                normalise(j * 2 + 3)
                take(j * 2 + 2, 0)
                exps(j * 2 + 1, 1)

            if not capacity:
                act.wait_ge(rstd_done, 2)
            normalise(0)
            take(0, 0)
            normalise(1)
            pair(0)
            with act.Fori(1, NQ // 2 - 1) as j:
                pair(j)
            take(NQ - 1, 1)
            exps(NQ - 2, 0)
            exps(NQ - 1, 1)
            if capacity:
                act.wait_ge(steps, 2)
                flat = lg[:, :, :].rearrange("p t e -> p (t e)")
                act.activation(flat, flat, ACT.Exp).then_inc(exp_done, 1)

        @block.vector
        def _(dve):
            dve.wait_ge(root, 1)
            dve.reciprocal(RSTD[:, 0, :], RSTD[:, 1, :]).then_inc(rstd_done, 1)
            dve.wait_ge(rstd_done, 1)
            if not capacity:
                dve.scalar_tensor_tensor(nmr[:, :], MV[:, :, 0], -1.0, RSTD[:, 0, :], ALU.mult, ALU.mult).then_inc(
                    rstd_done, 1)
            dve.wait_ge(loaded, 16 if capacity else 32)

            def normalise(q):
                if not capacity:
                    return
                for t in range(4):
                    i = q * 4 + t
                    dve.tensor_scalar(XN[:, i, :], X[:, i, :], MV[:, i, 0:1], RSTD[:, 0, bass.ds(i, 1)],
                                      ALU.subtract, ALU.mult).then_inc(xn_ready, 1)

            def top_logits(q, par):
                if capacity:
                    dve.wait_ge(l_ready, q + 1)
                    dve.tensor_copy(lg[:, bass.ds(q * 4, 4), :], psL[:, par, 0, 0, 0:4 * E].rearrange(
                        "p (t e) -> p t e", t=4)).then_inc(l_taken, 1)
                    return
                for pair in range(2):
                    n = q * 2 + pair
                    dve.wait_ge(l_ready, n + 1)
                    if not (isinstance(n, int) and n < 4):
                        dve.wait_ge(exp_done, n * 2 - 6)
                    dve.tensor_tensor(lg[:, par, pair, :, :], psL[:, par, pair, :, :],
                                      bg[:, :].unsqueeze(1).to_broadcast([P, 2, D]), ALU.add).then_inc(l_taken, 1)
                    dve.wait_ge(l_taken, apart(dve, n + 1, loaded))
                    for t in range(2):
                        dve.max(top[:, 2 * pair + t, :], lg[:, par, pair, t, :]).then_inc(top_done, 1)
                    dve.wait_ge(top_done, apart(dve, (q * 4 + 2 * pair) * 3 + 2, loaded))
                    for t in range(2):
                        i = q * 4 + (2 * pair + t)
                        k = 2 * pair + t
                        dve.max_index(idx[:, k, :], top[:, k, :], lg[:, par, pair, t, :]).then_inc(top_done, 1)
                        dve.tensor_scalar(ntop[:, bass.ds(i, 1)], top[:, k, 0:1], -1.0, None, ALU.mult).then_inc(top_done, 1)
                dve.wait_ge(top_done, q * 12 + 12)
                dve.tensor_copy(first[:, bass.ds(q * 4, 4)], idx[:, :, 0]).then_inc(first_done, 1)

            def pair(j):
                normalise(j * 2 + 2)
                top_logits(j * 2, 0)
                normalise(j * 2 + 3)
                top_logits(j * 2 + 1, 1)

            normalise(0)
            normalise(1)
            pair(0)
            with dve.Fori(1, NQ // 2 - 1) as j:
                pair(j)
            top_logits(NQ - 2, 0)
            top_logits(NQ - 1, 1)

            done = [0]

            def link(ins_):
                done[0] += 1
                ins_.then_inc(steps, 1)
                dve.wait_ge(steps, done[0])

            def over_experts(ap):
                return ap.unsqueeze(2).to_broadcast([P, NT, E])

            def over_tiles(ap):
                return ap.unsqueeze(1).to_broadcast([P, NT, E])

            if capacity:
                dve.wait_ge(l_taken, NQ)
                link(dve.tensor_reduce(best[:, :], lg[:, :, :], AX.X, ALU.max))
                link(dve.tensor_tensor(lg[:, :, :], lg[:, :, :], over_experts(best[:, :]), ALU.subtract))
                dve.wait_ge(exp_done, 1)
                link(dve.tensor_reduce(sums[:, :], lg[:, :, :], AX.X, ALU.add))
                link(dve.tensor_scalar(rk[:, :, :], lg[:, :, :], 1.0, None, ALU.is_ge))
                link(dve.tensor_tensor(rk[:, :, :], rk[:, :, :], over_tiles(con["down8"]), ALU.mult))
                link(dve.tensor_reduce(best[:, :], rk[:, :, :], AX.X, ALU.max))
                link(dve.tensor_tensor(oh[:, :, :], over_tiles(con["down8"]), over_experts(best[:, :]), ALU.is_equal))
            else:
                dve.wait_ge(exp_done, NT)
                dve.wait_ge(first_done, NQ)
                link(dve.tensor_scalar(low3[:, :], first[:, :], E - 1, None, ALU.bitwise_and))
                link(dve.tensor_copy(best[:, :], low3[:, :]))
                link(dve.tensor_tensor(oh[:, :, :], over_tiles(con["up8"]), over_experts(best[:, :]), ALU.is_equal))
            dve.tensor_copy(ohb[:, :, :], oh[:, :, :]).then_inc(oh_ready, 1)
            link(dve.reciprocal(weight[:, :], sums[:, :]))
            dve.wait_ge(counted, 2)
            link(dve.tensor_copy(tot[:, :, :], psC[:, :, :].rearrange("p t e -> p e t")))
            link(dve.tensor_tensor_scan(inc[:, :, :].rearrange("p e t -> p (e t)"), con["resets"],
                                        tot[:, :, :].rearrange("p e t -> p (e t)"), 0.0, ALU.mult, ALU.add))
            link(dve.tensor_tensor(tot[:, :, :], inc[:, :, :], tot[:, :, :], ALU.subtract))
            link(dve.tensor_tensor(rk[:, :, :], psR[:, :, :], tot[:, :, :].rearrange("p e t -> p t e"), ALU.add))
            if not capacity:
                link(dve.tensor_scalar(cnt_i[:, :], inc[:, :, NT - 1], float(P - 1), None, ALU.add))
                link(dve.tensor_scalar(cnt_i[:, :], cnt_i[:, :], P.bit_length() - 1, None, ALU.arith_shift_right))
                link(dve.tensor_copy(blk[:, :], cnt_i[:, :]))
                link(dve.tensor_tensor_scan(blk_inc[:, :], con["ones8"], blk[:, :], 0.0, ALU.mult, ALU.add))
                link(dve.tensor_tensor(blk[:, :], blk_inc[:, :], blk[:, :], ALU.subtract))
                link(dve.tensor_scalar(blk[:, :], blk[:, :], float(P), None, ALU.mult))
                link(dve.tensor_tensor(rk[:, :, :], rk[:, :, :], over_tiles(blk[:, :]), ALU.add))
                link(dve.tensor_tensor(past[:, :, :], con["tiles"].unsqueeze(2).to_broadcast([P, EXPERT_TILES, E]),
                                       blk_inc[:, :].unsqueeze(1).to_broadcast([P, EXPERT_TILES, E]), ALU.is_ge))
                link(dve.tensor_reduce(tef[:, :], past[:, :, :], AX.X, ALU.add))
                link(dve.tensor_scalar(tef[:, :], tef[:, :], float(E - 1), float(D), ALU.min, ALU.mult))
                link(dve.tensor_copy(te[:, :], tef[:, :]))
            link(dve.tensor_tensor(rk[:, :, :], rk[:, :, :], oh[:, :, :], ALU.mult))
            link(dve.tensor_reduce(rank[:, :], rk[:, :, :], AX.X, ALU.add))
            if capacity:
                link(dve.tensor_scalar(keep[:, :], rank[:, :], float(CAP), BIG, ALU.is_ge, ALU.mult))
                link(dve.tensor_tensor(rank[:, :], rank[:, :], keep[:, :], ALU.add))
                link(dve.tensor_scalar(best[:, :], best[:, :], -float(CAP), float(CAP * E), ALU.mult, ALU.add))
                link(dve.tensor_tensor(rank[:, :], rank[:, :], best[:, :], ALU.add))
            link(dve.tensor_copy(slot[:, :], rank[:, :]))
            link(dve.tensor_scalar(keep[:, :], rank[:, :], float(ZERO_ROW), None, ALU.min))
            link(dve.tensor_copy(back[:, :], keep[:, :]))


def dispatch(pool, g, scattered):
    for i in range(NT):
        pool.indirect_dma_start(out=g["xe"][0:SLOTS, :], out_offset=bass.IndirectOffsetOnAxis(ap=g["slot"][:, i:i + 1], axis=0),
                                in_=g["XN"][:, i, :], in_offset=None, bounds_check=SLOTS - 1,
                                oob_is_err=False).then_inc(scattered, 16)


def collect(pool, g, gathered, added):
    NG = len(gathered)
    for i in range(NT):
        if i >= NG:
            pool.wait_ge(added, i - NG + 1)
        pool.indirect_dma_start(out=g["XN"][:, i, :], out_offset=None, in_=g["ye"][0:SLOTS + 1, :],
                                in_offset=bass.IndirectOffsetOnAxis(ap=g["back"][:, i:i + 1], axis=0)).then_inc(
            gathered[i % NG], 16)


def statistics(dve, g, st, bns_done, i):
    dve.bn_stats(st[:, i % 4, :], g["X"][:, i, :]).then_inc(bns_done, 1)
    dve.wait_ge(bns_done, i + 1)
    dve.bn_aggr(g["MV"][:, i, :], st[:, i % 4, :])


def experts_small(nc, g, ins):
    X, XN, te, weight = g["X"], g["XN"], g["te"], g["weight"]
    RING = 4
    with ExitStack() as ctx:
        def sb(name, shape, dt):
            return ctx.enter_context(nc.sbuf_tensor(f"{g['layer']}x_{name}", shape, dt))

        def sem(name):
            return nc.alloc_semaphore(f"{g['layer']}x_{name}")

        psT = ctx.enter_context(nc.psum_tensor(f"{g['layer']}x_turned", [P, 2, S], F32))
        psY = ctx.enter_context(nc.psum_tensor(f"{g['layer']}x_results", [P, 2, S], F32))
        we, be = sb("we", [P, 2, E * D], F32), sb("be", [P, E * D], F32)
        xin, xT = sb("xin", [P, RING, D], F32), sb("xT", [P, 2, 2, P], F32)
        y, st = sb("y", [P, RING, D], F32), sb("st", [P, 4, 6], F32)
        loaded, scattered = sem("loaded"), sem("scattered")
        x_loaded = [sem(f"x_loaded{i}") for i in range(RING)]
        y_stored = [sem(f"y_stored{i}") for i in range(RING)]
        t_ready, t_taken, y_ready, y_taken = sem("t_ready"), sem("t_taken"), sem("y_ready"), sem("y_taken")
        gathered = [sem(f"gathered{i}") for i in range(8)]
        relu_done, added, bns_done = sem("relu_done"), sem("added"), sem("bns_done")
        block = ctx.enter_context(nc.Block())
        NB4 = EXPERT_TILES // RING

        @block.gpsimd
        def _(pool):
            dispatch(pool, g, scattered)
            for r in range(RING):
                pool.wait_ge(y_stored[r], 16 * NB4)
            collect(pool, g, gathered, added)

        @block.sync
        def _(sp):
            sp.dma_start(we[:, :, :], ins["we"]).then_inc(loaded, 16)
            sp.dma_start(be[:, :], ins["be"]).then_inc(loaded, 16)
            sp.wait_ge(scattered, 16 * NT)

            def load(b, r):
                if not (isinstance(b, int) and b == 0):
                    sp.wait_ge(t_ready, b * RING + (r - RING + 1))
                sp.dma_start(xin[:, r, :], g["xe"][bass.ds((b * RING + r) * P, P), :]).then_inc(x_loaded[r], 16)

            def store(b, r):
                sp.wait_ge(y_taken, b * RING + (r + 1))
                sp.dma_start(g["ye"][bass.ds((b * RING + r) * P, P), :], y[:, r, :]).then_inc(y_stored[r], 16)

            for r in range(RING):
                load(0, r)
            with sp.Fori(0, NB4 - 1) as b:
                for r in range(RING):
                    store(b, r)
                    load(b + 1, r)
            for r in range(RING):
                store(NB4 - 1, r)
            for r in range(RING):
                sp.wait_ge(y_stored[r], 16 * NB4)

        @block.tensor
        def _(pe):
            pe.wait_ge(loaded, 32)

            def turn(b, r):
                pe.wait_ge(x_loaded[r], b * 16 + 16)
                n = b * RING + r
                if not (isinstance(n, int) and n < 2):
                    pe.wait_ge(t_taken, n - 1)
                for c in range(2):
                    last = pe.transpose(psT[:, r % 2, c * P:(c + 1) * P], xin[:, r, c * P:(c + 1) * P], g["ident"][:, :])
                last.then_inc(t_ready, 1)

            def expert(b, r, at):
                n = b * RING + r
                pe.wait_ge(t_taken, n + 1)
                if not (isinstance(n, int) and n < 2):
                    pe.wait_ge(y_taken, n - 1)
                for c in range(2):
                    last = pe.matmul(psY[:, r % 2, 0:D], xT[:, r % 2, c, :], we[:, c, bass.ds(at, D)], start=(c == 0), stop=(c == 1))
                last.then_inc(y_ready, 1)

            def ring(b, more):
                def tile_expert(r):
                    return pe.value_load(te[0:1, bass.ds(b * RING + r, 1)], min_val=0, max_val=(E - 1) * D)

                at = tile_expert(0)
                for r in range(RING):
                    if r < RING - 1:
                        turn(b, r + 1)
                    elif more:
                        turn(b + 1, 0)
                    expert(b, r, at)
                    if r < RING - 1:
                        at = tile_expert(r + 1)

            turn(0, 0)
            ring(0, True)
            with pe.Fori(1, NB4 - 1) as b:
                ring(b, True)
            ring(NB4 - 1, False)

        @block.scalar
        def _(act):
            def take(b, r):
                n = b * RING + r
                act.wait_ge(t_ready, n + 1)
                if not (isinstance(n, int) and n < 2):
                    act.wait_ge(y_ready, n - 1)
                act.copy(xT[:, r % 2, :, :].rearrange("p c t -> p (c t)"), psT[:, r % 2, 0:D]).then_inc(t_taken, 1)

            for r in range(RING):
                take(0, r)
            with act.Fori(1, NB4) as b:
                for r in range(RING):
                    take(b, r)
            for i in range(NT):
                act.wait_ge(gathered[i % 8], 16 * (i // 8 + 1))
                act.activation(XN[:, i, :], XN[:, i, :], ACT.Relu, scale=weight[:, i:i + 1]).then_inc(relu_done, 1)

        @block.vector
        def _(dve):
            dve.wait_ge(loaded, 32)

            def result(b, r, at):
                n = b * RING + r
                dve.wait_ge(y_ready, n + 1)
                if not (isinstance(b, int) and b == 0):
                    dve.wait_ge(y_stored[r], b * 16)
                dve.tensor_tensor(y[:, r, :], psY[:, r % 2, 0:D], be[:, bass.ds(at, D)], ALU.add).then_inc(y_taken, 1)

            def ring(b):
                for r in range(RING):
                    result(b, r, dve.value_load(te[0:1, bass.ds(b * RING + r, 1)], min_val=0, max_val=(E - 1) * D))

            ring(0)
            with dve.Fori(1, NB4) as b:
                ring(b)
            for i in range(NT):
                dve.wait_ge(relu_done, i + 1)
                dve.tensor_tensor(X[:, i, :], X[:, i, :], XN[:, i, :], ALU.add).then_inc(added, 1)
                dve.wait_ge(added, i + 1)
                statistics(dve, g, st, bns_done, i)


def experts_large(nc, g, ins, last_layer):
    X, XN, weight = g["X"], g["XN"], g["weight"]
    FC = F // P
    QT = CAP // P
    with ExitStack() as ctx:
        def sb(name, shape, dt):
            return ctx.enter_context(nc.sbuf_tensor(f"{g['layer']}x_{name}", shape, dt))

        def sem(name):
            return nc.alloc_semaphore(f"{g['layer']}x_{name}")

        psT = ctx.enter_context(nc.psum_tensor(f"{g['layer']}x_turned", [P, 2, S], F32))
        psH = ctx.enter_context(nc.psum_tensor(f"{g['layer']}x_inner", [P, 3, S], F32))
        psY = ctx.enter_context(nc.psum_tensor(f"{g['layer']}x_results", [P, 2, S], F32))
        w1, w2 = sb("w1", [P, 2, 2, F], F32), sb("w2", [P, 2, FC, D], F32)
        xin, xT = sb("xin", [P, 2, QT, D], F32), sb("xT", [P, 2, 2, S], F32)
        hT = sb("hT", [P, FC, S], F32)
        y, st = sb("y", [P, 2, QT, D], F32), sb("st", [P, 4, 6], F32)
        scattered = sem("scattered")
        w_loaded = [sem(f"w_loaded{i}") for i in range(2)]
        x_loaded = [sem(f"x_loaded{i}") for i in range(2)]
        y_stored = [sem(f"y_stored{i}") for i in range(2)]
        t_ready, t_taken = sem("t_ready"), sem("t_taken")
        h_ready, y_ready = sem("h_ready"), sem("y_ready")
        h_even, h_odd = sem("h_even_taken"), sem("h_odd_taken")
        y_taken = sem("y_taken")
        gathered = [sem(f"gathered{i}") for i in range(8)]
        added, bns_done, out_stored = sem("added"), sem("bns_done"), sem("out_stored")
        block = ctx.enter_context(nc.Block())

        @block.gpsimd
        def _(pool):
            dispatch(pool, g, scattered)
            for p in range(2):
                pool.wait_ge(y_stored[p], 16 * (E // 2))
            collect(pool, g, gathered, added)

        @block.sync
        def _(sp):
            def weights(e, p):
                sp.dma_start(w1[:, p, :, :], ins["w1"][e]).then_inc(w_loaded[p], 16)
                sp.dma_start(w2[:, p, :, :], ins["w2"][e]).then_inc(w_loaded[p], 16)

            def tokens(e, p):
                sp.dma_start(xin[:, p, :, :], g["xe"][bass.ds(e * CAP, CAP), :].rearrange("(q p) d -> p q d", p=P)).then_inc(
                    x_loaded[p], 16)

            def store(e, p):
                sp.wait_ge(y_taken, e * QT + QT)
                sp.dma_start(g["ye"][bass.ds(e * CAP, CAP), :].rearrange("(q p) d -> p q d", p=P), y[:, p, :, :]).then_inc(
                    y_stored[p], 16)

            for p in range(2):
                weights(p, p)
            sp.wait_ge(scattered, 16 * NT)
            for p in range(2):
                tokens(p, p)
            with sp.Fori(0, E // 2 - 1) as j:
                for p in range(2):
                    e = j * 2 + p
                    store(e, p)
                    weights(e + 2, p)
                    tokens(e + 2, p)
            for p in range(2):
                store(E - 2 + p, p)
            for p in range(2):
                sp.wait_ge(y_stored[p], 16 * (E // 2))
            if last_layer:
                for q in range(NB):
                    sp.wait_ge(added, 4 * q + 4)
                    sp.dma_start(ins["out"][q], X[:, 4 * q:4 * q + 4, :]).then_inc(out_stored, 16)
                sp.wait_ge(out_stored, 16 * NB)

        @block.tensor
        def _(pe):
            def turn(j, p):
                pe.wait_ge(x_loaded[p], j * 16 + 16)
                n = j * 2 + p
                for c in range(2):
                    if not (isinstance(n, int) and n == 0):
                        pe.wait_ge(t_taken, n * 2 + (c - 1))
                    for t in range(QT):
                        last = pe.transpose(psT[:, c, t * P:(t + 1) * P], xin[:, p, t, c * P:(c + 1) * P], g["ident"][:, :])
                    last.then_inc(t_ready, 1)

            def inner(j, p):
                n = j * 2 + p
                pe.wait_ge(w_loaded[p], j * 32 + 32)
                pe.wait_ge(t_taken, n * 2 + 2)
                for f in range(FC):
                    if not (isinstance(n, int) and n == 0 and f < 2):
                        pe.wait_ge(h_even if f % 2 == 0 else h_odd, n * (FC // 2) + f // 2)
                    for c in range(2):
                        last = pe.matmul(psH[:, f % 2, :], w1[:, p, c, f * P:(f + 1) * P], xT[:, p, c, :],
                                         start=(c == 0), stop=(c == 1))
                    last.then_inc(h_ready, 1)

            def outer(j, p):
                n = j * 2 + p
                pe.wait_ge(h_even, n * (FC // 2) + FC // 2)
                pe.wait_ge(h_odd, n * (FC // 2) + FC // 2)
                for t in range(QT):
                    if not (isinstance(n, int) and n == 0 and t < 2):
                        pe.wait_ge(y_taken, n * QT + (t - 1))
                    for f in range(FC):
                        last = pe.matmul(psY[:, t % 2, 0:D], hT[:, f, t * P:(t + 1) * P], w2[:, p, f, :],
                                         start=(f == 0), stop=(f == FC - 1))
                    last.then_inc(y_ready, 1)

            turn(0, 0)

            def pair(j, more):
                inner(j, 0)
                turn(j, 1)
                outer(j, 0)
                inner(j, 1)
                if more:
                    turn(j + 1, 0)
                outer(j, 1)

            pair(0, True)
            with pe.Fori(1, E // 2 - 1) as j:
                pair(j, True)
            pair(E // 2 - 1, False)

        @block.scalar
        def _(act):
            def take(j, p):
                n = j * 2 + p
                for c in range(2):
                    act.wait_ge(t_ready, n * 2 + (c + 1))
                    act.copy(xT[:, p, c, :], psT[:, c, :]).then_inc(t_taken, 1)

            def relus(j, p):
                n = j * 2 + p
                for f in range(0, FC, 2):
                    act.wait_ge(h_ready, n * FC + (f + 1))
                    if not (isinstance(n, int) and n == 0):
                        act.wait_ge(y_ready, n * QT)
                    act.activation(hT[:, f, :], psH[:, f % 2, :], ACT.Relu).then_inc(h_even, 1)

            take(0, 0)

            def pair(j, more):
                relus(j, 0)
                take(j, 1)
                relus(j, 1)
                if more:
                    take(j + 1, 0)

            pair(0, True)
            with act.Fori(1, E // 2 - 1) as j:
                pair(j, True)
            pair(E // 2 - 1, False)

        @block.vector
        def _(dve):
            def relus(j, p):
                n = j * 2 + p
                for f in range(1, FC, 2):
                    dve.wait_ge(h_ready, n * FC + (f + 1))
                    if not (isinstance(n, int) and n == 0):
                        dve.wait_ge(y_ready, n * QT)
                    dve.tensor_scalar(hT[:, f, :], psH[:, f % 2, :], 0.0, None, ALU.max).then_inc(h_odd, 1)

            def results(j, p):
                n = j * 2 + p
                for t in range(QT):
                    dve.wait_ge(y_ready, n * QT + (t + 1))
                    if t == 0 and not (isinstance(j, int) and j == 0):
                        dve.wait_ge(y_stored[p], j * 16)
                    dve.tensor_copy(y[:, p, t, :], psY[:, t % 2, 0:D]).then_inc(y_taken, 1)

            def pair(j):
                for p in range(2):
                    relus(j, p)
                    results(j, p)

            pair(0)
            with dve.Fori(1, E // 2) as j:
                pair(j)
            for i in range(NT):
                dve.wait_ge(gathered[i % 8], 16 * (i // 8 + 1))
                dve.scalar_tensor_tensor(X[:, i, :], XN[:, i, :], weight[:, i:i + 1], X[:, i, :], ALU.mult,
                                         ALU.add).then_inc(added, 1)
                if not last_layer:
                    dve.wait_ge(added, i + 1)
                    statistics(dve, g, st, bns_done, i)
CON = [("up8", E), ("down8", E), ("ones8", E), ("resets", E * NT), ("tiles", EXPERT_TILES)]
CON_WIDTH = sum(n for _, n in CON)


def global_tensors(nc, ctx):
    def sb(name, shape, dt):
        return ctx.enter_context(nc.sbuf_tensor(name, shape, dt))

    g = {"X": sb("X", [P, NT, D], F32), "MV": sb("MV", [P, NT, 2], F32), "RSTD": sb("RSTD", [P, 2, NT], F32),
         "ident": sb("ident_sb", [P, P], F32), "identb": sb("identb", [P, P], BF16), "eps": sb("eps", [P, 1], F32),
         "before": sb("before", [P, P], BF16), "ones": sb("ones", [P, P], BF16),
         "con_sb": sb("con_sb", [P, CON_WIDTH], F32),
         "xe": nc.dram_tensor("dispatched", [SLOTS, D], F32, kind="Internal").ap(),
         "ye": nc.dram_tensor("expert_results", [SLOTS + 1, D], F32, kind="Internal").ap()}
    at, g["con"] = 0, {}
    for name, n in CON:
        g["con"][name] = g["con_sb"][:, at:at + n]
        at += n
    return g


def load_tokens(nc, g, ins):
    with ExitStack() as ctx:
        fl = ctx.enter_context(nc.sbuf_tensor("before_f", [P, P], F32))
        zero = ctx.enter_context(nc.sbuf_tensor("zero", [P, D], F32))
        st = ctx.enter_context(nc.sbuf_tensor("st", [P, NT, 6], F32))
        x_loaded = [nc.alloc_semaphore(f"x_loaded{q}") for q in range(NB)]
        con_loaded = nc.alloc_semaphore("con_loaded")
        zeroed = nc.alloc_semaphore("zeroed")
        cleared = nc.alloc_semaphore("cleared")
        bns_done = nc.alloc_semaphore("bns_done")
        block = ctx.enter_context(nc.Block())

        @block.sync
        def _(sp):
            for q in range(NB):
                sp.dma_start(g["X"][:, 4 * q:4 * q + 4, :], ins["x"][q]).then_inc(x_loaded[q], 16)
            sp.dma_start(g["ident"][:, :], ins["ident"]).then_inc(con_loaded, 16)
            sp.dma_start(fl[:, :], ins["before"]).then_inc(con_loaded, 16)
            sp.dma_start(g["con_sb"][:, :], ins["con"]).then_inc(con_loaded, 16)
            sp.wait_ge(zeroed, 1)
            sp.dma_start(g["xe"].rearrange("(a p) d -> p a d", p=P),
                         zero[:, :].unsqueeze(1).to_broadcast([P, EXPERT_TILES, D])).then_inc(cleared, 16)
            sp.dma_start(g["ye"][ZERO_ROW:ZERO_ROW + 1, :], zero[0:1, :]).then_inc(cleared, 16)
            sp.wait_ge(cleared, 32)

        @block.gpsimd
        def _(pool):
            pool.memset(zero[:, :], 0.0).then_inc(zeroed, 1)
            pool.memset(g["eps"][:, :], EPS)
            pool.memset(g["ones"][:, :], 1.0)

        @block.vector
        def _(dve):
            for q in range(NB):
                dve.wait_ge(x_loaded[q], 16)
                for i in range(4 * q, 4 * q + 4):
                    dve.bn_stats(st[:, i, :], g["X"][:, i, :]).then_inc(bns_done, 1)
            dve.wait_ge(bns_done, NT)
            for i in range(NT):
                dve.bn_aggr(g["MV"][:, i, :], st[:, i, :])
            dve.wait_ge(con_loaded, 48)
            dve.tensor_copy(g["identb"][:, :], g["ident"][:, :])
            dve.tensor_copy(g["before"][:, :], fl[:, :])


def routed_layer(nc, g, ins, capacity, last_layer=False):
    with ExitStack() as ctx:
        def sb(name, shape, dt):
            return ctx.enter_context(nc.sbuf_tensor(f"{g['layer']}_{name}", shape, dt))

        g = dict(g, XN=sb("XN", [P, NT, D], F32), slot=sb("slot", [P, NT], I32), back=sb("back", [P, NT], I32),
                 weight=sb("weight", [P, NT], F32), te=None if capacity else sb("te", [P, EXPERT_TILES], I32))
        routing(nc, g, ins, capacity)
        if capacity:
            experts_large(nc, g, ins, last_layer)
        else:
            experts_small(nc, g, ins)


def shape_constants():
    rows = {"up8": np.arange(E), "down8": E - np.arange(E), "ones8": np.ones(E),
            "resets": (np.arange(E * NT) % NT != 0), "tiles": np.arange(EXPERT_TILES)}
    row = np.concatenate([rows[n] for n, _ in CON]).astype(np.float32)
    return np.ascontiguousarray(np.broadcast_to(row, (P, CON_WIDTH)))
DL = 64
FOLDED = {"a_wk": [P, 2, D], "a_wv": [P, 2, D], "c_wg": [P, 2, D], "c_wv": [P, 2, D], "d_wk": [P, 2, D],
          "d_wv": [P, 2, D], "d_kb": [P, 2], "d_xb": [P, D]}


def fold_weights(nc, w, folded):
    SHAPES = {"wkT": [P, 2, D], "wvT": [P, 2, D], "wdown": [P, 2, DL], "upk": [DL, D], "upv": [DL, D],
              "cq": [P, 2, D], "ck": [P, 2, D], "cv": [P, 2, D], "coT": [P, 2, D],
              "dkT": [P, D], "dvT": [P, D], "uk": [P, D], "uv": [P, D], 
              "bdk": [P, 1], "bdv": [P, 1], "buk": [P, 2], "buv": [P, 2], "dwo": [P, 2, D], "bo": [P, D]}
    BANKS = ["a_wk", "a_wv", "c_wg", "c_wv", "d_wk", "d_wv"]
    with ExitStack() as ctx:
        t = {n: ctx.enter_context(nc.sbuf_tensor(f"fold_{n}", s, F32)) for n, s in SHAPES.items() if n in w}
        lat = ctx.enter_context(nc.sbuf_tensor("fold_lat", [DL, D], F32))
        res = ctx.enter_context(nc.sbuf_tensor("fold_res", [P, len(BANKS), 2 * D], F32))
        kb = ctx.enter_context(nc.sbuf_tensor("fold_kb", [P, 2], F32))
        vb = ctx.enter_context(nc.sbuf_tensor("fold_vb", [P, 2], F32))
        vbw = ctx.enter_context(nc.sbuf_tensor("fold_vbw", [P, 2, P], F32))
        xb = ctx.enter_context(nc.sbuf_tensor("fold_xb", [P, D], F32))
        psF = ctx.enter_context(nc.psum_tensor("fold_products", [P, 8, S], F32))

        def sem(name):
            return nc.alloc_semaphore(f"fold_{name}")

        loaded = {n: sem(f"{n}_loaded") for n in ("a", "c", "d")}
        lat_ready, lat_taken = sem("lat_ready"), sem("lat_taken")
        bias_ready, bias_done, xb_ready = sem("bias_ready"), sem("bias_done"), sem("xb_ready")
        ready, taken, stored = sem("ready"), sem("taken"), sem("stored")
        groups = {"a": ["wkT", "wvT", "wdown", "upk", "upv"], "c": ["cq", "ck", "cv", "coT"],
                  "d": ["dkT", "dvT", "uk", "uv", "bdk", "bdv", "buk", "buv", "dwo", "bo"]}
        block = ctx.enter_context(nc.Block())

        @block.sync
        def _(sp):
            for grp, names in groups.items():
                for n in names:
                    sp.dma_start(t[n][tuple(slice(None) for _ in SHAPES[n])], w[n]).then_inc(loaded[grp], 16)
            for i, n in enumerate(BANKS):
                sp.wait_ge(taken, i + 1)
                sp.dma_start(folded[n].rearrange("p c d -> p (c d)"), res[:, i, :]).then_inc(stored, 16)
            sp.wait_ge(bias_done, 2)
            sp.dma_start(folded["d_kb"], kb[:, :]).then_inc(stored, 16)
            sp.wait_ge(bias_done, 4)
            sp.dma_start(folded["d_xb"], xb[:, :]).then_inc(stored, 16)
            sp.wait_ge(stored, 16 * (len(BANKS) + 2))

        @block.tensor
        def _(pe):
            pe.wait_ge(loaded["a"], 16 * len(groups["a"]))
            for i, n in enumerate(("wkT", "wvT")):
                for c in range(2):
                    last = pe.matmul(psF[0:DL, 0, 0:D], t["wdown"][:, c, :], t[n][:, c, :], start=(i + c == 0),
                                     stop=(i + c == 2))
            last.then_inc(lat_ready, 1)
            pe.wait_ge(lat_taken, 1)
            for bank, n in ((1, "upk"), (2, "upv")):
                for m in range(2):
                    last = pe.matmul(psF[:, bank, m * D:(m + 1) * D], lat[:, m * P:(m + 1) * P], t[n][:, :],
                                     start=True, stop=True)
                last.then_inc(ready, 1)
            pe.wait_ge(loaded["c"], 16 * len(groups["c"]))
            for bank, a, b in ((3, "cq", "ck"), (4, "cv", "coT")):
                for m in range(2):
                    for c in range(2):
                        last = pe.matmul(psF[:, bank, m * D:(m + 1) * D], t[a][:, c, m * P:(m + 1) * P], t[b][:, c, :],
                                         start=(c == 0), stop=(c == 1))
                last.then_inc(ready, 1)
            pe.wait_ge(loaded["d"], 16 * len(groups["d"]))
            for bank, a, b in ((5, "dkT", "uk"), (6, "dvT", "uv")):
                for m in range(2):
                    last = pe.matmul(psF[:, bank, m * D:(m + 1) * D], t[a][:, m * P:(m + 1) * P], t[b][:, :],
                                     start=True, stop=True)
                last.then_inc(ready, 1)
            for i, (up, b) in enumerate((("uk", "bdk"), ("uv", "bdv"))):
                for m in range(2):
                    last = pe.matmul(psF[:, 0, 2 * i + m:2 * i + m + 1], t[up][:, m * P:(m + 1) * P], t[b][:, :],
                                     start=True, stop=True)
            last.then_inc(bias_ready, 1)
            pe.wait_ge(bias_done, 3)
            for m in range(2):
                last = pe.matmul(psF[:, 7, 0:D], vbw[:, m, :], t["dwo"][:, m, :], start=(m == 0), stop=(m == 1))
            last.then_inc(xb_ready, 1)

        @block.scalar
        def _(act):
            act.wait_ge(lat_ready, 1)
            act.copy(lat[:, :], psF[0:DL, 0, 0:D]).then_inc(lat_taken, 1)
            for i in range(len(BANKS)):
                act.wait_ge(ready, i + 1)
                act.copy(res[:, i, :], psF[:, i + 1, :]).then_inc(taken, 1)

        @block.vector
        def _(dve):
            dve.wait_ge(bias_ready, 1)
            dve.tensor_tensor(vb[:, :], psF[:, 0, 2:4], t["buv"][:, :], ALU.add).then_inc(bias_done, 1)
            dve.tensor_tensor(kb[:, :], psF[:, 0, 0:2], t["buk"][:, :], ALU.add).then_inc(bias_done, 1)
            dve.wait_ge(bias_done, 2)
            dve.tensor_copy(vbw[:, :, :], vb[:, :].unsqueeze(2).to_broadcast([P, 2, P])).then_inc(bias_done, 1)
            dve.wait_ge(xb_ready, 1)
            dve.tensor_tensor(xb[:, :], psF[:, 7, 0:D], t["bo"][:, :], ALU.add).then_inc(bias_done, 1)


def mha_layer(nc, g, ins, decay, scale, project_q, biased):
    X, MV, RSTD = g["X"], g["MV"], g["RSTD"]
    ident, identb = g["ident"], g["identb"]
    NV = 2 if decay else 1
    NCH = 4 * NV
    NAG = 16
    A_AT = [[-19 + 10 * a // 15 for a in range(NAG)], [-22 + 13 * a // 15 for a in range(NAG)]] * 2
    SPLIT_AT = [[-8]] * 4
    A_RING = 2 if decay else 3
    A_BANK = [a % A_RING for a in range(63)] + [1]
    A_LAST = [max(i for i in range(-64, a) if A_BANK[i % 64] == A_BANK[a]) for a in range(64)]
    ROW_DMAS = 3 * NV
    PSLOTS = 4 if decay else 2
    XN = 4 if project_q else 8
    PV_AT = 3 if decay else 1
    KQ = ["k0", "k1"] + (["q0", "q1"] if project_q else [])
    PRO = ["xT0", "xT1"] + KQ + ["v0", "v1"]
    PREV = ["OT3", "aT0", "aT1", "Wo0", "Wo1"]
    late = 2 if decay else 0
    USES = [(4 + late, "OT3"), (5 + late, "xT0"), (6 + late, "xT1"), (8 + late, "k0"), (9 + late, "aT0"), (10, "mT1"),
            (11 + late, "k1"), (13 + late, "aT1"), (15 + late, "q0"), (17 + late, "q1"), (19 + late, "Wo0"),
            (20 + late, "OT0"), (22 + late, "Wo1"), (24, "v0"), (28, "v1"), (26, "mT2"),
            (36 + late, "OT1"), (42, "mT3"), (52 + late, "OT2"), (58, "mT0")]
    USES = sorted(u for u in USES if u[1] in PRO + PREV + ["OT0", "OT1", "OT2", "mT0", "mT1", "mT2", "mT3"])
    MID = [n for _, n in USES]
    ORDER = {"pre": PRO + ["mT0"], "first": [n for n in MID if n not in PREV], "mid": MID,
             "last": [n for n in MID if n not in PRO + ["mT0"]], "post": PREV}
    BY_ACT = PRO + ["mT0", "mT1", "mT2", "mT3", "aT0", "aT1"]
    CHAINS = [(o, c, v) for o in "kq" for c in range(2) for v in range(NV)]
    ROTATE_AT = [12, 13, 16, 17, 20, 21, 24, 25] if decay else [10, 13, 19, 21]
    FIRST_AT = [s + 1 for s in ROTATE_AT] if decay else [15, 17, 25, 27]
    MIDDLE_AT = [s + 3 for s in ROTATE_AT] if decay else [19, 20, 29, 30]
    THIRD_AT = 3

    def base(tag, b):
        if tag == "pre":
            return 0
        if tag == "first":
            return len(ORDER["pre"])
        if tag == "post":
            return base("last", NB - 1) + len(ORDER["last"])
        return (b - 1) * len(MID) + (len(ORDER["pre"]) + len(ORDER["first"]))

    def use(tag, b, name):
        return base(tag, b) + ORDER[tag].index(name)

    def bank(tag, b, name):
        return use(tag, 1 if tag == "mid" else b, name) % 2

    def emptied(tag, b, name):
        if tag != "mid":
            return use(tag, b, name) // 2 + 1
        return (b - 1) * (len(MID) // 2) + (use(tag, 1, name) // 2 + 1)

    def groups(s, tag, at):
        return [(g // 4, g % 4, a) for g in range(6) for a in range(len(at[g % 4])) if 16 * g + at[g % 4][a] == s
                and not (tag == "last" and g > 3)]

    with ExitStack() as ctx:
        def sb(name, shape, dt):
            return ctx.enter_context(nc.sbuf_tensor(f"{g['layer']}_{name}", shape, dt))

        def sem(name):
            return nc.alloc_semaphore(f"{g['layer']}_{name}")

        psA = ctx.enter_context(nc.psum_tensor(f"{g['layer']}_scores_q", [P, 3, S], F32))
        psB = ctx.enter_context(nc.psum_tensor(f"{g['layer']}_scores_k", [P, 2, S], F32))
        psO = ctx.enter_context(nc.psum_tensor(f"{g['layer']}_out_heads", [P, S], F32))
        psM = ctx.enter_context(nc.psum_tensor(f"{g['layer']}_work", [P, 2, S], F32))

        wk, wv, wo = (sb(n, [P, 2, D], F32) for n in ("wk", "wv", "wo"))
        wq = sb("wq", [P, 2, D], F32) if project_q else None
        xn, xnT = sb("xn", [P, 4, D], F32), sb("xnT", [P, 2, S], F32)
        f, fc = sb("f", [P, 2, S], F32), sb("fc", [P, 2, S], F32)
        rr = sb("rr", [P, 2, S], F32)
        parts = sb("parts", [P, 2, 3, S], BF16)
        QS = sb("QS", [99, NV, 2, 8, S], BF16)
        KS = sb("KS", [99, NV, 2, 8, S], BF16)
        probs = sb("probs", [P, PSLOTS, 4, S], F32)
        Vraw, Vaug = sb("Vraw", [P, 4, D], F32), sb("Vaug", [P, 4, H, 32], F32)
        mx, mr = sb("mx", [P, 4, 4], F32), sb("mr", [P, 4, 4], F32)
        mp, mT = sb("mp", [P, 4, 3, 4], BF16), sb("mT", [12, S], BF16)
        Osb, warm = sb("Osb", [P, S], F32), sb("warm", [P, 1], F32)
        rec = sb("rec", [P, 4, 4, 4], F32)
        attn, attnT = sb("attn", [P, 4, D], F32), sb("attnT", [P, 2, S], F32)
        st, mv = sb("st", [P, 2, 6], F32), sb("mv", [P, 2, 2], F32)
        if decay:
            tab = sb("tab", [P, 2, S], F32)
            corr = sb("corr", [P, 4, S], F32)
            low = sb("low", [P, 2, 4, P], F32)
            junk = sb("junk", [P, 2, S], BF16)
        else:
            tab = sb("tab", [P, 2, S], F32)
            sh = sb("sh", [P, 2, S], F32)
        if biased:
            kb = sb("kb", [P, 2], F32)
            xb = sb("xb", [P, D], F32)
        scr = nc.dram_tensor(f"{g['layer']}_parts_dram", [2, NV, 2, 3, P, S], BF16, kind="Internal").ap()

        loaded_by = {name: sem(f"{name}_loaded") for name, _ in ins["load"]}
        loaded = loaded_by["wk"]
        folded = sem("folded")
        ones_set = sem("ones_set")
        root, rstd_done = sem("root"), sem("rstd_done")
        xn_ready = sem("xn_ready")
        xbias_done = sem("xbias_done")
        m_ready = sem("work_ready")
        m_taken = [sem(f"work_taken{i}") for i in range(2)]
        rot_done, sin_done, sum_done = sem("rot_done"), sem("sin_done"), sem("sum_done")
        p0_done, r1_done, p1_done, p2_done = (sem(n) for n in ("p0_done", "r1_done", "p1_done", "p2_done"))
        scr_written = [sem(f"scr_written{i}") for i in range(2)]
        half_loaded = [sem(f"half_loaded{i}") for i in range(2)]
        a_ready, a_done = sem("a_ready"), sem("a_done")
        ms_done = sem("max_split")
        rows_loaded = sem("rows_loaded")
        b_ready, exp_done = sem("b_ready"), sem("exp_done")
        e_ready, e_exp, sel_done = sem("e_ready"), sem("e_exp"), sem("sel_done")
        vaug_done, pv_done, o_taken = sem("vaug_done"), sem("pv_done"), sem("o_taken")
        rec_done = sem("rec_done")
        bns_done, agg_done = sem("bns_done"), sem("agg_done")
        NLOAD = len(ins["load"])

        tiles = {"wq": wq, "wk": wk, "wv": wv, "wo": wo, "tab": tab}
        if decay:
            tiles["corr"] = corr
        if biased:
            tiles["kb"], tiles["xb"] = kb, xb

        def wait_parts(eng, nb, j):
            cnt = nb * (16 * NCH // 2) + 16 * (j // 2)
            if not (isinstance(cnt, int) and cnt == 0):
                eng.wait_ge(scr_written[j % 2], cnt)

        def rotary_sums(eng, nb, pair):
            for j in (pair, pair + 1) if not decay else ():
                eng.wait_ge(rot_done, nb * 8 + (2 * j + 2))
                eng.tensor_tensor(sh[:, j % 2, :], sh[:, j % 2, :], tab[:, 1, :], ALU.mult).then_inc(sin_done, 1)
                eng.wait_ge(sin_done, nb * NCH + (j + 1))
                eng.tensor_tensor(fc[:, j % 2, :], fc[:, j % 2, :], sh[:, j % 2, :], ALU.add).then_inc(sum_done, 1)

        def leave_first(eng, nb, pair):
            for j in (pair, pair + 1):
                eng.wait_ge(p0_done, nb * NCH + (j + 1))
                eng.tensor_tensor(rr[:, j % 2, :], fc[:, j % 2, :], parts[:, j % 2, 0, :], ALU.subtract).then_inc(r1_done, 1)

        def leave_second(eng, nb, pair):
            for j in (pair, pair + 1):
                eng.wait_ge(p1_done, nb * NCH + (j + 1))
                eng.tensor_tensor(parts[:, j % 2, 2, :], rr[:, j % 2, :], parts[:, j % 2, 1, :],
                                  ALU.subtract).then_inc(p2_done, 1)

        block = ctx.enter_context(nc.Block())

        @block.sync
        def _(sp):
            for name, src in ins["load"]:
                sp.dma_start(tiles[name][:], src).then_inc(loaded_by[name], 16)

            def write_parts(nb, j):
                o, c, v = CHAINS[j]
                sp.wait_ge(p2_done, nb * NCH + (j + 1))
                sp.dma_start(scr["kq".index(o), v, c].rearrange("s p t -> p s t"), parts[:, j % 2, :, :]).then_inc(
                    scr_written[j % 2], 16)

            def load_half(nb, c):
                for n in range(2):
                    sp.wait_ge(scr_written[n], (nb + 1) * (16 * NCH // 2))
                for v in range(NV):
                    k3, q3 = scr[0, v, c], scr[1, v, c]
                    for at, n in ((0, 3), (48, 2), (80, 1)):
                        dst = KS[at:at + 16 * n, v, c, :, :].rearrange("p h t -> p (h t)")
                        src = k3[0:n].rearrange("s (d h) t -> (s d) (h t)", d=16)
                        sp.dma_start(dst, src).then_inc(half_loaded[c], 16)
                    for part, (at, n) in enumerate(((0, 3), (48, 2), (80, 1))):
                        dst = QS[at:at + 16 * n, v, c, :, :].rearrange("p h t -> p (h t)")
                        one = q3[part].rearrange("(d h) t -> d (h t)", d=16)
                        src = bass.AP(one.tensor, one.offset, [[0, n]] + [list(x) for x in one.ap])
                        sp.dma_start(dst, src if n > 1 else one).then_inc(half_loaded[c], 16)

            def max_rows(tag, b, nb, grp):
                sp.wait_ge(m_taken[bank(tag, b, f"mT{grp}")], emptied(tag, b, f"mT{grp}"))
                c, h0 = grp // 2, 4 * (grp % 2)
                for v in range(NV):
                    for s in range(3):
                        sp.dma_start(QS[96 + s:97 + s, v, c, h0:h0 + 4, :], mT[4 * s:4 * s + 4, :]).then_inc(
                            rows_loaded, 16)

            for j in range(NCH):
                write_parts(0, j)
            load_half(0, 0)
            max_rows("pre", 0, 0, 0)

            def body(tag, b):
                if tag != "first":
                    sp.wait_ge(b_ready, apart(sp, b * 64, loaded))
                    if decay:
                        sp.wait_ge(e_ready, b * 16)
                load_half(b, 1)
                if tag == "last":
                    for grp in (1, 2, 3):
                        max_rows(tag, b, b, grp)
                    return
                max_rows(tag, b, b, 1)
                for c in range(2):
                    sp.wait_ge(half_loaded[c], (b + 1) * (16 * 6 * NV))
                cut = 6 if decay else 2
                for j in range(cut):
                    write_parts(b + 1, j)
                max_rows(tag, b, b, 2)
                for j in range(cut, NCH):
                    write_parts(b + 1, j)
                sp.wait_ge(b_ready, apart(sp, b * 64 + 32, loaded))
                if decay:
                    sp.wait_ge(e_ready, b * 16 + 8)
                load_half(b + 1, 0)
                max_rows(tag, b, b, 3)
                max_rows(tag, b, b + 1, 0)

            body("first", 0)
            with sp.Fori(1, NB - 1) as b:
                body("mid", b)
            body("last", NB - 1)

        @block.tensor
        def _(pe):
            def work(tag, b, nb, name):
                m, before = bank(tag, b, name), emptied(tag, b, name) - 1
                if not (isinstance(before, int) and before == 0):
                    pe.wait_ge(m_taken[m], before)
                kind, n = name[:-1], int(name[-1])
                if name in ("k0", "aT0", "Wo0"):
                    first, second = {"k0": ("xT0", "xT1"), "aT0": ("OT3", "OT3"), "Wo0": ("aT0", "aT1")}[name]
                    if bank(tag, b, first) not in (m, bank(tag, b, second)):
                        pe.wait_ge(m_taken[bank(tag, b, first)], emptied(tag, b, first))
                    if bank(tag, b, second) != m:
                        pe.wait_ge(m_taken[bank(tag, b, second)], emptied(tag, b, second))
                if kind == "xT":
                    pe.wait_ge(xn_ready, (nb + 1) * XN)
                    for t in range(4):
                        src = xn[:, t, n * P:(n + 1) * P]
                        last = pe.transpose(psM[:, m, t * P:(t + 1) * P], src, ident[:, :])
                elif kind in "kq":
                    w = wk if kind == "k" else wq
                    for c in range(2):
                        last = pe.matmul(psM[:, m, :], w[:, c, n * P:(n + 1) * P], xnT[:, c, :], start=(c == 0), stop=(c == 1))
                elif kind == "v":
                    for t in range(2):
                        for c in range(2):
                            tok = (2 * n + t) * P
                            last = pe.matmul(psM[:, m, t * D:(t + 1) * D], xnT[:, c, tok:tok + P], wv[:, c, :],
                                             start=(c == 0), stop=(c == 1))
                elif kind == "mT":
                    grp = nb * 4 + n
                    pe.wait_ge(ms_done, grp * 4 + 4)
                    for t in range(4):
                        last = pe.transpose(psM[:, m, :].bitcast(BF16)[0:12, t * P:(t + 1) * P],
                                            mp[:, t, :, :].rearrange("p s h -> p (s h)"), identb[:, :])
                elif kind == "OT":
                    pe.wait_ge(o_taken, nb * 4 + (n + 1))
                    for t in range(4):
                        last = pe.transpose(psM[:, m, t * P:(t + 1) * P], Osb[:, t * P:(t + 1) * P], ident[:, :])
                elif kind == "aT":
                    for t in range(4):
                        last = pe.transpose(psM[:, m, t * P:(t + 1) * P], attn[:, t, n * P:(n + 1) * P], ident[:, :])
                elif kind == "Wo":
                    for t in range(2):
                        for c in range(2):
                            tok = (2 * n + t) * P
                            last = pe.matmul(psM[:, m, t * D:(t + 1) * D], attnT[:, c, tok:tok + P], wo[:, c, :],
                                             start=(c == 0), stop=(c == 1))
                last.then_inc(m_ready, 1)

            def max_scores(nb, grp, a):
                k = grp * NAG + a
                if a == 0:
                    pe.wait_ge(half_loaded[grp // 2], (nb + 1) * (16 * 6 * NV))
                if not (isinstance(nb, int) and nb * 64 + A_LAST[k] < 0):
                    pe.wait_ge(a_done, nb * 64 + (A_LAST[k] + 1))
                c, (qt, h) = grp // 2, divmod(a, 4)
                hh = 4 * (grp % 2) + h
                pe.matmul(psA[:, A_BANK[k], :], QS[0:96, 0, c, hh, qt * P:(qt + 1) * P],
                          KS[0:96, NV - 1, c, hh, :], start=True, stop=True).then_inc(a_ready, 1)

            def exp_scores(b, s):
                grp, kt, h = s // 16, s // 4 % 4, s % 4
                c, hh = grp // 2, 4 * (grp % 2) + h
                if s % 16 == 0:
                    pe.wait_ge(rows_loaded, (b * 4 + (grp + 1)) * (16 * ROW_DMAS))
                if not (isinstance(b, int) and b * 64 + s < 2):
                    pe.wait_ge(exp_done, b * 64 + (s - 1))
                keys = slice(kt * P, (kt + 1) * P)
                if not decay:
                    last = pe.matmul(psB[:, s % 2, :], KS[:, 0, c, hh, keys], QS[:, 0, c, hh, :], start=True, stop=True)
                else:
                    end = (kt + 1) * P
                    last = pe.matmul(psB[:, s % 2, 0:end], KS[:, 1, c, hh, keys], QS[:, 0, c, hh, 0:end],
                                     start=True, stop=True)
                    if end < S:
                        last = pe.matmul(psB[:, s % 2, end:S], KS[:, 0, c, hh, keys], QS[:, 1, c, hh, end:S],
                                         start=True, stop=True)
                last.then_inc(b_ready, 1)
                if decay and h == 3:
                    kk = s // 4
                    if not (isinstance(b, int) and b * 16 + kk < 1):
                        pe.wait_ge(e_exp, b * 16 + kk)
                    for i in range(4):
                        hh = 4 * (grp % 2) + i
                        last = pe.matmul(psA[:, 2, i * P:(i + 1) * P], KS[:, 0, c, hh, keys], QS[:, 1, c, hh, keys],
                                         start=True, stop=True)
                    last.then_inc(e_ready, 1)

            def value_sums(b, kk):
                grp, kt = kk // 4, kk % 4
                if kk == 0:
                    pe.wait_ge(vaug_done, b + 1)
                if kt == 0 and not (isinstance(b, int) and b * 4 + grp < 1):
                    pe.wait_ge(o_taken, b * 4 + grp)
                pe.wait_ge(sel_done if decay else exp_done, (b * 16 + (kk + 1)) * (2 if decay else 4))
                if decay and kt:
                    for h in range(4):
                        pe.matmul(psO[32 * h:32 * h + 32, kt * P:(kt + 1) * P], Vaug[:, kt, 4 * grp + h, :],
                                  low[:, kk % 2, h, :], start=False, stop=False)
                for h in range(4):
                    last = pe.matmul(psO[32 * h:32 * h + 32, :], Vaug[:, kt, 4 * grp + h, :],
                                     probs[:, kk % PSLOTS, h, :], start=(kt == 0), stop=(kt == 3))
                if decay and not kt:
                    for h in range(4):
                        last = pe.matmul(psO[32 * h:32 * h + 32, 0:P], Vaug[:, kt, 4 * grp + h, :],
                                         low[:, kk % 2, h, :], start=False, stop=False)
                last.then_inc(pv_done, 1)

            for name in ORDER["pre"][:-1]:
                if name in ("k0", "q0", "v0"):
                    pe.wait_ge(loaded_by[f"w{name[0]}"], 16)
                work("pre", 0, 0, name)
            for a in range(NAG):
                max_scores(0, 0, a)
            work("pre", 0, 0, "mT0")
            for g in (1, 2):
                for a in range(NAG):
                    if 16 * g + A_AT[g][a] < 0:
                        max_scores(0, g, a)

            pe.wait_ge(ones_set, 1 + NV)
            pe.wait_ge(loaded_by["wo"], 16)

            def body(tag, b):
                for s in range(64):
                    grp, o = divmod(s, 16)
                    exp_scores(b, s)
                    if o % 4 == PV_AT:
                        if s > PV_AT:
                            value_sums(b, s // 4 - 1)
                        elif tag != "first":
                            value_sums(b - 1, 15)
                    for ahead, of, a in groups(s, tag, A_AT):
                        max_scores(b + ahead, of, a)
                    for at, name in USES:
                        if at == s and name in ORDER[tag]:
                            nb = b - 1 if name in PREV else b + 1 if name in PRO + ["mT0"] else b
                            work(tag, b, nb, name)

            body("first", 0)
            with pe.Fori(1, NB - 1) as b:
                body("mid", b)
            body("last", NB - 1)
            value_sums(NB - 1, 15)
            for name in ORDER["post"]:
                work("post", NB, NB - 1, name)

        @block.scalar
        def _(act):
            act.activation(RSTD[:, 1, :], MV[:, :, 1], ACT.Sqrt, bias=g["eps"][:, :]).then_inc(root, 1)
            act.activation(warm[:, :], g["eps"][:, :], ACT.Exp)
            if biased:
                act.wait_ge(loaded_by["kb"], 16)

            def take(tag, b, nb, name):
                act.wait_ge(m_ready, use(tag, b, name) + 1)
                kind, n, m = name[:-1], int(name[-1]), bank(tag, b, name)
                if kind == "xT":
                    if not project_q and not (isinstance(nb, int) and nb == 0):
                        act.wait_ge(rot_done, nb * 8)
                    ins_ = act.copy(xnT[:, n, :], psM[:, m, :])
                elif kind in "kq":
                    u = 2 * (kind == "q") + n
                    cnt = nb * 8 + (2 * u - 2)
                    if not (isinstance(cnt, int) and cnt <= 0):
                        act.wait_ge(rot_done, cnt)
                    if biased:
                        ins_ = act.activation(f[:, n, :], psM[:, m, :], ACT.Identity, bias=kb[:, n:n + 1])
                    else:
                        ins_ = act.copy(f[:, n, :], psM[:, m, :])
                elif kind == "v":
                    if not (isinstance(nb, int) and nb == 0):
                        act.wait_ge(vaug_done, nb)
                    ins_ = act.copy(Vraw[:, 2 * n:2 * n + 2, :].rearrange("p t d -> p (t d)"), psM[:, m, :])
                elif kind == "mT":
                    grp = nb * 4 + n
                    if not (isinstance(grp, int) and grp == 0):
                        act.wait_ge(rows_loaded, grp * (16 * ROW_DMAS))
                    ins_ = act.copy(mT[:, :], psM[:, m, :].bitcast(BF16)[0:12, 0:S])
                else:
                    ins_ = act.copy(attnT[:, n, :], psM[:, m, :])
                ins_.then_inc(m_taken[m], 1)

            def middle_part(nb, j):
                act.wait_ge(r1_done, nb * NCH + (j + 1))
                wait_parts(act, nb, j)
                act.copy(parts[:, j % 2, 1, :], rr[:, j % 2, :]).then_inc(p1_done, 1)

            for name in ORDER["pre"][:2]:
                take("pre", 0, 0, name)
            for i, (o, c, v) in enumerate(CHAINS):
                if v == 0 and f"{o}{c}" in PRO:
                    take("pre", 0, 0, f"{o}{c}")
                if i:
                    middle_part(0, i - 1)
            middle_part(0, NCH - 1)
            for name in ("v0", "v1", "mT0"):
                take("pre", 0, 0, name)

            def take_heads(b, grp):
                act.wait_ge(pv_done, b * 16 + (4 * grp + 4))
                n = b * 4 + grp
                act.copy(Osb[:, :], psO[:, :]).then_inc(o_taken, 1)

            def body(tag, b):
                for s in range(64):
                    grp, o = divmod(s, 16)
                    kk, h = s // 4, s % 4
                    if h == 0 and not (isinstance(b, int) and b * 16 + kk < PSLOTS):
                        act.wait_ge(pv_done, b * 16 + (kk - PSLOTS + 1))
                    act.wait_ge(b_ready, b * 64 + (s + 1))
                    act.activation(probs[:, kk % PSLOTS, h, :], psB[:, s % 2, :], ACT.Exp, scale=scale).then_inc(
                        exp_done, 1)
                    if decay and h == 3:
                        act.wait_ge(e_ready, b * 16 + (kk + 1))
                        if not (isinstance(b, int) and b * 16 + kk < 2):
                            act.wait_ge(pv_done, b * 16 + (kk - 1))
                        act.activation(low[:, kk % 2, :, :].rearrange("p h q -> p (h q)"), psA[:, 2, :], ACT.Exp,
                                       scale=scale).then_inc(e_exp, 1)
                    if o == PV_AT + 1:
                        if grp:
                            take_heads(b, grp - 1)
                        elif tag != "first":
                            take_heads(b - 1, 3)
                    for at, name in USES:
                        if at + 1 == s and name in ORDER[tag] and name in BY_ACT:
                            nb = b - 1 if name in PREV else b + 1 if name in PRO + ["mT0"] else b
                            take(tag, b, nb, name)
                    if tag != "last":
                        for j in range(NCH):
                            if MIDDLE_AT[j] == s:
                                middle_part(b + 1, j)

            body("first", 0)
            with act.Fori(1, NB - 1) as b:
                body("mid", b)
            body("last", NB - 1)
            take_heads(NB - 1, 3)
            for name in ("aT0", "aT1"):
                take("post", NB, NB - 1, name)

        @block.vector
        def _(dve):
            dve.wait_ge(root, 1)
            dve.reciprocal(RSTD[:, 0, :], RSTD[:, 1, :]).then_inc(rstd_done, 1)
            dve.wait_ge(rstd_done, 1)

            def normalise(nb, t):
                i = nb * 4 + t
                if project_q:
                    dve.tensor_scalar(xn[:, t, :], X[:, i, :], MV[:, i, 0:1], RSTD[:, 0, bass.ds(i, 1)],
                                      ALU.subtract, ALU.mult).then_inc(xn_ready, 1)
                    return
                for c in range(2):
                    half = slice(c * P, (c + 1) * P)
                    dve.tensor_scalar(xn[:, t, half].rearrange("p (a y h) -> p h y a", a=8, y=2),
                                      X[:, i, half].rearrange("p (h y a) -> p h y a", y=2, a=8), MV[:, i, 0:1],
                                      RSTD[:, 0, bass.ds(i, 1)], ALU.subtract, ALU.mult).then_inc(xn_ready, 1)

            def rotate(tag, b, nb, j):
                o, c, v = CHAINS[j]
                if project_q or o == "k":
                    of, src = f"{o}{c}", f[:, c, :]
                else:
                    of, src = f"xT{c}", xnT[:, c, :]
                dve.wait_ge(m_taken[bank(tag, b, of)], apart(dve, emptied(tag, b, of), loaded))
                cnt = nb * NCH + (j - 1)
                if not (isinstance(cnt, int) and cnt <= 0):
                    dve.wait_ge(r1_done, apart(dve, cnt, loaded))
                if decay:
                    dve.tensor_tensor(fc[:, j % 2, :], src, tab[:, v, :], ALU.mult).then_inc(rot_done, 1)
                else:
                    dve.stream_shuffle(sh[:, j % 2, :], src, [i ^ 8 for i in range(32)]).then_inc(rot_done, 1)
                    dve.tensor_tensor(fc[:, j % 2, :], src, tab[:, 0, :], ALU.mult).then_inc(rot_done, 1)

            def first_part(nb, j):
                if decay:
                    dve.wait_ge(rot_done, nb * 8 + (j + 1))
                else:
                    dve.wait_ge(sum_done, nb * NCH + (j + 1))
                wait_parts(dve, nb, j)
                dve.tensor_copy(parts[:, j % 2, 0, :], fc[:, j % 2, :]).then_inc(p0_done, 1)

            def maxima(nb, grp, a):
                k = grp * NAG + a
                dve.wait_ge(a_ready, apart(dve, nb * 64 + (k + 1), loaded))
                if a == 0 and not (isinstance(nb, int) and nb * 4 + grp == 0):
                    dve.wait_ge(ms_done, apart(dve, (nb * 4 + grp) * 4, loaded))
                qt, h = divmod(a, 4)
                if decay:
                    if not (isinstance(nb, int) and nb * 64 + k < 2):
                        dve.wait_ge(a_done, apart(dve, nb * 64 + (k - 1), loaded))
                    dve.tensor_tensor_reduce(junk[:, a % 2, :], psA[:, A_BANK[k], :], corr[:, qt, :], 1.0, -3.0e38, ALU.mult,
                                             ALU.max, mx[:, qt, h:h + 1]).then_inc(a_done, 1)
                else:
                    dve.tensor_reduce(mx[:, qt, h:h + 1], psA[:, A_BANK[k], :], AX.X, ALU.max).then_inc(a_done, 1)

            def split_maxima(tag, b, nb, grp):
                n = nb * 4 + grp
                dve.wait_ge(a_done, (n + 1) * NAG)
                if tag != "pre":
                    dve.wait_ge(m_ready, base(tag, b) if grp == 1 else use(tag, b, f"mT{(grp - 1) % 4}") + 1)
                flat = mx[:, :, :]
                dve.tensor_scalar(mp[:, :, 0, :], flat, -1.0, None, ALU.mult).then_inc(ms_done, 1)
                dve.wait_ge(ms_done, n * 4 + 1)
                dve.scalar_tensor_tensor(mr[:, :, :], flat, -1.0, mp[:, :, 0, :], ALU.mult, ALU.subtract).then_inc(
                    ms_done, 1)
                dve.wait_ge(ms_done, n * 4 + 2)
                dve.tensor_copy(mp[:, :, 1, :], mr[:, :, :]).then_inc(ms_done, 1)
                dve.wait_ge(ms_done, n * 4 + 3)
                dve.tensor_tensor(mp[:, :, 2, :], mr[:, :, :], mp[:, :, 1, :], ALU.subtract).then_inc(ms_done, 1)

            def lay_values(tag, b):
                for v in ("v0", "v1"):
                    if tag == "first":
                        dve.wait_ge(m_taken[bank("pre", 0, v)], emptied("pre", 0, v))
                    else:
                        dve.wait_ge(m_taken[bank("mid", 1, v)],
                                    b * (len(MID) // 2) + (emptied("mid", 1, v) - len(MID)))
                if tag != "first":
                    dve.wait_ge(pv_done, b * 16)
                dve.tensor_copy(Vaug[:, :, :, 0:16], Vraw[:, :, :].rearrange("p t (h d) -> p t h d", d=16)).then_inc(
                    vaug_done, 1)

            def normalise_heads(tag, b, nb, name):
                n, m = use(tag, b, name), bank(tag, b, name)
                grp = int(name[-1])
                dve.wait_ge(m_ready, n + 1)
                ov = psM[:, m, :].rearrange("p (t h e) -> p t h e", t=4, h=4)
                dve.reciprocal(rec[:, grp, :, :], ov[:, :, :, 16]).then_inc(rec_done, 1)
                dve.wait_ge(rec_done, nb * 4 + (grp + 1))
                dve.tensor_tensor(attn[:, :, 64 * grp:64 * grp + 64].rearrange("p t (h d) -> p t h d", d=16),
                                  ov[:, :, :, 0:16], rec[:, grp, :, :].unsqueeze(3).to_broadcast([P, 4, 4, 16]),
                                  ALU.mult).then_inc(m_taken[m], 1)

            def add_out(tag, b, nb, name):
                j = int(name[-1])
                n, m = use(tag, b, name), bank(tag, b, name)
                dve.wait_ge(m_ready, n + 1)
                if biased:
                    dve.wait_ge(xbias_done, nb + 1)
                i = nb * 4 + 2 * j
                xs = X[:, bass.ds(i, 2), :]
                dve.tensor_tensor(xs, xs, psM[:, m, :].rearrange("p (t d) -> p t d", t=2), ALU.add).then_inc(m_taken[m], 1)
                dve.wait_ge(m_taken[m], apart(dve, emptied(tag, b, name), loaded))
                for t in range(2):
                    dve.bn_stats(st[:, t, :], X[:, i + t, :]).then_inc(bns_done, 1)
                dve.wait_ge(bns_done, apart(dve, nb * 4 + (2 * j + 2), loaded))
                for t in range(2):
                    dve.bn_aggr(mv[:, t, :], st[:, t, :]).then_inc(agg_done, 1)
                dve.wait_ge(agg_done, nb * 4 + (2 * j + 2))
                dve.tensor_copy(MV[:, bass.ds(i, 2), :], mv[:, :, :])

            for t in range(4):
                normalise(0, t)
            dve.wait_ge(loaded_by["tab"], 16)
            for j in range(0, NCH, 2):
                rotate("pre", 0, 0, j)
                rotate("pre", 0, 0, j + 1)
                rotary_sums(dve, 0, j)
                first_part(0, j)
                first_part(0, j + 1)
                leave_first(dve, 0, j)
                leave_second(dve, 0, j)
            if decay:
                dve.wait_ge(loaded_by["corr"], 16)
            for a in range(NAG):
                maxima(0, 0, a)
            split_maxima("pre", 0, 0, 0)
            for g in (1, 2):
                for a in range(NAG):
                    if 16 * g + A_AT[g][a] < 0:
                        maxima(0, g, a)

            def body(tag, b):
                for s in range(64):
                    grp, o = divmod(s, 16)
                    if s == 0 and tag != "last":
                        dve.wait_ge(m_ready, base(tag, b))
                    if s < 4 and tag != "last":
                        normalise(b + 1, s)
                    if s == 2:
                        lay_values(tag, b)
                    for ahead, of, a in groups(s, tag, A_AT):
                        maxima(b + ahead, of, a)
                    for ahead, of, a in groups(s, tag, SPLIT_AT):
                        split_maxima(tag, b, b + ahead, of)
                    for at, name in USES:
                        if at + 1 == s and name in ORDER[tag] and name not in BY_ACT:
                            nb = b - 1 if name in PREV else b
                            (normalise_heads if name[:2] == "OT" else add_out)(tag, b, nb, name)
                    if tag != "last":
                        for j in range(NCH):
                            if ROTATE_AT[j] == s:
                                rotate(tag, b, b + 1, j)
                            if FIRST_AT[j] == s:
                                first_part(b + 1, j)

            body("first", 0)
            with dve.Fori(1, NB - 1) as b:
                body("mid", b)
            body("last", NB - 1)
            for name in ("OT3", "Wo0", "Wo1"):
                (normalise_heads if name[:2] == "OT" else add_out)("post", NB, NB - 1, name)

        @block.gpsimd
        def _(pool):
            for v in range(NV):
                nc.gpsimd.memset(KS[96:99, v, :, :, :], 1.0).then_inc(ones_set, 1)
                pool.wait_ge(ones_set, v + 1)
            nc.gpsimd.memset(Vaug[:, :, :, 16:32], 1.0).then_inc(ones_set, 1)
            pool.wait_ge(ones_set, NV + 1)
            pool.wait_ge(loaded_by["xb" if biased else "tab"], 16)

            def add_bias(nb):
                pool.wait_ge(xn_ready, (nb + 1) * XN)
                xs = X[:, bass.ds(nb * 4, 4), :]
                nc.gpsimd.tensor_tensor(xs, xs, xb[:, :].unsqueeze(1).to_broadcast([P, 4, D]), ALU.add).then_inc(
                    xbias_done, 1)

            def select(b, kk):
                kt = kk % 4
                pool.wait_ge(exp_done, apart(pool, b * 64 + (4 * kk + 4), loaded))
                diag = probs[:, kk % PSLOTS, :, kt * P:(kt + 1) * P]
                nc.gpsimd.affine_select(out=diag, in_=diag, compare_op=ALU.is_ge, fill=0.0, base=0,
                                        pattern=[[0, 4], [-1, P]], channel_multiplier=1).then_inc(sel_done, 1)
                pool.wait_ge(e_exp, apart(pool, b * 16 + (kk + 1), loaded))
                lo = low[:, kk % 2, :, :]
                nc.gpsimd.affine_select(out=lo, in_=lo, compare_op=ALU.is_ge, fill=0.0, base=-1,
                                        pattern=[[0, 4], [1, P]], channel_multiplier=-1).then_inc(sel_done, 1)

            if biased:
                add_bias(0)

            def body(tag, b):
                for s in range(64):
                    if decay and s % 4 == 3:
                        select(b, s // 4)
                    if tag != "last":
                        if biased and s == 4:
                            add_bias(b + 1)
                        for j in range(0, NCH, 2):
                            if ROTATE_AT[j + 1] + 1 == s:
                                rotary_sums(pool, b + 1, j)
                                leave_first(pool, b + 1, j)
                            if ROTATE_AT[j + 1] + 1 + THIRD_AT == s:
                                leave_second(pool, b + 1, j)

            body("first", 0)
            with pool.Fori(1, NB - 1) as b:
                body("mid", b)
            body("last", NB - 1)
def single_head_layer(nc, g, ins):
    X, MV, RSTD, ident = g["X"], g["MV"], g["RSTD"], g["ident"]
    scale = 1.0 / D ** 0.5
    WI = 6
    with ExitStack() as ctx:
        def sb(name, shape):
            return ctx.enter_context(nc.sbuf_tensor(f"{g['layer']}_{name}", shape, F32))

        def ps(name, shape):
            return ctx.enter_context(nc.psum_tensor(f"{g['layer']}_{name}", shape, F32))

        def sem(name):
            return nc.alloc_semaphore(f"{g['layer']}_{name}")

        psW, psS = ps("work", [P, 2, S]), ps("scores", [P, 2, S])
        psP, psO = ps("probs_turned", [P, 2, S]), ps("out", [P, 2, S])
        wg, wv, xb, mask = sb("wg", [P, 2, D]), sb("wv", [P, 2, D]), sb("xb", [P, D]), sb("mask", [P, S])
        xn, xnT = sb("xn", [P, 2, 4, D]), sb("xnT", [P, 2, 2, S])
        tT, v = sb("tT", [P, 2, 2, S]), sb("v", [P, 2, 4, D])
        sc, pr, pT = sb("masked", [P, 2, S]), sb("probs", [P, 2, S]), sb("probsT", [P, 2, S])
        mx, nm = sb("mx", [P, 4]), sb("nm", [P, 4])
        total, rec = sb("total", [P, 4]), sb("rec", [P, 4])
        st, mv = sb("st", [P, 4, 6]), sb("mv", [P, 4, 2])

        loaded, root, rstd_done = sem("loaded"), sem("root"), sem("rstd_done")
        xn_ready, xbias_done = sem("xn_ready"), sem("xbias_done")
        w_ready, w_taken = sem("work_ready"), sem("work_taken")
        s_ready, max_done, nm_done, exp_done = sem("scores_ready"), sem("max_done"), sem("nm_done"), sem("exp_done")
        p_ready, pT_taken = sem("probs_turned"), sem("probsT_taken")
        o_ready, rec_done, added = sem("out_ready"), sem("rec_done"), sem("added")
        bns_done, agg_done = sem("bns_done"), sem("agg_done")
        block = ctx.enter_context(nc.Block())
        LOADS = [(wg, ins["wg"]), (wv, ins["wv"]), (xb, ins["xb"]), (mask, ins["mask"])]

        @block.sync
        def _(sp):
            for to, src in LOADS:
                sp.dma_start(to[tuple(slice(None) for _ in src.shape)], src).then_inc(loaded, 16)

        @block.tensor
        def _(pe):
            pe.wait_ge(loaded, 16 * len(LOADS))

            def work(b, p, i):
                n = b * WI + i
                if not (isinstance(n, int) and n < 2):
                    pe.wait_ge(w_taken, n - 1)
                if i < 2:
                    pe.wait_ge(xn_ready, b * 4 + 4)
                    for t in range(4):
                        last = pe.transpose(psW[:, i, t * P:(t + 1) * P], xn[:, p, t, i * P:(i + 1) * P], ident[:, :])
                elif i < 4:
                    pe.wait_ge(w_taken, b * WI + 2)
                    for c in range(2):
                        last = pe.matmul(psW[:, i % 2, :], wg[:, c, (i - 2) * P:(i - 1) * P], xnT[:, p, c, :],
                                         start=(c == 0), stop=(c == 1))
                else:
                    for t in range(2):
                        k = 2 * (i - 4) + t
                        for c in range(2):
                            last = pe.matmul(psW[:, i % 2, t * D:(t + 1) * D], xnT[:, p, c, k * P:(k + 1) * P],
                                             wv[:, c, :], start=(c == 0), stop=(c == 1))
                last.then_inc(w_ready, 1)

            def scores(b, p, qt):
                n = b * 4 + qt
                if not (isinstance(n, int) and n < 2):
                    pe.wait_ge(max_done, n - 1)
                pe.wait_ge(w_taken, b * WI + 4)
                W = (qt + 1) * P
                for c in range(2):
                    last = pe.matmul(psS[:, qt % 2, 0:W], tT[:, p, c, qt * P:W], xnT[:, p, c, 0:W], start=(c == 0), stop=(c == 1))
                last.then_inc(s_ready, 1)

            def turn(b, qt):
                n = b * 4 + qt
                pe.wait_ge(exp_done, n + 1)
                if not (isinstance(n, int) and n < 2):
                    pe.wait_ge(pT_taken, n - 1)
                for k in range(qt + 1):
                    last = pe.transpose(psP[:, qt % 2, k * P:(k + 1) * P], pr[:, qt % 2, k * P:(k + 1) * P], ident[:, :])
                last.then_inc(p_ready, 1)

            def values(b, p, qt):
                n = b * 4 + qt
                pe.wait_ge(pT_taken, n + 1)
                pe.wait_ge(w_taken, b * WI + 6)
                if not (isinstance(n, int) and n < 2):
                    pe.wait_ge(added, n - 1)
                for k in range(qt + 1):
                    last = pe.matmul(psO[:, qt % 2, 0:D], pT[:, qt % 2, k * P:(k + 1) * P], v[:, p, k, :],
                                     start=(k == 0), stop=(k == qt))
                last.then_inc(o_ready, 1)

            for i in range(WI):
                work(0, 0, i)
            scores(0, 0, 0)
            scores(0, 0, 1)

            def body(b, p, last=False):
                def ahead(i):
                    if not last:
                        work(b + 1, 1 - p, i)
                ahead(0)
                turn(b, 0)
                ahead(1)
                values(b, p, 0)
                scores(b, p, 2)
                turn(b, 1)
                ahead(2)
                values(b, p, 1)
                scores(b, p, 3)
                turn(b, 2)
                ahead(3)
                values(b, p, 2)
                ahead(4)
                turn(b, 3)
                ahead(5)
                if not last:
                    scores(b + 1, 1 - p, 0)
                values(b, p, 3)
                if not last:
                    scores(b + 1, 1 - p, 1)

            body(0, 0)
            body(1, 1)
            with pe.Fori(1, NB // 2 - 1) as j:
                body(j * 2, 0)
                body(j * 2 + 1, 1)
            body(NB - 2, 0)
            body(NB - 1, 1, True)

        @block.scalar
        def _(act):
            act.activation(RSTD[:, 1, :], MV[:, :, 1], ACT.Sqrt, bias=g["eps"][:, :]).then_inc(root, 1)

            def take(b, p, i):
                act.wait_ge(w_ready, b * WI + (i + 1))
                src = psW[:, i % 2, :]
                if i < 2:
                    if not (isinstance(b, int) and b < 2) and i == 0:
                        act.wait_ge(s_ready, b * 4 - 4)
                    act.copy(xnT[:, p, i, :], src).then_inc(w_taken, 1)
                elif i < 4:
                    act.copy(tT[:, p, i - 2, :], src).then_inc(w_taken, 1)
                else:
                    if not (isinstance(b, int) and b < 2) and i == 4:
                        act.wait_ge(o_ready, b * 4 - 4)
                    k = 2 * (i - 4)
                    act.copy(v[:, p, k:k + 2, :].rearrange("p t d -> p (t d)"), src).then_inc(w_taken, 1)

            def exps(b, qt):
                n = b * 4 + qt
                W = (qt + 1) * P
                act.wait_ge(nm_done, n + 1)
                if not (isinstance(n, int) and n < 2):
                    act.wait_ge(p_ready, n - 1)
                if not (isinstance(n, int) and n < 4):
                    act.wait_ge(rec_done, n - 3)
                act.activation(pr[:, qt % 2, 0:W], sc[:, qt % 2, 0:W], ACT.Exp, bias=nm[:, qt:qt + 1], scale=scale,
                               accum_out=total[:, qt:qt + 1]).then_inc(exp_done, 1)

            def take_probs(b, qt):
                n = b * 4 + qt
                W = (qt + 1) * P
                act.wait_ge(p_ready, n + 1)
                if not (isinstance(n, int) and n < 2):
                    act.wait_ge(o_ready, n - 1)
                act.copy(pT[:, qt % 2, 0:W], psP[:, qt % 2, 0:W]).then_inc(pT_taken, 1)

            for i in range(WI):
                take(0, 0, i)
            exps(0, 0)
            exps(0, 1)

            def body(b, p, last=False):
                def ahead(i):
                    if not last:
                        take(b + 1, 1 - p, i)
                ahead(0)
                take_probs(b, 0)
                ahead(1)
                exps(b, 2)
                take_probs(b, 1)
                ahead(2)
                exps(b, 3)
                take_probs(b, 2)
                ahead(3)
                ahead(4)
                take_probs(b, 3)
                ahead(5)
                if not last:
                    exps(b + 1, 0)
                    exps(b + 1, 1)

            body(0, 0)
            body(1, 1)
            with act.Fori(1, NB // 2 - 1) as j:
                body(j * 2, 0)
                body(j * 2 + 1, 1)
            body(NB - 2, 0)
            body(NB - 1, 1, True)

        @block.vector
        def _(dve):
            dve.wait_ge(root, 1)
            dve.reciprocal(RSTD[:, 0, :], RSTD[:, 1, :]).then_inc(rstd_done, 1)
            dve.wait_ge(rstd_done, 1)
            dve.wait_ge(loaded, 16 * len(LOADS))

            def normalise(b, p):
                if not (isinstance(b, int) and b < 2):
                    dve.wait_ge(w_ready, b * WI - 10)
                for t in range(4):
                    i = b * 4 + t
                    dve.tensor_scalar(xn[:, p, t, :], X[:, i, :], MV[:, i, 0:1], RSTD[:, 0, bass.ds(i, 1)],
                                      ALU.subtract, ALU.mult).then_inc(xn_ready, 1)

            def maximum(b, qt):
                n = b * 4 + qt
                W = (qt + 1) * P
                dve.wait_ge(s_ready, apart(dve, n + 1, loaded))
                if not (isinstance(n, int) and n < 2):
                    dve.wait_ge(exp_done, apart(dve, n - 1, loaded))
                dve.tensor_tensor_reduce(sc[:, qt % 2, 0:W], psS[:, qt % 2, 0:W], mask[:, S - W:S], 1.0, -3.0e38, ALU.add,
                                         ALU.max, mx[:, qt:qt + 1]).then_inc(max_done, 1)
                dve.wait_ge(max_done, n + 1)
                dve.tensor_scalar(nm[:, qt:qt + 1], mx[:, qt:qt + 1], -scale, None, ALU.mult).then_inc(nm_done, 1)

            def add_out(b, qt):
                n = b * 4 + qt
                dve.wait_ge(exp_done, n + 1)
                dve.reciprocal(rec[:, qt:qt + 1], total[:, qt:qt + 1]).then_inc(rec_done, 1)
                dve.wait_ge(rec_done, n + 1)
                dve.wait_ge(o_ready, n + 1)
                if qt == 0:
                    dve.wait_ge(xbias_done, b + 1)
                dve.scalar_tensor_tensor(X[:, n, :], psO[:, qt % 2, 0:D], rec[:, qt:qt + 1], X[:, n, :], ALU.mult,
                                         ALU.add).then_inc(added, 1)
                dve.wait_ge(added, apart(dve, n + 1, loaded))
                dve.bn_stats(st[:, qt, :], X[:, n, :]).then_inc(bns_done, 1)
                dve.wait_ge(bns_done, apart(dve, n + 1, loaded))
                dve.bn_aggr(mv[:, qt, :], st[:, qt, :]).then_inc(agg_done, 1)
                if qt == 3:
                    dve.wait_ge(agg_done, n + 1)
                    dve.tensor_copy(MV[:, bass.ds(b * 4, 4), :], mv[:, :, :])

            normalise(0, 0)
            normalise(1, 1)
            maximum(0, 0)
            maximum(0, 1)

            def body(b, p, more=True, last=False):
                maximum(b, 2)
                add_out(b, 0)
                maximum(b, 3)
                if more:
                    normalise(b + 2, p)
                add_out(b, 1)
                add_out(b, 2)
                if not last:
                    maximum(b + 1, 0)
                    maximum(b + 1, 1)
                add_out(b, 3)

            body(0, 0)
            body(1, 1)
            with dve.Fori(1, NB // 2 - 1) as j:
                body(j * 2, 0)
                body(j * 2 + 1, 1)
            body(NB - 2, 0, False)
            body(NB - 1, 1, False, True)

        @block.gpsimd
        def _(pool):
            pool.wait_ge(loaded, 16 * len(LOADS))
            with pool.Fori(0, NB) as b:
                pool.wait_ge(xn_ready, b * 4 + 4)
                xs = X[:, bass.ds(b * 4, 4), :]
                nc.gpsimd.tensor_tensor(xs, xs, xb[:, :].unsqueeze(1).to_broadcast([P, 4, D]), ALU.add).then_inc(
                    xbias_done, 1)




HEAD_DIMS = [a + HD // 2 * y for a in range(HD // 2) for y in range(2)]
COLS = [(8 * c + h) * HD + d for c in range(2) for d in HEAD_DIMS for h in range(8)]


def hybrid_stack(nc, w, out):
    with ExitStack() as ctx:
        g = global_tensors(nc, ctx)
        folded = {n: nc.dram_tensor(f"folded_{n}", s, F32, kind="Internal").ap() for n, s in FOLDED.items()}
        experts_a = {"wg": w["gate_a"], "bg": w["gate_bias"], "we": w["we"], "be": w["be"]}
        experts_b = {"wg": w["gate_b"], "w1": w["w1"], "w2": w["w2"], "out": out}
        decay = {"load": [("wk", folded["a_wk"]), ("tab", w["decay_tab"]), ("wq", w["a_wq"]), ("wv", folded["a_wv"]),
                          ("wo", w["a_wo"]), ("corr", w["corr"])]}
        rope = {"load": [("wk", w["b_wk"]), ("tab", w["rope_tab"]), ("wq", w["b_wq"]), ("wv", w["b_wv"]), ("wo", w["b_wo"])]}
        causal = {"wg": folded["c_wg"], "wv": folded["c_wv"], "xb": w["c_bias"], "mask": w["mask"]}
        latent = {"load": [("wk", folded["d_wk"]), ("tab", w["rope_tab"]), ("wv", folded["d_wv"]), ("wo", w["dwo"]),
                           ("kb", folded["d_kb"]), ("xb", folded["d_xb"])]}

        def layer(name):
            g["layer"] = name
            return nc.cleanup_on_exit()

        with layer("tokens"):
            load_tokens(nc, g, w)
        with layer("fold"):
            fold_weights(nc, w, folded)
        with layer("decay"):
            mha_layer(nc, g, decay, True, 1.0 / D ** 0.5, True, False)
        with layer("experts1"):
            routed_layer(nc, g, experts_a, False)
        with layer("rope"):
            mha_layer(nc, g, rope, False, HD ** -0.5, True, False)
        with layer("experts2"):
            routed_layer(nc, g, experts_a, False)
        with layer("causal"):
            single_head_layer(nc, g, causal)
        with layer("experts3"):
            routed_layer(nc, g, experts_b, True)
        with layer("latent"):
            mha_layer(nc, g, latent, False, HD ** -0.5, False, True)
        with layer("experts4"):
            routed_layer(nc, g, experts_b, True, last_layer=True)


def chunked(a):
    return np.ascontiguousarray(a.reshape(-1, P, a.shape[-1]).transpose(1, 0, 2))


def every_partition(a):
    return np.ascontiguousarray(np.broadcast_to(a.reshape(-1), (P, a.size)))


def tables():
    i = np.arange(S)
    angles = np.outer(i, 1.0 / 10000.0 ** (np.arange(0, HD, 2) / HD))
    angles = np.concatenate([angles, angles], -1).T
    sign = np.where(np.arange(HD) < HD // 2, -1.0, 1.0)[:, None]
    dims = [d for d in HEAD_DIMS for _ in range(8)]
    rope = np.stack([np.cos(angles)[dims], (np.sin(angles) * sign)[dims]], 1)
    decay = np.broadcast_to(np.stack([np.exp(.01 * (i - S / 2)), np.exp(-.01 * (i - S / 2))]), (P, 2, S))
    q, k = i[:, None], i[None]
    corr = np.where(k >= q, 1.0, np.exp(-.02 * (q - k))).reshape(4, P, S).transpose(1, 0, 2)
    mask = np.where(k[:, :] - (S - P) > np.arange(P)[:, None], -1e30, 0.0)
    t = {"rope_tab": rope, "decay_tab": decay, "corr": corr, "mask": mask, "ident": np.eye(P),
         "before": np.triu(np.ones((P, P)), 1), "con": shape_constants()}
    return {n: np.ascontiguousarray(a, dtype=np.float32) for n, a in t.items()}


def layouts(L0_attn_a_x, L0_attn_a_W_q, L0_attn_a_W_k, L0_attn_a_W_v, L0_attn_a_W_o, L0_attn_a_W_down_kv,
            L0_attn_a_W_up_k, L0_attn_a_W_up_v, L0_attn_b_Wqkv, L0_attn_b_Wo, L0_ffn_Wg, L0_ffn_bg, L0_ffn_We, L0_ffn_be,
            L1_attn_a_qkv_w, L1_attn_a_out_w, L1_attn_a_out_b, L1_attn_b_w_dk, L1_attn_b_b_dk, L1_attn_b_w_dv,
            L1_attn_b_b_dv, L1_attn_b_w_uk, L1_attn_b_b_uk, L1_attn_b_w_uv, L1_attn_b_b_uv, L1_attn_b_w_o,
            L1_attn_b_b_o, L1_ffn_Wr, L1_ffn_W1, L1_ffn_W2):
    tiles = L0_attn_a_x.reshape(NB, 4, P, D).transpose(0, 2, 1, 3)
    q, k, v = (L0_attn_b_Wqkv[:, i * D:(i + 1) * D] for i in range(3))
    cq, ck, cv = (L1_attn_a_qkv_w[i * D:(i + 1) * D] for i in range(3))
    return {
        "x": tiles,
        "a_wq": chunked(L0_attn_a_W_q[:, COLS]), "a_wo": chunked(L0_attn_a_W_o),
        "wkT": chunked(L0_attn_a_W_k.T), "wvT": chunked(L0_attn_a_W_v.T), "wdown": chunked(L0_attn_a_W_down_kv),
        "upk": L0_attn_a_W_up_k[:, COLS], "upv": L0_attn_a_W_up_v,
        "b_wq": chunked(q[:, COLS]), "b_wk": chunked(k[:, COLS]), "b_wv": chunked(v), "b_wo": chunked(L0_attn_b_Wo),
        "gate_a": chunked(L0_ffn_Wg), "gate_bias": every_partition(L0_ffn_bg),
        "we": L0_ffn_We.reshape(E, 2, P, D).transpose(2, 1, 0, 3).reshape(P, 2, E * D), "be": every_partition(L0_ffn_be),
        "cq": chunked(cq), "ck": chunked(ck), "cv": chunked(cv), "coT": chunked(L1_attn_a_out_w.T),
        "c_bias": every_partition(L1_attn_a_out_b),
        "dkT": L1_attn_b_w_dk[COLS].T, "dvT": L1_attn_b_w_dv[COLS].T, "uk": L1_attn_b_w_uk[:, COLS], "uv": L1_attn_b_w_uv,
        "bdk": L1_attn_b_b_dk.reshape(P, 1), "bdv": L1_attn_b_b_dv.reshape(P, 1),
        "buk": L1_attn_b_b_uk[COLS].reshape(2, P).T, "buv": L1_attn_b_b_uv.reshape(2, P).T,
        "dwo": chunked(L1_attn_b_w_o), "bo": every_partition(L1_attn_b_b_o),
        "gate_b": chunked(L1_ffn_Wr),
        "w1": L1_ffn_W1.reshape(E, 2, P, F).transpose(0, 2, 1, 3),
        "w2": L1_ffn_W2.reshape(E, F // P, P, D).transpose(0, 2, 1, 3),
    }


def kernel(**inputs):
    import concourse.bacc as _bacc
    from concourse.bass_utils import run_bass_kernel_spmd as _run

    nc = _bacc.Bacc("TRN2", target_bir_lowering=False, num_devices=1)
    data = layouts(**{n: np.asarray(a) for n, a in inputs.items()})
    data.update(tables())
    arrays, w = {}, {}
    for name, a in data.items():
        a = np.ascontiguousarray(a)
        arrays[f"in_{name}_dram"] = a
        w[name] = nc.dram_tensor(f"in_{name}_dram", a.shape, mybir.dt.from_np(a.dtype), kind="ExternalInput").ap()
    out = nc.dram_tensor("out_0_dram", (NB, S, D), F32, kind="ExternalOutput").ap()
    hybrid_stack(nc, w, [out[q].rearrange("(t p) d -> p t d", p=P) for q in range(NB)])
    return _run(nc, [arrays], core_ids=[0]).results[0]["out_0_dram"]
```

```python
from contextlib import ExitStack

import numpy as np

import concourse.bass as bass
from concourse import mybir

F32, BF16 = mybir.dt.float32, mybir.dt.bfloat16
I32, U32 = mybir.dt.int32, mybir.dt.uint32
ALU, ACT, AX = mybir.AluOpType, mybir.ActivationFunctionType, mybir.AxisListType

P = 128
NB, S, D = 8, 512, 256
H, HD = 16, 16
E = 8
F = 1024
T = NB * S
NT = T // P
EPS = 1e-5


def apart(eng, value, held):
    if isinstance(value, int):
        return value
    value = eng.to_reg(value)
    eng.wait_ge(held, 16)
    return value


HALF_TILES = NT // 2
CAP = T // E
HALF_SLOTS = T // 2 + E * P
EXPERT_TILES = HALF_SLOTS // P
CAP_SLOTS = E * CAP
ZERO_ROW = CAP_SLOTS
BIG = 65536.0


CLEARS = 4


def routing(nc, g, ins, capacity, half=0, alongside=None):
    t0, nt = half * HALF_TILES, HALF_TILES
    X, MV, RSTD, XN = g["X"], g["MV"], g["RSTD"], g["XN"]
    ident, con = g["ident"], g["con"]
    slot, back, weight = (g[n][:, t0:t0 + nt] for n in ("slot", "back", "weight"))
    te, wg, bg, nmr, loaded = g["te"][half], g["wg"], g["bg"], g["nmr"], g["gate_loaded"]
    LP = 1 if capacity else 2
    NQ = nt // 4

    with ExitStack() as ctx:
        def sb(name, shape, dt):
            return ctx.enter_context(nc.sbuf_tensor(f"{g['layer']}r{half}_{name}", shape, dt))

        def sem(name):
            return nc.alloc_semaphore(f"{g['layer']}r{half}_{name}")

        psT = ctx.enter_context(nc.psum_tensor(f"{g['layer']}r{half}_turned", [P, 2, S], F32))
        psL = ctx.enter_context(nc.psum_tensor(f"{g['layer']}r{half}_logits", [P, 2, LP, 2, D], F32))
        psR = ctx.enter_context(nc.psum_tensor(f"{g['layer']}r{half}_ranks", [P, nt, E], F32))
        psC = ctx.enter_context(nc.psum_tensor(f"{g['layer']}r{half}_totals", [P, nt, E], F32))
        xnT = sb("xnT", [P, 2, 2, S], F32)
        lg = sb("lg", [P, nt, E] if capacity else [P, 2, 2, 2, D], F32)
        if not capacity:
            top = sb("top", [P, 4, 8], F32)
            ntop = sb("ntop", [P, nt], F32)
            idx = sb("idx", [P, 4, 8], U32)
            first = sb("first", [P, nt], U32)
            low3 = sb("low3", [P, nt], U32)
            ex = sb("ex", [P, 2, D], F32)
            cnt_i = sb("cnt_i", [P, E], I32)
            blk, blk_inc = sb("blk", [P, E], F32), sb("blk_inc", [P, E], F32)
            past = sb("past", [P, EXPERT_TILES, E], F32)
            tef = sb("tef", [P, EXPERT_TILES], F32)
        sums = sb("sums", [P, nt], F32)
        best = sb("best", [P, nt], F32)
        oh, ohb = sb("oh", [P, nt, E], F32), sb("ohb", [P, nt, E], BF16)
        tot, inc = sb("tot", [P, E, nt], F32), sb("inc", [P, E, nt], F32)
        rk = sb("rk", [P, nt, E], F32)
        rank, keep = sb("rank", [P, nt], F32), sb("keep", [P, nt], F32)

        root, rstd_done = sem("root"), sem("rstd_done")
        xn_ready = sem("xn_ready")
        t_ready, t_taken = sem("turned_ready"), sem("turned_taken")
        l_ready, l_taken = sem("logits_ready"), sem("logits_taken")
        top_done, first_done, exp_done = sem("top_done"), sem("first_done"), sem("exp_done")
        steps = sem("steps")
        oh_ready, counted = sem("oh_ready"), sem("counted")

        block = ctx.enter_context(nc.Block())

        if alongside:
            @block.gpsimd
            def _(pool):
                alongside(pool)

        @block.sync
        def _(sp):
            if half:
                return
            sp.dma_start(wg[:, :, :], ins["wg"]).then_inc(loaded, 16)
            if not capacity:
                sp.dma_start(bg[:, :], ins["bg"]).then_inc(loaded, 16)

        @block.tensor
        def _(pe):
            pe.wait_ge(loaded, 16 if capacity else 32)

            def turn(q, par):
                pe.wait_ge(xn_ready, q * 4 + 4)
                for c in range(2):
                    if q:
                        pe.wait_ge(t_taken, q * 2 + (c - 1))
                    for t in range(4):
                        last = pe.transpose(psT[:, c, t * P:(t + 1) * P], XN[:, t0 + q * 4 + t, c * P:(c + 1) * P], ident[:, :])
                    last.then_inc(t_ready, 1)

            def score(q, par):
                pe.wait_ge(t_taken, q * 2 + 2)
                for pair in range(2):
                    n = q * 2 + pair
                    if not capacity:
                        if n >= 4:
                            pe.wait_ge(l_taken, n - 3)
                    elif pair == 0 and q >= 2:
                        pe.wait_ge(l_taken, q - 1)
                    for t in range(2):
                        tok = (2 * pair + t) * P
                        if capacity:
                            out = psL[:, par, 0, 0, (2 * pair + t) * E:(2 * pair + t + 1) * E]
                        else:
                            out = psL[:, par, pair, t, :]
                        for c in range(2):
                            last = pe.matmul(out, xnT[:, par, c, tok:tok + P], wg[:, c, :], start=(c == 0), stop=(c == 1))
                    if not capacity or pair == 1:
                        last.then_inc(l_ready, 1)

            turn(0, 0)
            for q in range(1, NQ):
                turn(q, q % 2)
                score(q - 1, (q - 1) % 2)
            score(NQ - 1, (NQ - 1) % 2)
            pe.wait_ge(oh_ready, 1)
            flat = ohb[:, :, :].rearrange("p t e -> p (t e)")
            pe.matmul(psR[:, :, :].rearrange("p t e -> p (t e)"), g["before"][:, :], flat, start=True, stop=True).then_inc(
                counted, 1)
            pe.matmul(psC[:, :, :].rearrange("p t e -> p (t e)"), g["ones"][:, :], flat, start=True, stop=True).then_inc(
                counted, 1)

        @block.scalar
        def _(act):
            if not half:
                act.activation(RSTD[:, 1, :], MV[:, :, 1], ACT.Sqrt, bias=g["eps"][:, :]).then_inc(root, 1)

            def take(q, par):
                for c in range(2):
                    act.wait_ge(t_ready, q * 2 + (c + 1))
                    if c == 0 and not (isinstance(q, int) and q < 2):
                        act.wait_ge(l_ready, q * LP - LP)
                    act.copy(xnT[:, par, c, :], psT[:, c, :]).then_inc(t_taken, 1)

            def normalise(q):
                if capacity:
                    return
                for t in range(4):
                    i = q * 4 + t
                    act.activation(XN[:, i + t0, :], X[:, i + t0, :], ACT.Identity, bias=nmr[:, bass.ds(i + t0, 1)],
                                   scale=RSTD[:, 0, bass.ds(i + t0, 1)]).then_inc(xn_ready, 1)

            def exps(q, par):
                if capacity:
                    return
                for t in range(4):
                    i = q * 4 + t
                    act.wait_ge(top_done, i * 3 + 4 - t % 2)
                    if not (isinstance(i, int) and i < 2):
                        act.wait_ge(exp_done, i - 1)
                    act.activation(ex[:, t % 2, :], lg[:, par, t // 2, t % 2, :], ACT.Exp, bias=ntop[:, bass.ds(i, 1)],
                                   accum_out=sums[:, bass.ds(i, 1)]).then_inc(exp_done, 1)

            def pair(j):
                normalise(j * 2 + 2)
                take(j * 2 + 1, 1)
                exps(j * 2, 0)
                normalise(j * 2 + 3)
                take(j * 2 + 2, 0)
                exps(j * 2 + 1, 1)

            if not capacity and not half:
                act.wait_ge(rstd_done, 2)
            normalise(0)
            take(0, 0)
            normalise(1)
            pair(0)
            take(NQ - 1, 1)
            exps(NQ - 2, 0)
            exps(NQ - 1, 1)
            if capacity:
                act.wait_ge(steps, 2)
                flat = lg[:, :, :].rearrange("p t e -> p (t e)")
                act.activation(flat, flat, ACT.Exp).then_inc(exp_done, 1)

        @block.vector
        def _(dve):
            if not half:
                dve.wait_ge(root, 1)
                dve.reciprocal(RSTD[:, 0, :], RSTD[:, 1, :]).then_inc(rstd_done, 1)
                dve.wait_ge(rstd_done, 1)
            if not capacity and not half:
                dve.scalar_tensor_tensor(nmr[:, :], MV[:, :, 0], -1.0, RSTD[:, 0, :], ALU.mult, ALU.mult).then_inc(
                    rstd_done, 1)
            dve.wait_ge(loaded, 16 if capacity else 32)

            def normalise(q):
                if not capacity:
                    return
                for t in range(4):
                    i = t0 + q * 4 + t
                    dve.tensor_scalar(XN[:, i, :], X[:, i, :], MV[:, i, 0:1], RSTD[:, 0, bass.ds(i, 1)],
                                      ALU.subtract, ALU.mult).then_inc(xn_ready, 1)

            def top_logits(q, par):
                if capacity:
                    dve.wait_ge(l_ready, q + 1)
                    dve.tensor_copy(lg[:, bass.ds(q * 4, 4), :], psL[:, par, 0, 0, 0:4 * E].rearrange(
                        "p (t e) -> p t e", t=4)).then_inc(l_taken, 1)
                    return
                for pair in range(2):
                    n = q * 2 + pair
                    dve.wait_ge(l_ready, n + 1)
                    if not (isinstance(n, int) and n < 4):
                        dve.wait_ge(exp_done, n * 2 - 6)
                    dve.tensor_tensor(lg[:, par, pair, :, :], psL[:, par, pair, :, :],
                                      bg[:, :].unsqueeze(1).to_broadcast([P, 2, D]), ALU.add).then_inc(l_taken, 1)
                    dve.wait_ge(l_taken, apart(dve, n + 1, loaded))
                    for t in range(2):
                        dve.max(top[:, 2 * pair + t, :], lg[:, par, pair, t, :]).then_inc(top_done, 1)
                    dve.wait_ge(top_done, apart(dve, (q * 4 + 2 * pair) * 3 + 2, loaded))
                    for t in range(2):
                        i = q * 4 + (2 * pair + t)
                        k = 2 * pair + t
                        dve.max_index(idx[:, k, :], top[:, k, :], lg[:, par, pair, t, :]).then_inc(top_done, 1)
                        dve.tensor_scalar(ntop[:, bass.ds(i, 1)], top[:, k, 0:1], -1.0, None, ALU.mult).then_inc(top_done, 1)
                dve.wait_ge(top_done, q * 12 + 12)
                dve.tensor_copy(first[:, bass.ds(q * 4, 4)], idx[:, :, 0]).then_inc(first_done, 1)

            def pair(j):
                normalise(j * 2 + 2)
                top_logits(j * 2, 0)
                normalise(j * 2 + 3)
                top_logits(j * 2 + 1, 1)

            normalise(0)
            normalise(1)
            pair(0)
            top_logits(NQ - 2, 0)
            top_logits(NQ - 1, 1)

            done = [0]

            def link(ins_):
                done[0] += 1
                ins_.then_inc(steps, 1)
                dve.wait_ge(steps, done[0])

            def over_experts(ap):
                return ap.unsqueeze(2).to_broadcast([P, nt, E])

            def over_tiles(ap):
                return ap.unsqueeze(1).to_broadcast([P, nt, E])

            if capacity:
                dve.wait_ge(l_taken, NQ)
                link(dve.tensor_reduce(best[:, :], lg[:, :, :], AX.X, ALU.max))
                link(dve.tensor_tensor(lg[:, :, :], lg[:, :, :], over_experts(best[:, :]), ALU.subtract))
                dve.wait_ge(exp_done, 1)
                link(dve.tensor_reduce(sums[:, :], lg[:, :, :], AX.X, ALU.add))
                link(dve.tensor_scalar(rk[:, :, :], lg[:, :, :], 1.0, None, ALU.is_ge))
                link(dve.tensor_tensor(rk[:, :, :], rk[:, :, :], over_tiles(con["down8"]), ALU.mult))
                link(dve.tensor_reduce(best[:, :], rk[:, :, :], AX.X, ALU.max))
                link(dve.tensor_tensor(oh[:, :, :], over_tiles(con["down8"]), over_experts(best[:, :]), ALU.is_equal))
            else:
                dve.wait_ge(exp_done, nt)
                dve.wait_ge(first_done, NQ)
                link(dve.tensor_scalar(low3[:, :], first[:, :], E - 1, None, ALU.bitwise_and))
                link(dve.tensor_copy(best[:, :], low3[:, :]))
                link(dve.tensor_tensor(oh[:, :, :], over_tiles(con["up8"]), over_experts(best[:, :]), ALU.is_equal))
            dve.tensor_copy(ohb[:, :, :], oh[:, :, :]).then_inc(oh_ready, 1)
            link(dve.reciprocal(weight[:, :], sums[:, :]))
            dve.wait_ge(counted, 2)
            link(dve.tensor_copy(tot[:, :, :], psC[:, :, :].rearrange("p t e -> p e t")))
            link(dve.tensor_tensor_scan(inc[:, :, :].rearrange("p e t -> p (e t)"), con["resets"],
                                        tot[:, :, :].rearrange("p e t -> p (e t)"), 0.0, ALU.mult, ALU.add))
            link(dve.tensor_tensor(tot[:, :, :], inc[:, :, :], tot[:, :, :], ALU.subtract))
            link(dve.tensor_tensor(rk[:, :, :], psR[:, :, :], tot[:, :, :].rearrange("p e t -> p t e"), ALU.add))
            if capacity and half == 0:
                link(dve.tensor_copy(g["carry"][:, :], inc[:, :, nt - 1]))
            elif capacity:
                link(dve.tensor_tensor(rk[:, :, :], rk[:, :, :], over_tiles(g["carry"][:, :]), ALU.add))
            if not capacity:
                link(dve.tensor_scalar(cnt_i[:, :], inc[:, :, nt - 1], float(P - 1), None, ALU.add))
                link(dve.tensor_scalar(cnt_i[:, :], cnt_i[:, :], P.bit_length() - 1, None, ALU.arith_shift_right))
                link(dve.tensor_copy(blk[:, :], cnt_i[:, :]))
                link(dve.tensor_tensor_scan(blk_inc[:, :], con["ones8"], blk[:, :], 0.0, ALU.mult, ALU.add))
                link(dve.tensor_tensor(blk[:, :], blk_inc[:, :], blk[:, :], ALU.subtract))
                link(dve.tensor_scalar(blk[:, :], blk[:, :], float(P), None, ALU.mult))
                link(dve.tensor_tensor(rk[:, :, :], rk[:, :, :], over_tiles(blk[:, :]), ALU.add))
                link(dve.tensor_tensor(past[:, :, :], con["tiles"].unsqueeze(2).to_broadcast([P, EXPERT_TILES, E]),
                                       blk_inc[:, :].unsqueeze(1).to_broadcast([P, EXPERT_TILES, E]), ALU.is_ge))
                link(dve.tensor_reduce(tef[:, :], past[:, :, :], AX.X, ALU.add))
                link(dve.tensor_scalar(tef[:, :], tef[:, :], float(E - 1), float(D), ALU.min, ALU.mult))
                link(dve.tensor_copy(te[:, :], tef[:, :]))
            link(dve.tensor_tensor(rk[:, :, :], rk[:, :, :], oh[:, :, :], ALU.mult))
            link(dve.tensor_reduce(rank[:, :], rk[:, :, :], AX.X, ALU.add))
            if capacity:
                link(dve.tensor_scalar(keep[:, :], rank[:, :], float(CAP), BIG, ALU.is_ge, ALU.mult))
                link(dve.tensor_tensor(rank[:, :], rank[:, :], keep[:, :], ALU.add))
                link(dve.tensor_scalar(best[:, :], best[:, :], -float(CAP), float(CAP * E), ALU.mult, ALU.add))
                link(dve.tensor_tensor(rank[:, :], rank[:, :], best[:, :], ALU.add))
            link(dve.tensor_copy(slot[:, :], rank[:, :]))
            link(dve.tensor_scalar(keep[:, :], rank[:, :], float(ZERO_ROW), None, ALU.min))
            link(dve.tensor_copy(back[:, :], keep[:, :]))


def dispatch(pool, g, xe, tiles, scattered):
    for i in tiles:
        pool.indirect_dma_start(out=xe, out_offset=bass.IndirectOffsetOnAxis(ap=g["slot"][:, i:i + 1], axis=0),
                                in_=g["XN"][:, i, :], in_offset=None, bounds_check=xe.shape[0] - 1,
                                oob_is_err=False).then_inc(scattered, 16)


def collect(pool, g, ye, tiles, gathered, taken=None, before=0):
    for n, i in enumerate(tiles):
        if taken is not None and n >= len(gathered):
            pool.wait_ge(taken, before + n - len(gathered) + 1)
        pool.indirect_dma_start(out=g["XN"][:, i, :], out_offset=None, in_=ye,
                                in_offset=bass.IndirectOffsetOnAxis(ap=g["back"][:, i:i + 1], axis=0)).then_inc(
            gathered[n % len(gathered)], 16)


def experts_small(nc, g, half, alongside):
    te, we, be, xe, ye = g["te"][half], g["we"], g["be"], g["xe"][half], g["ye"][half]
    RING = 8
    with ExitStack() as ctx:
        def sb(name, shape, dt):
            return ctx.enter_context(nc.sbuf_tensor(f"{g['layer']}x{half}_{name}", shape, dt))

        def sem(name):
            return nc.alloc_semaphore(f"{g['layer']}x{half}_{name}")

        psT = ctx.enter_context(nc.psum_tensor(f"{g['layer']}x{half}_turned", [P, 2, S], F32))
        psY = ctx.enter_context(nc.psum_tensor(f"{g['layer']}x{half}_results", [P, 2, S], F32))
        xin, xT = sb("xin", [P, RING, D], F32), sb("xT", [P, 2, 2, P], F32)
        y = sb("y", [P, RING, D], F32)
        x_loaded = [sem(f"x_loaded{i}") for i in range(RING)]
        y_stored = [sem(f"y_stored{i}") for i in range(RING)]
        t_ready, t_taken, y_ready, y_taken = sem("t_ready"), sem("t_taken"), sem("y_ready"), sem("y_taken")
        block = ctx.enter_context(nc.Block())
        NB4 = EXPERT_TILES // RING

        def tile_experts(engine, b):
            _, at = nc.values_load_multi_w_load_instructions(te[0:1, bass.ds(b * RING, RING)], engines=[engine], min_val=0,
                                                             max_val=(E - 1) * D)
            return at

        @block.gpsimd
        def _(pool):
            alongside(pool)

        @block.sync
        def _(sp):
            def load(b, r):
                if not (isinstance(b, int) and b == 0):
                    sp.wait_ge(t_ready, b * RING + (r - RING + 1))
                sp.dma_start(xin[:, r, :], xe[bass.ds((b * RING + r) * P, P), :]).then_inc(x_loaded[r], 16)

            def store(b, r):
                sp.wait_ge(y_taken, b * RING + (r + 1))
                sp.dma_start(ye[bass.ds((b * RING + r) * P, P), :], y[:, r, :]).then_inc(y_stored[r], 16)

            for r in range(RING):
                load(0, r)
            with sp.Fori(0, NB4 - 1) as b:
                for r in range(RING):
                    store(b, r)
                    load(b + 1, r)
            for r in range(RING):
                store(NB4 - 1, r)
            for r in range(RING):
                sp.wait_ge(y_stored[r], 16 * NB4)

        @block.tensor
        def _(pe):
            def turn(b, r):
                pe.wait_ge(x_loaded[r], b * 16 + 16)
                n = b * RING + r
                if not (isinstance(n, int) and n < 2):
                    pe.wait_ge(t_taken, n - 1)
                for c in range(2):
                    last = pe.transpose(psT[:, r % 2, c * P:(c + 1) * P], xin[:, r, c * P:(c + 1) * P], g["ident"][:, :])
                last.then_inc(t_ready, 1)

            def expert(b, r, at):
                n = b * RING + r
                pe.wait_ge(t_taken, n + 1)
                if not (isinstance(n, int) and n < 2):
                    pe.wait_ge(y_taken, n - 1)
                for c in range(2):
                    last = pe.matmul(psY[:, r % 2, 0:D], xT[:, r % 2, c, :], we[:, c, bass.ds(at, D)], start=(c == 0), stop=(c == 1))
                last.then_inc(y_ready, 1)

            def ring(b, more):
                at = tile_experts(mybir.EngineType.PE, b)
                for r in range(RING):
                    if r < RING - 1:
                        turn(b, r + 1)
                    elif more:
                        turn(b + 1, 0)
                    expert(b, r, at[r])

            turn(0, 0)
            ring(0, True)
            if NB4 > 2:
                with pe.Fori(1, NB4 - 1) as b:
                    ring(b, True)
            ring(NB4 - 1, False)

        @block.scalar
        def _(act):
            def take(b, r):
                n = b * RING + r
                act.wait_ge(t_ready, n + 1)
                if not (isinstance(n, int) and n < 2):
                    act.wait_ge(y_ready, n - 1)
                act.copy(xT[:, r % 2, :, :].rearrange("p c t -> p (c t)"), psT[:, r % 2, 0:D]).then_inc(t_taken, 1)

            for r in range(RING):
                take(0, r)
            with act.Fori(1, NB4) as b:
                for r in range(RING):
                    take(b, r)

        @block.vector
        def _(dve):
            def result(b, r, at):
                n = b * RING + r
                dve.wait_ge(y_ready, n + 1)
                if not (isinstance(b, int) and b == 0):
                    dve.wait_ge(y_stored[r], b * 16)
                dve.tensor_tensor(y[:, r, :], psY[:, r % 2, 0:D], be[:, bass.ds(at, D)], ALU.add).then_inc(y_taken, 1)

            def ring(b):
                at = tile_experts(mybir.EngineType.DVE, b)
                for r in range(RING):
                    result(b, r, at[r])

            ring(0)
            with dve.Fori(1, NB4) as b:
                ring(b)


def add_results(nc, g, early, gathered_early, collect_late, gathered_late):
    X, XN, weight = g["X"], g["XN"], g["weight"]
    with ExitStack() as ctx:
        st = ctx.enter_context(nc.sbuf_tensor(f"{g['layer']}s_st", [P, 4, 6], F32))
        relu_done, added, bns_done = (nc.alloc_semaphore(f"{g['layer']}s_{n}") for n in ("relu_done", "added", "bns_done"))
        block = ctx.enter_context(nc.Block())

        @block.gpsimd
        def _(pool):
            collect_late(pool, relu_done)

        @block.scalar
        def _(act):
            act.wait_ge(gathered_early, 16 * early)
            for i in range(NT):
                if i >= early:
                    n = i - early
                    act.wait_ge(gathered_late[n % len(gathered_late)], 16 * (n // len(gathered_late) + 1))
                act.activation(XN[:, i, :], XN[:, i, :], ACT.Relu, scale=weight[:, i:i + 1]).then_inc(relu_done, 1)

        @block.vector
        def _(dve):
            for i in range(NT + 2):
                if i < NT:
                    dve.wait_ge(relu_done, i + 1)
                    dve.tensor_tensor(X[:, i, :], X[:, i, :], XN[:, i, :], ALU.add).then_inc(added, 1)
                if 1 <= i <= NT:
                    dve.wait_ge(added, i)
                    dve.bn_stats(st[:, (i - 1) % 4, :], X[:, i - 1, :]).then_inc(bns_done, 1)
                if i >= 2:
                    dve.wait_ge(bns_done, i - 1)
                    dve.bn_aggr(g["MV"][:, i - 2, :], st[:, (i - 2) % 4, :])


def experts_large(nc, g, ins, last_layer):
    X, XN, weight = g["X"], g["XN"], g["weight"]
    FC = F // P
    QT = CAP // P
    with ExitStack() as ctx:
        def sb(name, shape, dt):
            return ctx.enter_context(nc.sbuf_tensor(f"{g['layer']}x_{name}", shape, dt))

        def sem(name):
            return nc.alloc_semaphore(f"{g['layer']}x_{name}")

        psT = ctx.enter_context(nc.psum_tensor(f"{g['layer']}x_turned", [P, 2, S], F32))
        psH = ctx.enter_context(nc.psum_tensor(f"{g['layer']}x_inner", [P, 3, S], F32))
        psY = ctx.enter_context(nc.psum_tensor(f"{g['layer']}x_results", [P, 2, S], F32))
        w1, w2 = sb("w1", [P, 2, 2, F], F32), sb("w2", [P, 2, FC, D], F32)
        xin, xT = sb("xin", [P, 2, QT, D], F32), sb("xT", [P, 2, 2, S], F32)
        hT = sb("hT", [P, FC, S], F32)
        y, st = sb("y", [P, 2, QT, D], F32), sb("st", [P, 4, 6], F32)
        scattered = sem("scattered")
        w_loaded = [sem(f"w_loaded{i}") for i in range(2)]
        x_loaded = [sem(f"x_loaded{i}") for i in range(2)]
        y_stored = [sem(f"y_stored{i}") for i in range(2)]
        t_ready, t_taken = sem("t_ready"), sem("t_taken")
        h_ready, y_ready = sem("h_ready"), sem("y_ready")
        h_even, h_odd = sem("h_even_taken"), sem("h_odd_taken")
        y_taken = sem("y_taken")
        gathered = [sem(f"gathered{i}") for i in range(8)]
        added, bns_done, out_stored = sem("added"), sem("bns_done"), sem("out_stored")
        block = ctx.enter_context(nc.Block())

        @block.gpsimd
        def _(pool):
            dispatch(pool, g, g["cap_xe"], range(HALF_TILES, NT), scattered)
            for p in range(2):
                pool.wait_ge(y_stored[p], 16 * (E // 2))
            collect(pool, g, g["cap_ye"], range(NT), gathered, added)

        @block.sync
        def _(sp):
            def weights(e, p):
                sp.dma_start(w1[:, p, :, :], ins["w1"][e]).then_inc(w_loaded[p], 16)
                sp.dma_start(w2[:, p, :, :], ins["w2"][e]).then_inc(w_loaded[p], 16)

            def tokens(e, p):
                sp.dma_start(xin[:, p, :, :], g["cap_xe"][bass.ds(e * CAP, CAP), :].rearrange("(q p) d -> p q d", p=P)).then_inc(
                    x_loaded[p], 16)

            def store(e, p):
                sp.wait_ge(y_taken, e * QT + QT)
                sp.dma_start(g["cap_ye"][bass.ds(e * CAP, CAP), :].rearrange("(q p) d -> p q d", p=P), y[:, p, :, :]).then_inc(
                    y_stored[p], 16)

            for p in range(2):
                weights(p, p)
            sp.wait_ge(scattered, 16 * HALF_TILES)
            for p in range(2):
                tokens(p, p)
            with sp.Fori(0, E // 2 - 1) as j:
                for p in range(2):
                    e = j * 2 + p
                    store(e, p)
                    weights(e + 2, p)
                    tokens(e + 2, p)
            for p in range(2):
                store(E - 2 + p, p)
            for p in range(2):
                sp.wait_ge(y_stored[p], 16 * (E // 2))
            if last_layer:
                for q in range(NB):
                    sp.wait_ge(added, 4 * q + 4)
                    sp.dma_start(ins["out"][q], X[:, 4 * q:4 * q + 4, :]).then_inc(out_stored, 16)
                sp.wait_ge(out_stored, 16 * NB)

        @block.tensor
        def _(pe):
            def turn(j, p):
                pe.wait_ge(x_loaded[p], j * 16 + 16)
                n = j * 2 + p
                for c in range(2):
                    if not (isinstance(n, int) and n == 0):
                        pe.wait_ge(t_taken, n * 2 + (c - 1))
                    for t in range(QT):
                        last = pe.transpose(psT[:, c, t * P:(t + 1) * P], xin[:, p, t, c * P:(c + 1) * P], g["ident"][:, :])
                    last.then_inc(t_ready, 1)

            def inner(j, p):
                n = j * 2 + p
                pe.wait_ge(w_loaded[p], j * 32 + 32)
                pe.wait_ge(t_taken, n * 2 + 2)
                for f in range(FC):
                    if not (isinstance(n, int) and n == 0 and f < 2):
                        pe.wait_ge(h_even if f % 2 == 0 else h_odd, n * (FC // 2) + f // 2)
                    for c in range(2):
                        last = pe.matmul(psH[:, f % 2, :], w1[:, p, c, f * P:(f + 1) * P], xT[:, p, c, :],
                                         start=(c == 0), stop=(c == 1))
                    last.then_inc(h_ready, 1)

            def outer(j, p):
                n = j * 2 + p
                pe.wait_ge(h_even, n * (FC // 2) + FC // 2)
                pe.wait_ge(h_odd, n * (FC // 2) + FC // 2)
                for t in range(QT):
                    if not (isinstance(n, int) and n == 0 and t < 2):
                        pe.wait_ge(y_taken, n * QT + (t - 1))
                    for f in range(FC):
                        last = pe.matmul(psY[:, t % 2, 0:D], hT[:, f, t * P:(t + 1) * P], w2[:, p, f, :],
                                         start=(f == 0), stop=(f == FC - 1))
                    last.then_inc(y_ready, 1)

            turn(0, 0)

            def pair(j, more):
                inner(j, 0)
                turn(j, 1)
                outer(j, 0)
                inner(j, 1)
                if more:
                    turn(j + 1, 0)
                outer(j, 1)

            pair(0, True)
            with pe.Fori(1, E // 2 - 1) as j:
                pair(j, True)
            pair(E // 2 - 1, False)

        @block.scalar
        def _(act):
            def take(j, p):
                n = j * 2 + p
                for c in range(2):
                    act.wait_ge(t_ready, n * 2 + (c + 1))
                    act.copy(xT[:, p, c, :], psT[:, c, :]).then_inc(t_taken, 1)

            def relus(j, p):
                n = j * 2 + p
                for f in range(0, FC, 2):
                    act.wait_ge(h_ready, n * FC + (f + 1))
                    if not (isinstance(n, int) and n == 0):
                        act.wait_ge(y_ready, n * QT)
                    act.activation(hT[:, f, :], psH[:, f % 2, :], ACT.Relu).then_inc(h_even, 1)

            take(0, 0)

            def pair(j, more):
                relus(j, 0)
                take(j, 1)
                relus(j, 1)
                if more:
                    take(j + 1, 0)

            pair(0, True)
            with act.Fori(1, E // 2 - 1) as j:
                pair(j, True)
            pair(E // 2 - 1, False)

        @block.vector
        def _(dve):
            def relus(j, p):
                n = j * 2 + p
                for f in range(1, FC, 2):
                    dve.wait_ge(h_ready, n * FC + (f + 1))
                    if not (isinstance(n, int) and n == 0):
                        dve.wait_ge(y_ready, n * QT)
                    dve.tensor_scalar(hT[:, f, :], psH[:, f % 2, :], 0.0, None, ALU.max).then_inc(h_odd, 1)

            def results(j, p):
                n = j * 2 + p
                for t in range(QT):
                    dve.wait_ge(y_ready, n * QT + (t + 1))
                    if t == 0 and not (isinstance(j, int) and j == 0):
                        dve.wait_ge(y_stored[p], j * 16)
                    dve.tensor_copy(y[:, p, t, :], psY[:, t % 2, 0:D]).then_inc(y_taken, 1)

            def pair(j):
                for p in range(2):
                    relus(j, p)
                    results(j, p)

            pair(0)
            with dve.Fori(1, E // 2) as j:
                pair(j)
            for i in range(NT + 2):
                if i < NT:
                    dve.wait_ge(gathered[i % 8], 16 * (i // 8 + 1))
                    dve.scalar_tensor_tensor(X[:, i, :], XN[:, i, :], weight[:, i:i + 1], X[:, i, :], ALU.mult,
                                             ALU.add).then_inc(added, 1)
                if 1 <= i <= NT and not last_layer:
                    dve.wait_ge(added, i)
                    dve.bn_stats(st[:, (i - 1) % 4, :], X[:, i - 1, :]).then_inc(bns_done, 1)
                if i >= 2 and not last_layer:
                    dve.wait_ge(bns_done, i - 1)
                    dve.bn_aggr(g["MV"][:, i - 2, :], st[:, (i - 2) % 4, :])


CON = [("up8", E), ("down8", E), ("ones8", E), ("resets", E * HALF_TILES), ("tiles", EXPERT_TILES)]
CON_WIDTH = sum(n for _, n in CON)


def global_tensors(nc, ctx):
    def sb(name, shape, dt):
        return ctx.enter_context(nc.sbuf_tensor(name, shape, dt))

    g = {"X": sb("X", [P, NT, D], F32), "MV": sb("MV", [P, NT, 2], F32), "RSTD": sb("RSTD", [P, 2, NT], F32),
         "ident": sb("ident_sb", [P, P], F32), "identb": sb("identb", [P, P], BF16), "eps": sb("eps", [P, 1], F32),
         "before": sb("before", [P, P], BF16), "ones": sb("ones", [P, P], BF16),
         "con_sb": sb("con_sb", [P, CON_WIDTH], F32),
         "cleared": nc.alloc_semaphore("cleared"),
         "xe": [nc.dram_tensor(f"dispatched{h}", [HALF_SLOTS, D], F32, kind="Internal").ap() for h in range(2)],
         "ye": [nc.dram_tensor(f"results{h}", [HALF_SLOTS, D], F32, kind="Internal").ap() for h in range(2)],
         "cap_xe": nc.dram_tensor("cap_dispatched", [CAP_SLOTS, D], F32, kind="Internal").ap(),
         "cap_ye": nc.dram_tensor("cap_results", [CAP_SLOTS + 1, D], F32, kind="Internal").ap()}
    at, g["con"] = 0, {}
    for name, n in CON:
        g["con"][name] = g["con_sb"][:, at:at + n]
        at += n
    return g


def clears(g, zeros):
    def clear(xe):
        n = xe.shape[0] // P
        return lambda eng: eng.dma_start(xe.rearrange("(a p) d -> p a d", p=P),
                                         zeros.unsqueeze(1).to_broadcast([P, n, D])).then_inc(g["cleared"], 16)

    def clear_row(eng):
        eng.dma_start(g["cap_ye"][ZERO_ROW:ZERO_ROW + 1, :], zeros[0:1, :]).then_inc(g["cleared"], 16)

    return [clear(g["xe"][0]), clear(g["xe"][1]), clear(g["cap_xe"]), clear_row]


def routed_layer(nc, g, ins, capacity, last_layer=False):
    with ExitStack() as ctx:
        def sb(name, shape, dt):
            return ctx.enter_context(nc.sbuf_tensor(f"{g['layer']}_{name}", shape, dt))

        g = dict(g, XN=sb("XN", [P, NT, D], F32), slot=sb("slot", [P, NT], I32), back=sb("back", [P, NT], I32),
                 weight=sb("weight", [P, NT], F32), te=[None, None],
                 wg=sb("wg", [P, 2, E if capacity else D], F32), bg=None if capacity else sb("bg", [P, D], F32),
                 nmr=None if capacity else sb("nmr", [P, NT], F32),
                 gate_loaded=nc.alloc_semaphore(f"{g['layer']}_gate_loaded"))
        scattered = [nc.alloc_semaphore(f"{g['layer']}_scattered{h}") for h in range(2)]
        first, second = range(HALF_TILES), range(HALF_TILES, NT)
        if capacity:
            g["carry"] = sb("carry", [P, E], F32)

            def dispatch_capped(pool):
                pool.wait_ge(g["cleared"], 16 * CLEARS)
                dispatch(pool, g, g["cap_xe"], first, scattered[0])
                pool.wait_ge(scattered[0], 16 * HALF_TILES)

            routing(nc, g, ins, True, 0)
            routing(nc, g, ins, True, 1, dispatch_capped)
            experts_large(nc, g, ins, last_layer)
            return
        g.update(te=[sb(f"te{h}", [P, EXPERT_TILES], I32) for h in range(2)], we=sb("we", [P, 2, E * D], F32),
                 be=sb("be", [P, E * D], F32))
        loaded = nc.alloc_semaphore(f"{g['layer']}_weights_loaded")
        gathered_early = nc.alloc_semaphore(f"{g['layer']}_gathered_early")
        gathered = [nc.alloc_semaphore(f"{g['layer']}_gathered{i}") for i in range(8)]

        def load_weights(pool):
            pool.dma_start(g["we"][:, :, :], ins["we"]).then_inc(loaded, 16)
            pool.dma_start(g["be"][:, :], ins["be"]).then_inc(loaded, 16)

        def dispatch_first(pool):
            pool.wait_ge(loaded, 32)
            pool.wait_ge(g["cleared"], 16 * CLEARS)
            dispatch(pool, g, g["xe"][0], first, scattered[0])
            pool.wait_ge(scattered[0], 16 * HALF_TILES)

        def dispatch_second(pool):
            dispatch(pool, g, g["xe"][1], second, scattered[1])
            pool.wait_ge(scattered[1], 16 * HALF_TILES)

        routing(nc, g, ins, False, 0, load_weights)
        routing(nc, g, ins, False, 1, dispatch_first)
        experts_small(nc, g, 0, dispatch_second)
        experts_small(nc, g, 1, lambda pool: collect(pool, g, g["ye"][0], first, [gathered_early]))
        add_results(nc, g, HALF_TILES, gathered_early, 
                    lambda pool, taken: collect(pool, g, g["ye"][1], second, gathered, taken, HALF_TILES), gathered)


def shape_constants():
    rows = {"up8": np.arange(E), "down8": E - np.arange(E), "ones8": np.ones(E),
            "resets": (np.arange(E * HALF_TILES) % HALF_TILES != 0),
            "tiles": np.arange(EXPERT_TILES)}
    row = np.concatenate([rows[n] for n, _ in CON]).astype(np.float32)
    return np.ascontiguousarray(np.broadcast_to(row, (P, CON_WIDTH)))
DL = 64
FOLDED = {"a_wk": [P, 2, D], "a_wv": [P, 2, D], "c_wg": [P, 2, D], "c_wv": [P, 2, D], "d_wk": [P, 2, D],
          "d_wv": [P, 2, D], "d_kb": [P, 2], "d_xb": [P, D]}


def prepare(nc, g, w, folded):
    SHAPES = {"wkT": [P, 2, D], "wvT": [P, 2, D], "wdown": [P, 2, DL], "upk": [DL, D], "upv": [DL, D],
              "cq": [P, 2, D], "ck": [P, 2, D], "cv": [P, 2, D], "coT": [P, 2, D],
              "dkT": [P, D], "dvT": [P, D], "uk": [P, D], "uv": [P, D], 
              "bdk": [P, 1], "bdv": [P, 1], "buk": [P, 2], "buv": [P, 2], "dwo": [P, 2, D], "bo": [P, D]}
    BANKS = ["a_wk", "a_wv", "c_wg", "c_wv", "d_wk", "d_wv"]
    with ExitStack() as ctx:
        X, MV = g["X"], g["MV"]
        before = ctx.enter_context(nc.sbuf_tensor("before_f", [P, P], F32))
        st = ctx.enter_context(nc.sbuf_tensor("st", [P, NT, 6], F32))
        t = {n: ctx.enter_context(nc.sbuf_tensor(f"fold_{n}", s, F32)) for n, s in SHAPES.items() if n in w}
        lat = ctx.enter_context(nc.sbuf_tensor("fold_lat", [DL, D], F32))
        res = ctx.enter_context(nc.sbuf_tensor("fold_res", [P, len(BANKS), 2 * D], F32))
        kb = ctx.enter_context(nc.sbuf_tensor("fold_kb", [P, 2], F32))
        vb = ctx.enter_context(nc.sbuf_tensor("fold_vb", [P, 2], F32))
        vbw = ctx.enter_context(nc.sbuf_tensor("fold_vbw", [P, 2, P], F32))
        xb = ctx.enter_context(nc.sbuf_tensor("fold_xb", [P, D], F32))
        psF = ctx.enter_context(nc.psum_tensor("fold_products", [P, 8, S], F32))

        def sem(name):
            return nc.alloc_semaphore(f"fold_{name}")

        loaded = {n: sem(f"{n}_loaded") for n in ("a", "c", "d")}
        lat_ready, lat_taken = sem("lat_ready"), sem("lat_taken")
        bias_ready, bias_done, xb_ready = sem("bias_ready"), sem("bias_done"), sem("xb_ready")
        ready, taken, stored = sem("ready"), sem("taken"), sem("stored")
        x_loaded = [sem(f"x_loaded{q}") for q in range(NB)]
        con_loaded, bns_done = sem("con_loaded"), sem("bns_done")
        groups = {"a": ["wkT", "wvT", "wdown", "upk", "upv"], "c": ["cq", "ck", "cv", "coT"],
                  "d": ["dkT", "dvT", "uk", "uv", "bdk", "bdv", "buk", "buv", "dwo", "bo"]}
        block = ctx.enter_context(nc.Block())

        @block.sync
        def _(sp):
            def load_tokens(batches):
                for q in batches:
                    sp.dma_start(X[:, 4 * q:4 * q + 4, :], w["x"][q]).then_inc(x_loaded[q], 16)

            for (grp, names), batches in zip(groups.items(), (range(2), range(2, 5), range(5, NB))):
                for n in names:
                    sp.dma_start(t[n][tuple(slice(None) for _ in SHAPES[n])], w[n]).then_inc(loaded[grp], 16)
                load_tokens(batches)
            sp.dma_start(g["ident"][:, :], w["ident"]).then_inc(con_loaded, 16)
            sp.dma_start(before[:, :], w["before"]).then_inc(con_loaded, 16)
            sp.dma_start(g["con_sb"][:, :], w["con"]).then_inc(con_loaded, 16)
            for i, n in enumerate(BANKS):
                sp.wait_ge(taken, i + 1)
                sp.dma_start(folded[n].rearrange("p c d -> p (c d)"), res[:, i, :]).then_inc(stored, 16)
            sp.wait_ge(bias_done, 2)
            sp.dma_start(folded["d_kb"], kb[:, :]).then_inc(stored, 16)
            sp.wait_ge(bias_done, 4)
            sp.dma_start(folded["d_xb"], xb[:, :]).then_inc(stored, 16)
            sp.wait_ge(stored, 16 * (len(BANKS) + 2))

        @block.tensor
        def _(pe):
            pe.wait_ge(loaded["a"], 16 * len(groups["a"]))
            for i, n in enumerate(("wkT", "wvT")):
                for c in range(2):
                    last = pe.matmul(psF[0:DL, 0, 0:D], t["wdown"][:, c, :], t[n][:, c, :], start=(i + c == 0),
                                     stop=(i + c == 2))
            last.then_inc(lat_ready, 1)
            pe.wait_ge(lat_taken, 1)
            for bank, n in ((1, "upk"), (2, "upv")):
                for m in range(2):
                    last = pe.matmul(psF[:, bank, m * D:(m + 1) * D], lat[:, m * P:(m + 1) * P], t[n][:, :],
                                     start=True, stop=True)
                last.then_inc(ready, 1)
            pe.wait_ge(loaded["c"], 16 * len(groups["c"]))
            for bank, a, b in ((3, "cq", "ck"), (4, "cv", "coT")):
                for m in range(2):
                    for c in range(2):
                        last = pe.matmul(psF[:, bank, m * D:(m + 1) * D], t[a][:, c, m * P:(m + 1) * P], t[b][:, c, :],
                                         start=(c == 0), stop=(c == 1))
                last.then_inc(ready, 1)
            pe.wait_ge(loaded["d"], 16 * len(groups["d"]))
            for bank, a, b in ((5, "dkT", "uk"), (6, "dvT", "uv")):
                for m in range(2):
                    last = pe.matmul(psF[:, bank, m * D:(m + 1) * D], t[a][:, m * P:(m + 1) * P], t[b][:, :],
                                     start=True, stop=True)
                last.then_inc(ready, 1)
            for i, (up, b) in enumerate((("uk", "bdk"), ("uv", "bdv"))):
                for m in range(2):
                    last = pe.matmul(psF[:, 0, 2 * i + m:2 * i + m + 1], t[up][:, m * P:(m + 1) * P], t[b][:, :],
                                     start=True, stop=True)
            last.then_inc(bias_ready, 1)
            pe.wait_ge(bias_done, 3)
            for m in range(2):
                last = pe.matmul(psF[:, 7, 0:D], vbw[:, m, :], t["dwo"][:, m, :], start=(m == 0), stop=(m == 1))
            last.then_inc(xb_ready, 1)

        @block.scalar
        def _(act):
            act.wait_ge(lat_ready, 1)
            act.copy(lat[:, :], psF[0:DL, 0, 0:D]).then_inc(lat_taken, 1)
            for i in range(len(BANKS)):
                act.wait_ge(ready, i + 1)
                act.copy(res[:, i, :], psF[:, i + 1, :]).then_inc(taken, 1)

        @block.gpsimd
        def _(pool):
            pool.memset(g["eps"][:, :], EPS)
            pool.memset(g["ones"][:, :], 1.0)

        @block.vector
        def _(dve):
            for q in range(NB):
                dve.wait_ge(x_loaded[q], 16)
                for i in range(4 * q, 4 * q + 4):
                    dve.bn_stats(st[:, i, :], X[:, i, :]).then_inc(bns_done, 1)
            dve.wait_ge(bns_done, NT)
            for i in range(NT):
                dve.bn_aggr(MV[:, i, :], st[:, i, :])
            dve.wait_ge(bias_ready, 1)
            dve.tensor_tensor(vb[:, :], psF[:, 0, 2:4], t["buv"][:, :], ALU.add).then_inc(bias_done, 1)
            dve.tensor_tensor(kb[:, :], psF[:, 0, 0:2], t["buk"][:, :], ALU.add).then_inc(bias_done, 1)
            dve.wait_ge(bias_done, 2)
            dve.tensor_copy(vbw[:, :, :], vb[:, :].unsqueeze(2).to_broadcast([P, 2, P])).then_inc(bias_done, 1)
            dve.wait_ge(xb_ready, 1)
            dve.tensor_tensor(xb[:, :], psF[:, 7, 0:D], t["bo"][:, :], ALU.add).then_inc(bias_done, 1)
            dve.wait_ge(con_loaded, 48)
            dve.tensor_copy(g["identb"][:, :], g["ident"][:, :])
            dve.tensor_copy(g["before"][:, :], before[:, :])


def mha_layer(nc, g, ins, decay, scale, project_q, biased, aside=()):
    X, MV, RSTD = g["X"], g["MV"], g["RSTD"]
    ident, identb = g["ident"], g["identb"]
    NV = 2 if decay else 1
    NCH = 4 * NV
    NAG = 16
    if decay:
        MAXIMA_SPAN = [(-20, -9), (-22, -13), (-20, -9), (-21, -11)]
        SPLIT_BEFORE, PV_AT, THIRD_AT = -9, 3, 1
        USES = [(6, "OT3"), (7, "xT0"), (8, "xT1"), (10, "mT1"), (11, "aT0"), (12, "k0"), (13, "k1"), (15, "aT1"),
                (16, "q0"), (19, "q1"), (21, "OT0"), (23, "Wo0"), (23, "Wo1"), (24, "v0"), (26, "mT2"), (28, "v1"),
                (40, "OT1"), (41, "mT3"), (54, "OT2"), (58, "mT0")]
        ROTATE_AT, FIRST_AT = [12, 13, 16, 17, 20, 21, 24, 25], [13, 14, 17, 18, 20, 21, 25, 26]
        MIDDLE_AT = [15, 16, 19, 20, 21, 24, 28, 28]
    elif project_q:
        MAXIMA_SPAN = [(-20, -9), (-24, -9), (-24, -12), (-21, -8)]
        SPLIT_BEFORE, PV_AT, THIRD_AT = -8, 2, 1
        USES = [(4, "OT3"), (5, "xT0"), (6, "xT1"), (7, "aT0"), (8, "k0"), (10, "mT1"), (12, "k1"), (13, "aT1"),
                (14, "q0"), (16, "Wo0"), (17, "q1"), (19, "Wo1"), (20, "OT0"), (25, "v0"), (26, "mT2"), (28, "v1"),
                (36, "OT1"), (42, "mT3"), (55, "OT2"), (58, "mT0")]
        ROTATE_AT, FIRST_AT = [10, 13, 17, 24], [15, 19, 25, 27]
        MIDDLE_AT = [17, 20, 28, 29]
    else:
        MAXIMA_SPAN = [(-20, -9), (-24, -9), (-24, -11), (-21, -9)]
        SPLIT_BEFORE, PV_AT, THIRD_AT = -9, 2, 2
        USES = [(4, "OT3"), (5, "xT0"), (6, "xT1"), (7, "aT0"), (8, "k0"), (10, "mT1"), (11, "k1"), (13, "aT1"),
                (16, "Wo0"), (19, "Wo1"), (20, "OT0"), (25, "v0"), (26, "mT2"), (28, "v1"), (36, "OT1"), (42, "mT3"),
                (55, "OT2"), (57, "mT0")]
        ROTATE_AT, FIRST_AT = [10, 13, 19, 24], [15, 19, 25, 27]
        MIDDLE_AT = [17, 20, 29, 30]
    A_AT = [[first + (last - first) * a // 15 for a in range(NAG)] for first, last in MAXIMA_SPAN]
    SPLIT_AT = [[SPLIT_BEFORE]] * 4
    ASIDE_FROM = 32
    A_RING = 2 if decay else 3
    A_BANK = [a % A_RING for a in range(63)] + [1]
    A_LAST = [max(i for i in range(-64, a) if A_BANK[i % 64] == A_BANK[a]) for a in range(64)]
    ROW_DMAS = 3 * NV
    PSLOTS = 4 if decay else 2
    XN = 4 if project_q else 8
    KQ = ["k0", "k1"] + (["q0", "q1"] if project_q else [])
    PRO = ["xT0", "xT1"] + KQ + ["v0", "v1"]
    PREV = ["OT3", "aT0", "aT1", "Wo0", "Wo1"]
    assert USES == sorted(USES) and {n for _, n in USES} == {*PRO, *PREV, "OT0", "OT1", "OT2", "mT0", "mT1", "mT2", "mT3"}
    MID = [n for _, n in USES]
    ORDER = {"pre": PRO + ["mT0"], "first": [n for n in MID if n not in PREV], "mid": MID,
             "last": [n for n in MID if n not in PRO + ["mT0"]], "post": PREV}
    BY_ACT = PRO + ["mT0", "mT1", "mT2", "mT3", "aT0", "aT1"]
    CHAINS = [(o, c, v) for o in "kq" for c in range(2) for v in range(NV)]

    def base(tag, b):
        if tag == "pre":
            return 0
        if tag == "first":
            return len(ORDER["pre"])
        if tag == "post":
            return base("last", NB - 1) + len(ORDER["last"])
        return (b - 1) * len(MID) + (len(ORDER["pre"]) + len(ORDER["first"]))

    def use(tag, b, name):
        return base(tag, b) + ORDER[tag].index(name)

    def bank(tag, b, name):
        return use(tag, 1 if tag == "mid" else b, name) % 2

    def emptied(tag, b, name):
        if tag != "mid":
            return use(tag, b, name) // 2 + 1
        return (b - 1) * (len(MID) // 2) + (use(tag, 1, name) // 2 + 1)

    def groups(s, tag, at):
        return [(g // 4, g % 4, a) for g in range(6) for a in range(len(at[g % 4])) if 16 * g + at[g % 4][a] == s
                and not (tag == "last" and g > 3)]

    with ExitStack() as ctx:
        def sb(name, shape, dt):
            return ctx.enter_context(nc.sbuf_tensor(f"{g['layer']}_{name}", shape, dt))

        def sem(name):
            return nc.alloc_semaphore(f"{g['layer']}_{name}")

        psA = ctx.enter_context(nc.psum_tensor(f"{g['layer']}_scores_q", [P, 3, S], F32))
        psB = ctx.enter_context(nc.psum_tensor(f"{g['layer']}_scores_k", [P, 2, S], F32))
        psO = ctx.enter_context(nc.psum_tensor(f"{g['layer']}_out_heads", [P, S], F32))
        psM = ctx.enter_context(nc.psum_tensor(f"{g['layer']}_work", [P, 2, S], F32))

        wk, wv, wo = (sb(n, [P, 2, D], F32) for n in ("wk", "wv", "wo"))
        wq = sb("wq", [P, 2, D], F32) if project_q else None
        xn, xnT = sb("xn", [P, 4, D], F32), sb("xnT", [P, 2, S], F32)
        f, fc = sb("f", [P, 2, S], F32), sb("fc", [P, 2, S], F32)
        rr = sb("rr", [P, 2, S], F32)
        parts = sb("parts", [P, 2, 3, S], BF16)
        QS = sb("QS", [99, NV, 2, 8, S], BF16)
        KS = sb("KS", [99, NV, 2, 8, S], BF16)
        probs = sb("probs", [P, PSLOTS, 4, S], F32)
        Vraw, Vaug = sb("Vraw", [P, 4, D], F32), sb("Vaug", [P, 4, H, 32], F32)
        mx, mr = sb("mx", [P, 2, 4, 4], F32), sb("mr", [P, 4, 4], F32)
        mp, mT = sb("mp", [P, 4, 3, 4], BF16), sb("mT", [12, S], BF16)
        Osb, warm = sb("Osb", [P, S], F32), sb("warm", [P, 1], F32)
        rec = sb("rec", [P, 4, 4, 4], F32)
        attn, attnT = sb("attn", [P, 4, D], F32), sb("attnT", [P, 2, S], F32)
        st, mv = sb("st", [P, 2, 6], F32), sb("mv", [P, 2, 2], F32)
        if decay:
            tab = sb("tab", [P, 2, S], F32)
            corr = sb("corr", [P, 4, S], F32)
            low = sb("low", [P, 2, 4, P], F32)
            junk = sb("junk", [P, 2, S], BF16)
        else:
            tab = sb("tab", [P, 2, S], F32)
            sh = sb("sh", [P, 2, S], F32)
        if biased:
            kb = sb("kb", [P, 2], F32)
            xb = sb("xb", [P, D], F32)
        scr = nc.dram_tensor(f"{g['layer']}_parts_dram", [2, NV, 2, 3, P, S], BF16, kind="Internal").ap()

        loaded_by = {name: sem(f"{name}_loaded") for name, _ in ins["load"]}
        loaded = loaded_by["wk"]
        folded = sem("folded")
        ones_set = sem("ones_set")
        root, rstd_done = sem("root"), sem("rstd_done")
        xn_ready = sem("xn_ready")
        xbias_done = sem("xbias_done")
        m_ready = sem("work_ready")
        m_taken = [sem(f"work_taken{i}") for i in range(2)]
        rot_done, sin_done, sum_done = sem("rot_done"), sem("sin_done"), sem("sum_done")
        p0_done, r1_done, p1_done, p2_done = (sem(n) for n in ("p0_done", "r1_done", "p1_done", "p2_done"))
        scr_written = [sem(f"scr_written{i}") for i in range(2)]
        half_loaded = [sem(f"half_loaded{i}") for i in range(2)]
        a_ready, a_done = sem("a_ready"), sem("a_done")
        ms_done = sem("max_split")
        rows_loaded = sem("rows_loaded")
        b_ready, exp_done = sem("b_ready"), sem("exp_done")
        e_ready, e_exp, sel_done = sem("e_ready"), sem("e_exp"), sem("sel_done")
        vaug_done, pv_done, o_taken = sem("vaug_done"), sem("pv_done"), sem("o_taken")
        rec_done = sem("rec_done")
        bns_done, agg_done = sem("bns_done"), sem("agg_done")
        NLOAD = len(ins["load"])

        tiles = {"wq": wq, "wk": wk, "wv": wv, "wo": wo, "tab": tab}
        if decay:
            tiles["corr"] = corr
        if biased:
            tiles["kb"], tiles["xb"] = kb, xb

        def wait_parts(eng, nb, j):
            cnt = nb * (16 * NCH // 2) + 16 * (j // 2)
            if not (isinstance(cnt, int) and cnt == 0):
                eng.wait_ge(scr_written[j % 2], cnt)

        def rotary_sums(eng, nb, pair):
            for j in (pair, pair + 1) if not decay else ():
                eng.wait_ge(rot_done, nb * 8 + (2 * j + 2))
                eng.tensor_tensor(sh[:, j % 2, :], sh[:, j % 2, :], tab[:, 1, :], ALU.mult).then_inc(sin_done, 1)
                eng.wait_ge(sin_done, nb * NCH + (j + 1))
                eng.tensor_tensor(fc[:, j % 2, :], fc[:, j % 2, :], sh[:, j % 2, :], ALU.add).then_inc(sum_done, 1)

        def leave_first(eng, nb, pair):
            for j in (pair, pair + 1):
                eng.wait_ge(p0_done, nb * NCH + (j + 1))
                eng.tensor_tensor(rr[:, j % 2, :], fc[:, j % 2, :], parts[:, j % 2, 0, :], ALU.subtract).then_inc(r1_done, 1)

        def leave_second(eng, nb, pair):
            for j in (pair, pair + 1):
                eng.wait_ge(p1_done, nb * NCH + (j + 1))
                eng.tensor_tensor(parts[:, j % 2, 2, :], rr[:, j % 2, :], parts[:, j % 2, 1, :],
                                  ALU.subtract).then_inc(p2_done, 1)

        block = ctx.enter_context(nc.Block())

        @block.sync
        def _(sp):
            for name, src in ins["load"]:
                sp.dma_start(tiles[name][:], src).then_inc(loaded_by[name], 16)

            def write_parts(nb, j):
                o, c, v = CHAINS[j]
                sp.wait_ge(p2_done, nb * NCH + (j + 1))
                sp.dma_start(scr["kq".index(o), v, c].rearrange("s p t -> p s t"), parts[:, j % 2, :, :]).then_inc(
                    scr_written[j % 2], 16)

            def load_keys(c):
                for v in range(NV):
                    for at, n in ((0, 3), (48, 2), (80, 1)):
                        dst = KS[at:at + 16 * n, v, c, :, :].rearrange("p h t -> p (h t)")
                        src = scr[0, v, c][0:n].rearrange("s (d h) t -> (s d) (h t)", d=16)
                        sp.dma_start(dst, src).then_inc(half_loaded[c], 16)

            def load_queries(c):
                for v in range(NV):
                    for part, (at, n) in enumerate(((0, 3), (48, 2), (80, 1))):
                        dst = QS[at:at + 16 * n, v, c, :, :].rearrange("p h t -> p (h t)")
                        one = scr[1, v, c][part].rearrange("(d h) t -> d (h t)", d=16)
                        src = bass.AP(one.tensor, one.offset, [[0, n]] + [list(x) for x in one.ap])
                        sp.dma_start(dst, src if n > 1 else one).then_inc(half_loaded[c], 16)

            def load_half(nb, c):
                for n in range(2):
                    sp.wait_ge(scr_written[n], (nb + 1) * (16 * NCH // 2))
                load_keys(c)
                load_queries(c)

            def max_rows(tag, b, nb, grp):
                sp.wait_ge(m_taken[bank(tag, b, f"mT{grp}")], emptied(tag, b, f"mT{grp}"))
                c, h0 = grp // 2, 4 * (grp % 2)
                for v in range(NV):
                    for s in range(3):
                        sp.dma_start(QS[96 + s:97 + s, v, c, h0:h0 + 4, :], mT[4 * s:4 * s + 4, :]).then_inc(
                            rows_loaded, 16)

            for j in range(NCH // 2):
                write_parts(0, j)
            for n in range(2):
                sp.wait_ge(scr_written[n], 16 * NCH // 4)
            load_keys(0)
            for j in range(NCH // 2, NCH):
                write_parts(0, j)
            for n in range(2):
                sp.wait_ge(scr_written[n], 16 * NCH // 2)
            load_queries(0)
            max_rows("pre", 0, 0, 0)

            def body(tag, b):
                if tag != "first":
                    sp.wait_ge(b_ready, apart(sp, b * 64, loaded))
                    if decay:
                        sp.wait_ge(e_ready, b * 16)
                load_half(b, 1)
                if tag == "last":
                    for grp in (1, 2, 3):
                        max_rows(tag, b, b, grp)
                    return
                max_rows(tag, b, b, 1)
                for c in range(2):
                    sp.wait_ge(half_loaded[c], (b + 1) * (16 * 6 * NV))
                cut = 6 if decay else 2
                for j in range(cut):
                    write_parts(b + 1, j)
                max_rows(tag, b, b, 2)
                for j in range(cut, NCH):
                    write_parts(b + 1, j)
                sp.wait_ge(b_ready, apart(sp, b * 64 + 32, loaded))
                if decay:
                    sp.wait_ge(e_ready, b * 16 + 8)
                load_half(b + 1, 0)
                max_rows(tag, b, b, 3)
                max_rows(tag, b, b + 1, 0)

            body("first", 0)
            with sp.Fori(1, NB - 1) as b:
                body("mid", b)
            body("last", NB - 1)

        @block.tensor
        def _(pe):
            def work(tag, b, nb, name):
                m, before = bank(tag, b, name), emptied(tag, b, name) - 1
                if not (isinstance(before, int) and before == 0):
                    pe.wait_ge(m_taken[m], before)
                kind, n = name[:-1], int(name[-1])
                if name in ("k0", "aT0", "Wo0"):
                    first, second = {"k0": ("xT0", "xT1"), "aT0": ("OT3", "OT3"), "Wo0": ("aT0", "aT1")}[name]
                    if bank(tag, b, first) not in (m, bank(tag, b, second)):
                        pe.wait_ge(m_taken[bank(tag, b, first)], emptied(tag, b, first))
                    if bank(tag, b, second) != m:
                        pe.wait_ge(m_taken[bank(tag, b, second)], emptied(tag, b, second))
                if kind == "xT":
                    pe.wait_ge(xn_ready, (nb + 1) * XN)
                    for t in range(4):
                        src = xn[:, t, n * P:(n + 1) * P]
                        last = pe.transpose(psM[:, m, t * P:(t + 1) * P], src, ident[:, :])
                elif kind in "kq":
                    w = wk if kind == "k" else wq
                    for c in range(2):
                        last = pe.matmul(psM[:, m, :], w[:, c, n * P:(n + 1) * P], xnT[:, c, :], start=(c == 0), stop=(c == 1))
                elif kind == "v":
                    for t in range(2):
                        for c in range(2):
                            tok = (2 * n + t) * P
                            last = pe.matmul(psM[:, m, t * D:(t + 1) * D], xnT[:, c, tok:tok + P], wv[:, c, :],
                                             start=(c == 0), stop=(c == 1))
                elif kind == "mT":
                    grp = nb * 4 + n
                    pe.wait_ge(ms_done, grp * 4 + 4)
                    for t in range(4):
                        last = pe.transpose(psM[:, m, :].bitcast(BF16)[0:12, t * P:(t + 1) * P],
                                            mp[:, t, :, :].rearrange("p s h -> p (s h)"), identb[:, :])
                elif kind == "OT":
                    pe.wait_ge(o_taken, nb * 4 + (n + 1))
                    for t in range(4):
                        last = pe.transpose(psM[:, m, t * P:(t + 1) * P], Osb[:, t * P:(t + 1) * P], ident[:, :])
                elif kind == "aT":
                    for t in range(4):
                        last = pe.transpose(psM[:, m, t * P:(t + 1) * P], attn[:, t, n * P:(n + 1) * P], ident[:, :])
                elif kind == "Wo":
                    for t in range(2):
                        for c in range(2):
                            tok = (2 * n + t) * P
                            last = pe.matmul(psM[:, m, t * D:(t + 1) * D], attnT[:, c, tok:tok + P], wo[:, c, :],
                                             start=(c == 0), stop=(c == 1))
                last.then_inc(m_ready, 1)

            def max_scores(nb, grp, a):
                k = grp * NAG + a
                if a == 0:
                    pe.wait_ge(half_loaded[grp // 2], (nb + 1) * (16 * 6 * NV))
                if not (isinstance(nb, int) and nb * 64 + A_LAST[k] < 0):
                    pe.wait_ge(a_done, nb * 64 + (A_LAST[k] + 1))
                c, (qt, h) = grp // 2, divmod(a, 4)
                hh = 4 * (grp % 2) + h
                pe.matmul(psA[:, A_BANK[k], :], QS[0:96, 0, c, hh, qt * P:(qt + 1) * P],
                          KS[0:96, NV - 1, c, hh, :], start=True, stop=True).then_inc(a_ready, 1)

            def exp_scores(b, s):
                grp, kt, h = s // 16, s // 4 % 4, s % 4
                c, hh = grp // 2, 4 * (grp % 2) + h
                if s % 16 == 0:
                    pe.wait_ge(rows_loaded, (b * 4 + (grp + 1)) * (16 * ROW_DMAS))
                if not (isinstance(b, int) and b * 64 + s < 2):
                    pe.wait_ge(exp_done, b * 64 + (s - 1))
                keys = slice(kt * P, (kt + 1) * P)
                if not decay:
                    last = pe.matmul(psB[:, s % 2, :], KS[:, 0, c, hh, keys], QS[:, 0, c, hh, :], start=True, stop=True)
                else:
                    end = (kt + 1) * P
                    last = pe.matmul(psB[:, s % 2, 0:end], KS[:, 1, c, hh, keys], QS[:, 0, c, hh, 0:end],
                                     start=True, stop=True)
                    if end < S:
                        last = pe.matmul(psB[:, s % 2, end:S], KS[:, 0, c, hh, keys], QS[:, 1, c, hh, end:S],
                                         start=True, stop=True)
                last.then_inc(b_ready, 1)
                if decay and h == 3:
                    kk = s // 4
                    if not (isinstance(b, int) and b * 16 + kk < 1):
                        pe.wait_ge(e_exp, b * 16 + kk)
                    for i in range(4):
                        hh = 4 * (grp % 2) + i
                        last = pe.matmul(psA[:, 2, i * P:(i + 1) * P], KS[:, 0, c, hh, keys], QS[:, 1, c, hh, keys],
                                         start=True, stop=True)
                    last.then_inc(e_ready, 1)

            def value_sums(b, kk):
                grp, kt = kk // 4, kk % 4
                if kk == 0:
                    pe.wait_ge(vaug_done, b + 1)
                if kt == 0 and not (isinstance(b, int) and b * 4 + grp < 1):
                    pe.wait_ge(o_taken, b * 4 + grp)
                pe.wait_ge(sel_done if decay else exp_done, (b * 16 + (kk + 1)) * (2 if decay else 4))
                if decay and kt:
                    for h in range(4):
                        pe.matmul(psO[32 * h:32 * h + 32, kt * P:(kt + 1) * P], Vaug[:, kt, 4 * grp + h, :],
                                  low[:, kk % 2, h, :], start=False, stop=False)
                for h in range(4):
                    last = pe.matmul(psO[32 * h:32 * h + 32, :], Vaug[:, kt, 4 * grp + h, :],
                                     probs[:, kk % PSLOTS, h, :], start=(kt == 0), stop=(kt == 3))
                if decay and not kt:
                    for h in range(4):
                        last = pe.matmul(psO[32 * h:32 * h + 32, 0:P], Vaug[:, kt, 4 * grp + h, :],
                                         low[:, kk % 2, h, :], start=False, stop=False)
                last.then_inc(pv_done, 1)

            for name in ORDER["pre"][:-1]:
                if name in ("k0", "q0", "v0"):
                    pe.wait_ge(loaded_by[f"w{name[0]}"], 16)
                work("pre", 0, 0, name)
            for a in range(NAG):
                max_scores(0, 0, a)
            work("pre", 0, 0, "mT0")
            for g in (1, 2):
                for a in range(NAG):
                    if 16 * g + A_AT[g][a] < 0:
                        max_scores(0, g, a)

            pe.wait_ge(ones_set, 1 + NV)
            pe.wait_ge(loaded_by["wo"], 16)

            def body(tag, b):
                for s in range(64):
                    grp, o = divmod(s, 16)
                    exp_scores(b, s)
                    if o % 4 == PV_AT:
                        if s > PV_AT:
                            value_sums(b, s // 4 - 1)
                        elif tag != "first":
                            value_sums(b - 1, 15)
                    for ahead, of, a in groups(s, tag, A_AT):
                        max_scores(b + ahead, of, a)
                    for at, name in USES:
                        if at == s and name in ORDER[tag]:
                            nb = b - 1 if name in PREV else b + 1 if name in PRO + ["mT0"] else b
                            work(tag, b, nb, name)

            body("first", 0)
            with pe.Fori(1, NB - 1) as b:
                body("mid", b)
            body("last", NB - 1)
            value_sums(NB - 1, 15)
            for name in ORDER["post"]:
                work("post", NB, NB - 1, name)

        @block.scalar
        def _(act):
            act.activation(RSTD[:, 1, :], MV[:, :, 1], ACT.Sqrt, bias=g["eps"][:, :]).then_inc(root, 1)
            act.activation(warm[:, :], g["eps"][:, :], ACT.Exp)
            if biased:
                act.wait_ge(loaded_by["kb"], 16)

            def take(tag, b, nb, name):
                act.wait_ge(m_ready, use(tag, b, name) + 1)
                kind, n, m = name[:-1], int(name[-1]), bank(tag, b, name)
                if kind == "xT":
                    if not project_q and not (isinstance(nb, int) and nb == 0):
                        act.wait_ge(rot_done, nb * 8)
                    ins_ = act.copy(xnT[:, n, :], psM[:, m, :])
                elif kind in "kq":
                    u = 2 * (kind == "q") + n
                    cnt = nb * 8 + (2 * u - 2)
                    if not (isinstance(cnt, int) and cnt <= 0):
                        act.wait_ge(rot_done, cnt)
                    if biased:
                        ins_ = act.activation(f[:, n, :], psM[:, m, :], ACT.Identity, bias=kb[:, n:n + 1])
                    else:
                        ins_ = act.copy(f[:, n, :], psM[:, m, :])
                elif kind == "v":
                    if not (isinstance(nb, int) and nb == 0):
                        act.wait_ge(vaug_done, nb)
                    ins_ = act.copy(Vraw[:, 2 * n:2 * n + 2, :].rearrange("p t d -> p (t d)"), psM[:, m, :])
                elif kind == "mT":
                    grp = nb * 4 + n
                    if not (isinstance(grp, int) and grp == 0):
                        act.wait_ge(rows_loaded, grp * (16 * ROW_DMAS))
                    ins_ = act.copy(mT[:, :], psM[:, m, :].bitcast(BF16)[0:12, 0:S])
                else:
                    ins_ = act.copy(attnT[:, n, :], psM[:, m, :])
                ins_.then_inc(m_taken[m], 1)

            def middle_part(nb, j):
                act.wait_ge(r1_done, nb * NCH + (j + 1))
                wait_parts(act, nb, j)
                act.copy(parts[:, j % 2, 1, :], rr[:, j % 2, :]).then_inc(p1_done, 1)

            for name in ORDER["pre"][:2]:
                take("pre", 0, 0, name)
            for i, (o, c, v) in enumerate(CHAINS):
                if v == 0 and f"{o}{c}" in PRO:
                    take("pre", 0, 0, f"{o}{c}")
                if i:
                    middle_part(0, i - 1)
            middle_part(0, NCH - 1)
            for name in ("v0", "v1", "mT0"):
                take("pre", 0, 0, name)

            def take_heads(b, grp):
                act.wait_ge(pv_done, b * 16 + (4 * grp + 4))
                n = b * 4 + grp
                act.copy(Osb[:, :], psO[:, :]).then_inc(o_taken, 1)

            def body(tag, b):
                for s in range(64):
                    grp, o = divmod(s, 16)
                    kk, h = s // 4, s % 4
                    if h == 0 and not (isinstance(b, int) and b * 16 + kk < PSLOTS):
                        act.wait_ge(pv_done, b * 16 + (kk - PSLOTS + 1))
                    act.wait_ge(b_ready, b * 64 + (s + 1))
                    act.activation(probs[:, kk % PSLOTS, h, :], psB[:, s % 2, :], ACT.Exp, scale=scale).then_inc(
                        exp_done, 1)
                    if decay and h == 3:
                        act.wait_ge(e_ready, b * 16 + (kk + 1))
                        if not (isinstance(b, int) and b * 16 + kk < 2):
                            act.wait_ge(pv_done, b * 16 + (kk - 1))
                        act.activation(low[:, kk % 2, :, :].rearrange("p h q -> p (h q)"), psA[:, 2, :], ACT.Exp,
                                       scale=scale).then_inc(e_exp, 1)
                    if o == PV_AT + 1:
                        if grp:
                            take_heads(b, grp - 1)
                        elif tag != "first":
                            take_heads(b - 1, 3)
                    for at, name in USES:
                        if at + 1 == s and name in ORDER[tag] and name in BY_ACT:
                            nb = b - 1 if name in PREV else b + 1 if name in PRO + ["mT0"] else b
                            take(tag, b, nb, name)
                    if tag != "last":
                        for j in range(NCH):
                            if MIDDLE_AT[j] == s:
                                middle_part(b + 1, j)

            body("first", 0)
            with act.Fori(1, NB - 1) as b:
                body("mid", b)
            body("last", NB - 1)
            take_heads(NB - 1, 3)
            for name in ("aT0", "aT1"):
                take("post", NB, NB - 1, name)

        @block.vector
        def _(dve):
            dve.wait_ge(root, 1)
            dve.reciprocal(RSTD[:, 0, :], RSTD[:, 1, :]).then_inc(rstd_done, 1)
            dve.wait_ge(rstd_done, 1)

            def normalise(nb, t):
                i = nb * 4 + t
                if project_q:
                    dve.tensor_scalar(xn[:, t, :], X[:, i, :], MV[:, i, 0:1], RSTD[:, 0, bass.ds(i, 1)],
                                      ALU.subtract, ALU.mult).then_inc(xn_ready, 1)
                    return
                for c in range(2):
                    half = slice(c * P, (c + 1) * P)
                    dve.tensor_scalar(xn[:, t, half].rearrange("p (a y h) -> p h y a", a=8, y=2),
                                      X[:, i, half].rearrange("p (h y a) -> p h y a", y=2, a=8), MV[:, i, 0:1],
                                      RSTD[:, 0, bass.ds(i, 1)], ALU.subtract, ALU.mult).then_inc(xn_ready, 1)

            def rotate(tag, b, nb, j):
                o, c, v = CHAINS[j]
                if project_q or o == "k":
                    of, src = f"{o}{c}", f[:, c, :]
                else:
                    of, src = f"xT{c}", xnT[:, c, :]
                dve.wait_ge(m_taken[bank(tag, b, of)], apart(dve, emptied(tag, b, of), loaded))
                cnt = nb * NCH + (j - 1)
                if not (isinstance(cnt, int) and cnt <= 0):
                    dve.wait_ge(r1_done, apart(dve, cnt, loaded))
                if decay:
                    dve.tensor_tensor(fc[:, j % 2, :], src, tab[:, v, :], ALU.mult).then_inc(rot_done, 1)
                else:
                    dve.stream_shuffle(sh[:, j % 2, :], src, [i ^ 8 for i in range(32)]).then_inc(rot_done, 1)
                    dve.tensor_tensor(fc[:, j % 2, :], src, tab[:, 0, :], ALU.mult).then_inc(rot_done, 1)

            def first_part(nb, j):
                if decay:
                    dve.wait_ge(rot_done, nb * 8 + (j + 1))
                else:
                    dve.wait_ge(sum_done, nb * NCH + (j + 1))
                wait_parts(dve, nb, j)
                dve.tensor_copy(parts[:, j % 2, 0, :], fc[:, j % 2, :]).then_inc(p0_done, 1)

            def maxima(nb, grp, a):
                k = grp * NAG + a
                dve.wait_ge(a_ready, apart(dve, nb * 64 + (k + 1), loaded))
                if a == 0 and not (isinstance(nb, int) and nb * 4 + grp < 2):
                    dve.wait_ge(ms_done, apart(dve, nb * 16 + 4 * (grp - 1), loaded))
                qt, h = divmod(a, 4)
                if decay:
                    if not (isinstance(nb, int) and nb * 64 + k < 2):
                        dve.wait_ge(a_done, apart(dve, nb * 64 + (k - 1), loaded))
                    dve.tensor_tensor_reduce(junk[:, a % 2, :], psA[:, A_BANK[k], :], corr[:, qt, :], 1.0, -3.0e38, ALU.mult,
                                             ALU.max, mx[:, grp % 2, qt, h:h + 1]).then_inc(a_done, 1)
                else:
                    dve.tensor_reduce(mx[:, grp % 2, qt, h:h + 1], psA[:, A_BANK[k], :], AX.X, ALU.max).then_inc(a_done, 1)

            def split_maxima(tag, b, nb, grp):
                n = nb * 4 + grp
                dve.wait_ge(a_done, (n + 1) * NAG)
                if tag != "pre":
                    dve.wait_ge(m_ready, base(tag, b) if grp == 1 else use(tag, b, f"mT{(grp - 1) % 4}") + 1)
                flat = mx[:, grp % 2, :, :]
                dve.tensor_scalar(mp[:, :, 0, :], flat, -1.0, None, ALU.mult).then_inc(ms_done, 1)
                dve.wait_ge(ms_done, n * 4 + 1)
                dve.scalar_tensor_tensor(mr[:, :, :], flat, -1.0, mp[:, :, 0, :], ALU.mult, ALU.subtract).then_inc(
                    ms_done, 1)
                dve.wait_ge(ms_done, n * 4 + 2)
                dve.tensor_copy(mp[:, :, 1, :], mr[:, :, :]).then_inc(ms_done, 1)
                dve.wait_ge(ms_done, n * 4 + 3)
                dve.tensor_tensor(mp[:, :, 2, :], mr[:, :, :], mp[:, :, 1, :], ALU.subtract).then_inc(ms_done, 1)

            def lay_values(tag, b):
                for v in ("v0", "v1"):
                    if tag == "first":
                        dve.wait_ge(m_taken[bank("pre", 0, v)], emptied("pre", 0, v))
                    else:
                        dve.wait_ge(m_taken[bank("mid", 1, v)],
                                    b * (len(MID) // 2) + (emptied("mid", 1, v) - len(MID)))
                if tag != "first":
                    dve.wait_ge(pv_done, b * 16)
                dve.tensor_copy(Vaug[:, :, :, 0:16], Vraw[:, :, :].rearrange("p t (h d) -> p t h d", d=16)).then_inc(
                    vaug_done, 1)

            def normalise_heads(tag, b, nb, name):
                n, m = use(tag, b, name), bank(tag, b, name)
                grp = int(name[-1])
                dve.wait_ge(m_ready, n + 1)
                ov = psM[:, m, :].rearrange("p (t h e) -> p t h e", t=4, h=4)
                dve.reciprocal(rec[:, grp, :, :], ov[:, :, :, 16]).then_inc(rec_done, 1)
                dve.wait_ge(rec_done, nb * 4 + (grp + 1))
                dve.tensor_tensor(attn[:, :, 64 * grp:64 * grp + 64].rearrange("p t (h d) -> p t h d", d=16),
                                  ov[:, :, :, 0:16], rec[:, grp, :, :].unsqueeze(3).to_broadcast([P, 4, 4, 16]),
                                  ALU.mult).then_inc(m_taken[m], 1)

            def add_out(tag, b, nb, name):
                j = int(name[-1])
                n, m = use(tag, b, name), bank(tag, b, name)
                dve.wait_ge(m_ready, n + 1)
                if biased:
                    dve.wait_ge(xbias_done, nb + 1)
                i = nb * 4 + 2 * j
                xs = X[:, bass.ds(i, 2), :]
                dve.tensor_tensor(xs, xs, psM[:, m, :].rearrange("p (t d) -> p t d", t=2), ALU.add).then_inc(m_taken[m], 1)
                dve.wait_ge(m_taken[m], apart(dve, emptied(tag, b, name), loaded))
                for t in range(2):
                    dve.bn_stats(st[:, t, :], X[:, i + t, :]).then_inc(bns_done, 1)
                dve.wait_ge(bns_done, apart(dve, nb * 4 + (2 * j + 2), loaded))
                for t in range(2):
                    dve.bn_aggr(mv[:, t, :], st[:, t, :]).then_inc(agg_done, 1)
                dve.wait_ge(agg_done, nb * 4 + (2 * j + 2))
                dve.tensor_copy(MV[:, bass.ds(i, 2), :], mv[:, :, :])

            for t in range(4):
                normalise(0, t)
            dve.wait_ge(loaded_by["tab"], 16)
            for j in range(0, NCH, 2):
                rotate("pre", 0, 0, j)
                rotate("pre", 0, 0, j + 1)
                rotary_sums(dve, 0, j)
                first_part(0, j)
                first_part(0, j + 1)
                leave_first(dve, 0, j)
                leave_second(dve, 0, j)
            if decay:
                dve.wait_ge(loaded_by["corr"], 16)
            for a in range(NAG):
                maxima(0, 0, a)
            split_maxima("pre", 0, 0, 0)
            for g in (1, 2):
                for a in range(NAG):
                    if 16 * g + A_AT[g][a] < 0:
                        maxima(0, g, a)

            def body(tag, b):
                for s in range(64):
                    grp, o = divmod(s, 16)
                    if s == 0 and tag != "last":
                        dve.wait_ge(m_ready, base(tag, b))
                    if s < 4 and tag != "last":
                        normalise(b + 1, s)
                    if s == 2:
                        lay_values(tag, b)
                    for ahead, of, a in groups(s, tag, A_AT):
                        maxima(b + ahead, of, a)
                    for ahead, of, a in groups(s, tag, SPLIT_AT):
                        split_maxima(tag, b, b + ahead, of)
                    for at, name in USES:
                        if at + 1 == s and name in ORDER[tag] and name not in BY_ACT:
                            nb = b - 1 if name in PREV else b
                            (normalise_heads if name[:2] == "OT" else add_out)(tag, b, nb, name)
                    if tag != "last":
                        for j in range(NCH):
                            if ROTATE_AT[j] == s:
                                rotate(tag, b, b + 1, j)
                            if FIRST_AT[j] == s:
                                first_part(b + 1, j)

            body("first", 0)
            with dve.Fori(1, NB - 1) as b:
                body("mid", b)
            body("last", NB - 1)
            for name in ("OT3", "Wo0", "Wo1"):
                (normalise_heads if name[:2] == "OT" else add_out)("post", NB, NB - 1, name)

        @block.gpsimd
        def _(pool):
            for v in range(NV):
                nc.gpsimd.memset(KS[96:99, v, :, :, :], 1.0).then_inc(ones_set, 1)
                pool.wait_ge(ones_set, v + 1)
            nc.gpsimd.memset(Vaug[:, :, :, 16:32], 1.0).then_inc(ones_set, 1)
            pool.wait_ge(ones_set, NV + 1)
            pool.wait_ge(loaded_by["xb" if biased else "tab"], 16)

            def add_bias(nb):
                pool.wait_ge(xn_ready, (nb + 1) * XN)
                xs = X[:, bass.ds(nb * 4, 4), :]
                nc.gpsimd.tensor_tensor(xs, xs, xb[:, :].unsqueeze(1).to_broadcast([P, 4, D]), ALU.add).then_inc(
                    xbias_done, 1)

            def select(b, kk):
                kt = kk % 4
                pool.wait_ge(exp_done, apart(pool, b * 64 + (4 * kk + 4), loaded))
                diag = probs[:, kk % PSLOTS, :, kt * P:(kt + 1) * P]
                nc.gpsimd.affine_select(out=diag, in_=diag, compare_op=ALU.is_ge, fill=0.0, base=0,
                                        pattern=[[0, 4], [-1, P]], channel_multiplier=1).then_inc(sel_done, 1)
                pool.wait_ge(e_exp, apart(pool, b * 16 + (kk + 1), loaded))
                lo = low[:, kk % 2, :, :]
                nc.gpsimd.affine_select(out=lo, in_=lo, compare_op=ALU.is_ge, fill=0.0, base=-1,
                                        pattern=[[0, 4], [1, P]], channel_multiplier=-1).then_inc(sel_done, 1)

            if biased:
                add_bias(0)

            def body(tag, b):
                for s in range(64):
                    if decay and s % 4 == 3:
                        select(b, s // 4)
                    if tag == "first" and s % 4 == 0 and ASIDE_FROM <= s < ASIDE_FROM + 4 * len(aside):
                        aside[(s - ASIDE_FROM) // 4](pool)
                    if tag != "last":
                        if biased and s == 4:
                            add_bias(b + 1)
                        for j in range(0, NCH, 2):
                            if ROTATE_AT[j + 1] + 1 == s:
                                rotary_sums(pool, b + 1, j)
                                leave_first(pool, b + 1, j)
                            if ROTATE_AT[j + 1] + 1 + THIRD_AT == s:
                                leave_second(pool, b + 1, j)

            body("first", 0)
            with pool.Fori(1, NB - 1) as b:
                body("mid", b)
            body("last", NB - 1)
def single_head_layer(nc, g, ins):
    X, MV, RSTD, ident = g["X"], g["MV"], g["RSTD"], g["ident"]
    scale = 1.0 / D ** 0.5
    WI = 6
    with ExitStack() as ctx:
        def sb(name, shape):
            return ctx.enter_context(nc.sbuf_tensor(f"{g['layer']}_{name}", shape, F32))

        def ps(name, shape):
            return ctx.enter_context(nc.psum_tensor(f"{g['layer']}_{name}", shape, F32))

        def sem(name):
            return nc.alloc_semaphore(f"{g['layer']}_{name}")

        psW, psS = ps("work", [P, 2, S]), ps("scores", [P, 2, S])
        psP, psO = ps("probs_turned", [P, 2, S]), ps("out", [P, 2, S])
        wg, wv, xb, mask = sb("wg", [P, 2, D]), sb("wv", [P, 2, D]), sb("xb", [P, D]), sb("mask", [P, S])
        xn, xnT = sb("xn", [P, 2, 4, D]), sb("xnT", [P, 2, 2, S])
        tT, v = sb("tT", [P, 2, 2, S]), sb("v", [P, 2, 4, D])
        sc, pr, pT = sb("masked", [P, 2, S]), sb("probs", [P, 2, S]), sb("probsT", [P, 2, S])
        mx, nm = sb("mx", [P, 4]), sb("nm", [P, 4])
        total, rec = sb("total", [P, 4]), sb("rec", [P, 4])
        st, mv = sb("st", [P, 4, 6]), sb("mv", [P, 4, 2])

        loaded, root, rstd_done = sem("loaded"), sem("root"), sem("rstd_done")
        xn_ready, xbias_done = sem("xn_ready"), sem("xbias_done")
        w_ready, w_taken = sem("work_ready"), sem("work_taken")
        s_ready, max_done, nm_done, exp_done = sem("scores_ready"), sem("max_done"), sem("nm_done"), sem("exp_done")
        p_ready, pT_taken = sem("probs_turned"), sem("probsT_taken")
        o_ready, rec_done, added = sem("out_ready"), sem("rec_done"), sem("added")
        bns_done, agg_done = sem("bns_done"), sem("agg_done")
        block = ctx.enter_context(nc.Block())
        LOADS = [(wg, ins["wg"]), (wv, ins["wv"]), (xb, ins["xb"]), (mask, ins["mask"])]

        @block.sync
        def _(sp):
            for to, src in LOADS:
                sp.dma_start(to[tuple(slice(None) for _ in src.shape)], src).then_inc(loaded, 16)

        @block.tensor
        def _(pe):
            pe.wait_ge(loaded, 16 * len(LOADS))

            def work(b, p, i):
                n = b * WI + i
                if not (isinstance(n, int) and n < 2):
                    pe.wait_ge(w_taken, n - 1)
                if i < 2:
                    pe.wait_ge(xn_ready, b * 4 + 4)
                    for t in range(4):
                        last = pe.transpose(psW[:, i, t * P:(t + 1) * P], xn[:, p, t, i * P:(i + 1) * P], ident[:, :])
                elif i < 4:
                    pe.wait_ge(w_taken, b * WI + 2)
                    for c in range(2):
                        last = pe.matmul(psW[:, i % 2, :], wg[:, c, (i - 2) * P:(i - 1) * P], xnT[:, p, c, :],
                                         start=(c == 0), stop=(c == 1))
                else:
                    for t in range(2):
                        k = 2 * (i - 4) + t
                        for c in range(2):
                            last = pe.matmul(psW[:, i % 2, t * D:(t + 1) * D], xnT[:, p, c, k * P:(k + 1) * P],
                                             wv[:, c, :], start=(c == 0), stop=(c == 1))
                last.then_inc(w_ready, 1)

            def scores(b, p, qt):
                n = b * 4 + qt
                if not (isinstance(n, int) and n < 2):
                    pe.wait_ge(max_done, n - 1)
                pe.wait_ge(w_taken, b * WI + 4)
                W = (qt + 1) * P
                for c in range(2):
                    last = pe.matmul(psS[:, qt % 2, 0:W], tT[:, p, c, qt * P:W], xnT[:, p, c, 0:W], start=(c == 0), stop=(c == 1))
                last.then_inc(s_ready, 1)

            def turn(b, qt):
                n = b * 4 + qt
                pe.wait_ge(exp_done, n + 1)
                if not (isinstance(n, int) and n < 2):
                    pe.wait_ge(pT_taken, n - 1)
                for k in range(qt + 1):
                    last = pe.transpose(psP[:, qt % 2, k * P:(k + 1) * P], pr[:, qt % 2, k * P:(k + 1) * P], ident[:, :])
                last.then_inc(p_ready, 1)

            def values(b, p, qt):
                n = b * 4 + qt
                pe.wait_ge(pT_taken, n + 1)
                pe.wait_ge(w_taken, b * WI + 6)
                if not (isinstance(n, int) and n < 2):
                    pe.wait_ge(added, n - 1)
                for k in range(qt + 1):
                    last = pe.matmul(psO[:, qt % 2, 0:D], pT[:, qt % 2, k * P:(k + 1) * P], v[:, p, k, :],
                                     start=(k == 0), stop=(k == qt))
                last.then_inc(o_ready, 1)

            for i in range(WI):
                work(0, 0, i)
            scores(0, 0, 0)
            scores(0, 0, 1)

            def body(b, p, last=False):
                def ahead(i):
                    if not last:
                        work(b + 1, 1 - p, i)
                ahead(0)
                turn(b, 0)
                ahead(1)
                values(b, p, 0)
                scores(b, p, 2)
                turn(b, 1)
                ahead(2)
                values(b, p, 1)
                scores(b, p, 3)
                turn(b, 2)
                ahead(3)
                values(b, p, 2)
                ahead(4)
                turn(b, 3)
                ahead(5)
                if not last:
                    scores(b + 1, 1 - p, 0)
                values(b, p, 3)
                if not last:
                    scores(b + 1, 1 - p, 1)

            body(0, 0)
            body(1, 1)
            with pe.Fori(1, NB // 2 - 1) as j:
                body(j * 2, 0)
                body(j * 2 + 1, 1)
            body(NB - 2, 0)
            body(NB - 1, 1, True)

        @block.scalar
        def _(act):
            act.activation(RSTD[:, 1, :], MV[:, :, 1], ACT.Sqrt, bias=g["eps"][:, :]).then_inc(root, 1)

            def take(b, p, i):
                act.wait_ge(w_ready, b * WI + (i + 1))
                src = psW[:, i % 2, :]
                if i < 2:
                    if not (isinstance(b, int) and b < 2) and i == 0:
                        act.wait_ge(s_ready, b * 4 - 4)
                    act.copy(xnT[:, p, i, :], src).then_inc(w_taken, 1)
                elif i < 4:
                    act.copy(tT[:, p, i - 2, :], src).then_inc(w_taken, 1)
                else:
                    if not (isinstance(b, int) and b < 2) and i == 4:
                        act.wait_ge(o_ready, b * 4 - 4)
                    k = 2 * (i - 4)
                    act.copy(v[:, p, k:k + 2, :].rearrange("p t d -> p (t d)"), src).then_inc(w_taken, 1)

            def exps(b, qt):
                n = b * 4 + qt
                W = (qt + 1) * P
                act.wait_ge(nm_done, n + 1)
                if not (isinstance(n, int) and n < 2):
                    act.wait_ge(p_ready, n - 1)
                if not (isinstance(n, int) and n < 4):
                    act.wait_ge(rec_done, n - 3)
                act.activation(pr[:, qt % 2, 0:W], sc[:, qt % 2, 0:W], ACT.Exp, bias=nm[:, qt:qt + 1], scale=scale,
                               accum_out=total[:, qt:qt + 1]).then_inc(exp_done, 1)

            def take_probs(b, qt):
                n = b * 4 + qt
                W = (qt + 1) * P
                act.wait_ge(p_ready, n + 1)
                if not (isinstance(n, int) and n < 2):
                    act.wait_ge(o_ready, n - 1)
                act.copy(pT[:, qt % 2, 0:W], psP[:, qt % 2, 0:W]).then_inc(pT_taken, 1)

            for i in range(WI):
                take(0, 0, i)
            exps(0, 0)
            exps(0, 1)

            def body(b, p, last=False):
                def ahead(i):
                    if not last:
                        take(b + 1, 1 - p, i)
                ahead(0)
                take_probs(b, 0)
                ahead(1)
                exps(b, 2)
                take_probs(b, 1)
                ahead(2)
                exps(b, 3)
                take_probs(b, 2)
                ahead(3)
                ahead(4)
                take_probs(b, 3)
                ahead(5)
                if not last:
                    exps(b + 1, 0)
                    exps(b + 1, 1)

            body(0, 0)
            body(1, 1)
            with act.Fori(1, NB // 2 - 1) as j:
                body(j * 2, 0)
                body(j * 2 + 1, 1)
            body(NB - 2, 0)
            body(NB - 1, 1, True)

        @block.vector
        def _(dve):
            dve.wait_ge(root, 1)
            dve.reciprocal(RSTD[:, 0, :], RSTD[:, 1, :]).then_inc(rstd_done, 1)
            dve.wait_ge(rstd_done, 1)
            dve.wait_ge(loaded, 16 * len(LOADS))

            def normalise(b, p):
                if not (isinstance(b, int) and b < 2):
                    dve.wait_ge(w_ready, b * WI - 10)
                for t in range(4):
                    i = b * 4 + t
                    dve.tensor_scalar(xn[:, p, t, :], X[:, i, :], MV[:, i, 0:1], RSTD[:, 0, bass.ds(i, 1)],
                                      ALU.subtract, ALU.mult).then_inc(xn_ready, 1)

            def maximum(b, qt):
                n = b * 4 + qt
                W = (qt + 1) * P
                dve.wait_ge(s_ready, apart(dve, n + 1, loaded))
                if not (isinstance(n, int) and n < 2):
                    dve.wait_ge(exp_done, apart(dve, n - 1, loaded))
                dve.tensor_tensor_reduce(sc[:, qt % 2, 0:W], psS[:, qt % 2, 0:W], mask[:, S - W:S], 1.0, -3.0e38, ALU.add,
                                         ALU.max, mx[:, qt:qt + 1]).then_inc(max_done, 1)
                dve.wait_ge(max_done, n + 1)
                dve.tensor_scalar(nm[:, qt:qt + 1], mx[:, qt:qt + 1], -scale, None, ALU.mult).then_inc(nm_done, 1)

            def add_out(b, qt):
                n = b * 4 + qt
                dve.wait_ge(exp_done, n + 1)
                dve.reciprocal(rec[:, qt:qt + 1], total[:, qt:qt + 1]).then_inc(rec_done, 1)
                dve.wait_ge(rec_done, n + 1)
                dve.wait_ge(o_ready, n + 1)
                if qt == 0:
                    dve.wait_ge(xbias_done, b + 1)
                dve.scalar_tensor_tensor(X[:, n, :], psO[:, qt % 2, 0:D], rec[:, qt:qt + 1], X[:, n, :], ALU.mult,
                                         ALU.add).then_inc(added, 1)
                dve.wait_ge(added, apart(dve, n + 1, loaded))
                dve.bn_stats(st[:, qt, :], X[:, n, :]).then_inc(bns_done, 1)
                dve.wait_ge(bns_done, apart(dve, n + 1, loaded))
                dve.bn_aggr(mv[:, qt, :], st[:, qt, :]).then_inc(agg_done, 1)
                if qt == 3:
                    dve.wait_ge(agg_done, n + 1)
                    dve.tensor_copy(MV[:, bass.ds(b * 4, 4), :], mv[:, :, :])

            normalise(0, 0)
            normalise(1, 1)
            maximum(0, 0)
            maximum(0, 1)

            def body(b, p, more=True, last=False):
                maximum(b, 2)
                add_out(b, 0)
                maximum(b, 3)
                if more:
                    normalise(b + 2, p)
                add_out(b, 1)
                add_out(b, 2)
                if not last:
                    maximum(b + 1, 0)
                    maximum(b + 1, 1)
                add_out(b, 3)

            body(0, 0)
            body(1, 1)
            with dve.Fori(1, NB // 2 - 1) as j:
                body(j * 2, 0)
                body(j * 2 + 1, 1)
            body(NB - 2, 0, False)
            body(NB - 1, 1, False, True)

        @block.gpsimd
        def _(pool):
            pool.wait_ge(loaded, 16 * len(LOADS))
            with pool.Fori(0, NB) as b:
                pool.wait_ge(xn_ready, b * 4 + 4)
                xs = X[:, bass.ds(b * 4, 4), :]
                nc.gpsimd.tensor_tensor(xs, xs, xb[:, :].unsqueeze(1).to_broadcast([P, 4, D]), ALU.add).then_inc(
                    xbias_done, 1)




HEAD_DIMS = [a + HD // 2 * y for a in range(HD // 2) for y in range(2)]
COLS = [(8 * c + h) * HD + d for c in range(2) for d in HEAD_DIMS for h in range(8)]


def hybrid_stack(nc, w, out):
    with ExitStack() as ctx:
        g = global_tensors(nc, ctx)
        folded = {n: nc.dram_tensor(f"folded_{n}", s, F32, kind="Internal").ap() for n, s in FOLDED.items()}
        experts_a = {"wg": w["gate_a"], "bg": w["gate_bias"], "we": w["we"], "be": w["be"]}
        experts_b = {"wg": w["gate_b"], "w1": w["w1"], "w2": w["w2"], "out": out}
        decay = {"load": [("wk", folded["a_wk"]), ("tab", w["decay_tab"]), ("wq", w["a_wq"]), ("wv", folded["a_wv"]),
                          ("wo", w["a_wo"]), ("corr", w["corr"])]}
        rope = {"load": [("wk", w["b_wk"]), ("tab", w["rope_tab"]), ("wq", w["b_wq"]), ("wv", w["b_wv"]), ("wo", w["b_wo"])]}
        causal = {"wg": folded["c_wg"], "wv": folded["c_wv"], "xb": w["c_bias"], "mask": w["mask"]}
        latent = {"load": [("wk", folded["d_wk"]), ("tab", w["rope_tab"]), ("wv", folded["d_wv"]), ("wo", w["dwo"]),
                           ("kb", folded["d_kb"]), ("xb", folded["d_xb"])]}

        def layer(name):
            g["layer"] = name
            return nc.cleanup_on_exit()

        with layer("prepare"):
            prepare(nc, g, w, folded)
        with layer("decay"):
            mha_layer(nc, g, decay, True, 1.0 / D ** 0.5, True, False, clears(g, w["zeros"]))
        with layer("experts1"):
            routed_layer(nc, g, experts_a, False)
        with layer("rope"):
            mha_layer(nc, g, rope, False, HD ** -0.5, True, False)
        with layer("experts2"):
            routed_layer(nc, g, experts_a, False)
        with layer("causal"):
            single_head_layer(nc, g, causal)
        with layer("experts3"):
            routed_layer(nc, g, experts_b, True)
        with layer("latent"):
            mha_layer(nc, g, latent, False, HD ** -0.5, False, True)
        with layer("experts4"):
            routed_layer(nc, g, experts_b, True, last_layer=True)


def chunked(a):
    return np.ascontiguousarray(a.reshape(-1, P, a.shape[-1]).transpose(1, 0, 2))


def every_partition(a):
    return np.ascontiguousarray(np.broadcast_to(a.reshape(-1), (P, a.size)))


def tables():
    i = np.arange(S)
    angles = np.outer(i, 1.0 / 10000.0 ** (np.arange(0, HD, 2) / HD))
    angles = np.concatenate([angles, angles], -1).T
    sign = np.where(np.arange(HD) < HD // 2, -1.0, 1.0)[:, None]
    dims = [d for d in HEAD_DIMS for _ in range(8)]
    rope = np.stack([np.cos(angles)[dims], (np.sin(angles) * sign)[dims]], 1)
    decay = np.broadcast_to(np.stack([np.exp(.01 * (i - S / 2)), np.exp(-.01 * (i - S / 2))]), (P, 2, S))
    q, k = i[:, None], i[None]
    corr = np.where(k >= q, 1.0, np.exp(-.02 * (q - k))).reshape(4, P, S).transpose(1, 0, 2)
    mask = np.where(k[:, :] - (S - P) > np.arange(P)[:, None], -1e30, 0.0)
    t = {"rope_tab": rope, "decay_tab": decay, "corr": corr, "mask": mask, "ident": np.eye(P),
         "before": np.triu(np.ones((P, P)), 1), "con": shape_constants(), "zeros": np.zeros((P, D))}
    return {n: np.ascontiguousarray(a, dtype=np.float32) for n, a in t.items()}


def layouts(L0_attn_a_x, L0_attn_a_W_q, L0_attn_a_W_k, L0_attn_a_W_v, L0_attn_a_W_o, L0_attn_a_W_down_kv,
            L0_attn_a_W_up_k, L0_attn_a_W_up_v, L0_attn_b_Wqkv, L0_attn_b_Wo, L0_ffn_Wg, L0_ffn_bg, L0_ffn_We, L0_ffn_be,
            L1_attn_a_qkv_w, L1_attn_a_out_w, L1_attn_a_out_b, L1_attn_b_w_dk, L1_attn_b_b_dk, L1_attn_b_w_dv,
            L1_attn_b_b_dv, L1_attn_b_w_uk, L1_attn_b_b_uk, L1_attn_b_w_uv, L1_attn_b_b_uv, L1_attn_b_w_o,
            L1_attn_b_b_o, L1_ffn_Wr, L1_ffn_W1, L1_ffn_W2):
    tiles = L0_attn_a_x.reshape(NB, 4, P, D).transpose(0, 2, 1, 3)
    q, k, v = (L0_attn_b_Wqkv[:, i * D:(i + 1) * D] for i in range(3))
    cq, ck, cv = (L1_attn_a_qkv_w[i * D:(i + 1) * D] for i in range(3))
    return {
        "x": tiles,
        "a_wq": chunked(L0_attn_a_W_q[:, COLS]), "a_wo": chunked(L0_attn_a_W_o),
        "wkT": chunked(L0_attn_a_W_k.T), "wvT": chunked(L0_attn_a_W_v.T), "wdown": chunked(L0_attn_a_W_down_kv),
        "upk": L0_attn_a_W_up_k[:, COLS], "upv": L0_attn_a_W_up_v,
        "b_wq": chunked(q[:, COLS]), "b_wk": chunked(k[:, COLS]), "b_wv": chunked(v), "b_wo": chunked(L0_attn_b_Wo),
        "gate_a": chunked(L0_ffn_Wg), "gate_bias": every_partition(L0_ffn_bg),
        "we": L0_ffn_We.reshape(E, 2, P, D).transpose(2, 1, 0, 3).reshape(P, 2, E * D), "be": every_partition(L0_ffn_be),
        "cq": chunked(cq), "ck": chunked(ck), "cv": chunked(cv), "coT": chunked(L1_attn_a_out_w.T),
        "c_bias": every_partition(L1_attn_a_out_b),
        "dkT": L1_attn_b_w_dk[COLS].T, "dvT": L1_attn_b_w_dv[COLS].T, "uk": L1_attn_b_w_uk[:, COLS], "uv": L1_attn_b_w_uv,
        "bdk": L1_attn_b_b_dk.reshape(P, 1), "bdv": L1_attn_b_b_dv.reshape(P, 1),
        "buk": L1_attn_b_b_uk[COLS].reshape(2, P).T, "buv": L1_attn_b_b_uv.reshape(2, P).T,
        "dwo": chunked(L1_attn_b_w_o), "bo": every_partition(L1_attn_b_b_o),
        "gate_b": chunked(L1_ffn_Wr),
        "w1": L1_ffn_W1.reshape(E, 2, P, F).transpose(0, 2, 1, 3),
        "w2": L1_ffn_W2.reshape(E, F // P, P, D).transpose(0, 2, 1, 3),
    }


def kernel(**inputs):
    import concourse.bacc as _bacc
    from concourse.bass_utils import run_bass_kernel_spmd as _run

    nc = _bacc.Bacc("TRN2", target_bir_lowering=False, num_devices=1)
    data = layouts(**{n: np.asarray(a) for n, a in inputs.items()})
    data.update(tables())
    arrays, w = {}, {}
    for name, a in data.items():
        a = np.ascontiguousarray(a)
        arrays[f"in_{name}_dram"] = a
        w[name] = nc.dram_tensor(f"in_{name}_dram", a.shape, mybir.dt.from_np(a.dtype), kind="ExternalInput").ap()
    out = nc.dram_tensor("out_0_dram", (NB, S, D), F32, kind="ExternalOutput").ap()
    hybrid_stack(nc, w, [out[q].rearrange("(t p) d -> p t d", p=P) for q in range(NB)])
    return _run(nc, [arrays], core_ids=[0]).results[0]["out_0_dram"]
```
